# Optimizing a Trainium2 kernel written in Bass

```python
import numpy as np
import jax
import jax.numpy as jnp

def _softmax(x, axis=-1):
    return jax.nn.softmax(x, axis=axis)

def _gelu(x):
    return jax.nn.gelu(x, approximate=True)

def _silu(x):
    return jax.nn.silu(x)

def _sigmoid(x):
    return jax.nn.sigmoid(x)

def _layernorm(x, axis=-1, eps=1e-05):
    m = jnp.mean(x, axis=axis, keepdims=True)
    v = jnp.var(x, axis=axis, keepdims=True)
    return (x - m) / jnp.sqrt(v + eps)

def _scatter_add(tgt, idx, src, axis=0):
    return tgt.at[idx].add(src)

def _segment_sum(src, seg, n):
    return jax.ops.segment_sum(src, seg, n)
kernel_name = 'mk_xattn_ffn_d1_seqx_r4_0f6130'

def setup_inputs(seed: int=0):
    np.random.seed(seed)
    _w = jnp.asarray

    def _rec_inputs():
        import jax
        import jax.numpy as jnp
        _rk = jax.random.key(seed)
        x = -0.0005146 + 1 * jax.random.normal(jax.random.fold_in(_rk, 1), (64, 128, 256), jnp.float32)
        _lenS = 128 - jax.random.randint(jax.random.fold_in(_rk, 7), (64,), 0, max(1, 128 // 4) + 1, jnp.int32)
        _lenS2 = 128 - jax.random.randint(jax.random.fold_in(_rk, 8), (64,), 0, max(1, 128 // 4) + 1, jnp.int32)
        _ctx_768P = jax.random.normal(jax.random.fold_in(_rk, 11), (64, 16, 192), jnp.float32)
        _ctx_768c = jax.random.dirichlet(jax.random.fold_in(_rk, 511), 0.3 * jnp.ones((16,), jnp.float32), (64, 128))
        _ctx_768t = jnp.einsum('bsk,bkd->bsd', _ctx_768c, _ctx_768P)
        _ctx_768t = _ctx_768t * jax.lax.rsqrt(jnp.mean(jnp.square(_ctx_768t)) + 1e-12) * 0.953939
        ctx_768 = -0.00040386 + 0.999972 * (_ctx_768t + 0.3 * jax.random.normal(jax.random.fold_in(_rk, 611), (64, 128, 192), jnp.float32))
        _validS = jnp.arange(128)[None, :] < _lenS[:, None]
        _validS2 = jnp.arange(128)[None, :] < _lenS2[:, None]
        _causal = jnp.tril(jnp.ones((128, 128), dtype=bool))
        mask_BxS2_bk0 = jnp.logical_not(jnp.broadcast_to(_validS2[:, :], (64, 128)))
        return (x, ctx_768, mask_BxS2_bk0)
    x, ctx_768, mask_BxS2_bk0 = _rec_inputs()

    def _L0_xattn_setup():
        import jax, jax.numpy as jnp
        import numpy as np
        DIM_IN, DIM_LAT, DIM_HEAD = (192, 256, 64)
        INNER = max(DIM_LAT, DIM_IN)
        HEADS = INNER // DIM_HEAD
        SCALE = DIM_HEAD ** (-0.5)
        RMS_EPS = 1e-08
        LN_EPS = 1e-05

        def layernorm(x, g, b):
            mu = jnp.mean(x, axis=-1, keepdims=True)
            var = jnp.mean((x - mu) ** 2, axis=-1, keepdims=True)
            return (x - mu) * jax.lax.rsqrt(var + LN_EPS) * g + b

        def rmsnorm(x, gamma):
            norm = jnp.sqrt(jnp.sum(x * x, axis=-1, keepdims=True)) * x.shape[-1] ** (-0.5)
            return x / jnp.maximum(norm, RMS_EPS) * gamma
        key = jax.random.key(seed)
        ks = jax.random.split(key, 12)
        b, n, m = (4, 1024, 128)
        x = jax.random.normal(ks[0], (b, n, DIM_IN), jnp.float32)
        latents = jax.random.normal(ks[1], (b, m, DIM_LAT), jnp.float32)
        mask = jax.random.randint(ks[2], (b, n), 0, 2).astype(bool)
        s = lambda k, sh, fan: jax.random.normal(k, sh, jnp.float32) * fan ** (-0.5)
        return {'x': x, 'latents': latents, 'mask': mask, 'ln_x_g': jnp.ones((DIM_IN,), jnp.float32), 'ln_x_b': jnp.zeros((DIM_IN,), jnp.float32), 'ln_l_g': jnp.ones((DIM_LAT,), jnp.float32), 'ln_l_b': jnp.zeros((DIM_LAT,), jnp.float32), 'qn_g': jnp.ones((DIM_HEAD,), jnp.float32), 'kn_g': jnp.ones((DIM_HEAD,), jnp.float32), 'Wq': s(ks[3], (INNER, DIM_LAT), DIM_LAT), 'Wkv': s(ks[4], (2 * INNER, DIM_IN), DIM_IN), 'Wlkv': s(ks[5], (2 * INNER, DIM_LAT), DIM_LAT), 'Wo': s(ks[6], (DIM_LAT, INNER), INNER), 'bo': jnp.zeros((DIM_LAT,), jnp.float32)}
    _L0_xattn_all = _L0_xattn_setup()
    _L0_xattn_in = {k: v for k, v in _L0_xattn_all.items() if k in ('ln_x_g', 'ln_x_b', 'ln_l_g', 'ln_l_b', 'qn_g', 'kn_g', 'Wq', 'Wkv', 'Wlkv', 'Wo', 'bo')}
    del _L0_xattn_all

    def _L0_ffn_setup():
        import jax, jax.numpy as jnp
        import numpy as np
        from jax import lax
        B, S, H = (2, 256, 256)
        I = 128
        E = 32
        TOP_K = 4
        N_GROUP = 4
        TOPK_GROUP = 2
        SCALE = 2.5
        N_SHARED = 2
        SH_I = I * N_SHARED

        def _route(tokens, router_weight, router_bias):
            logits = tokens.astype(jnp.float32) @ router_weight.astype(jnp.float32).T
            scores = jax.nn.sigmoid(logits)
            sfc = scores + router_bias[None, :]
            T = tokens.shape[0]
            grp = sfc.reshape(T, N_GROUP, E // N_GROUP)
            group_scores = lax.top_k(grp, 2)[0].sum(-1)
            _, gidx = lax.top_k(group_scores, TOPK_GROUP)
            gmask = jax.nn.one_hot(gidx, N_GROUP, dtype=sfc.dtype).sum(1)
            smask = jnp.broadcast_to(gmask[:, :, None], (T, N_GROUP, E // N_GROUP)).reshape(T, E)
            tmp = jnp.where(smask > 0, sfc, 0.0)
            _, topk_idx = lax.top_k(tmp, TOP_K)
            topk_w = jnp.take_along_axis(scores, topk_idx, axis=1)
            topk_w = topk_w / (topk_w.sum(-1, keepdims=True) + 1e-20)
            topk_w = topk_w * SCALE
            return (topk_idx, topk_w)
        key = jax.random.key(seed)
        ks = jax.random.split(key, 10)
        std = 0.02
        return {'hidden_states': jax.random.normal(ks[0], (B, S, H), jnp.float32), 'router_weight': jax.random.normal(ks[1], (E, H), jnp.float32) * std, 'router_bias': jnp.zeros((E,), jnp.float32), 'gate_w': jax.random.normal(ks[2], (E, I, H), jnp.float32) * std, 'up_w': jax.random.normal(ks[3], (E, I, H), jnp.float32) * std, 'down_w': jax.random.normal(ks[4], (E, H, I), jnp.float32) * std, 'shared_gate_w': jax.random.normal(ks[5], (SH_I, H), jnp.float32) * std, 'shared_up_w': jax.random.normal(ks[6], (SH_I, H), jnp.float32) * std, 'shared_down_w': jax.random.normal(ks[7], (H, SH_I), jnp.float32) * std}
    _L0_ffn_all = _L0_ffn_setup()
    _L0_ffn_in = {k: v for k, v in _L0_ffn_all.items() if k in ('router_weight', 'router_bias', 'gate_w', 'up_w', 'down_w', 'shared_gate_w', 'shared_up_w', 'shared_down_w')}
    del _L0_ffn_all
    return {'x': x, 'ctx_768': ctx_768, 'mask_BxS2_bk0': mask_BxS2_bk0, 'L0_xattn_ln_x_g': _L0_xattn_in['ln_x_g'], 'L0_xattn_ln_x_b': _L0_xattn_in['ln_x_b'], 'L0_xattn_ln_l_g': _L0_xattn_in['ln_l_g'], 'L0_xattn_ln_l_b': _L0_xattn_in['ln_l_b'], 'L0_xattn_qn_g': _L0_xattn_in['qn_g'], 'L0_xattn_kn_g': _L0_xattn_in['kn_g'], 'L0_xattn_Wq': _L0_xattn_in['Wq'], 'L0_xattn_Wkv': _L0_xattn_in['Wkv'], 'L0_xattn_Wlkv': _L0_xattn_in['Wlkv'], 'L0_xattn_Wo': _L0_xattn_in['Wo'], 'L0_xattn_bo': _L0_xattn_in['bo'], 'L0_ffn_router_weight': _L0_ffn_in['router_weight'], 'L0_ffn_router_bias': _L0_ffn_in['router_bias'], 'L0_ffn_gate_w': _L0_ffn_in['gate_w'], 'L0_ffn_up_w': _L0_ffn_in['up_w'], 'L0_ffn_down_w': _L0_ffn_in['down_w'], 'L0_ffn_shared_gate_w': _L0_ffn_in['shared_gate_w'], 'L0_ffn_shared_up_w': _L0_ffn_in['shared_up_w'], 'L0_ffn_shared_down_w': _L0_ffn_in['shared_down_w']}

def reference(x, ctx_768, mask_BxS2_bk0, L0_xattn_ln_x_g, L0_xattn_ln_x_b, L0_xattn_ln_l_g, L0_xattn_ln_l_b, L0_xattn_qn_g, L0_xattn_kn_g, L0_xattn_Wq, L0_xattn_Wkv, L0_xattn_Wlkv, L0_xattn_Wo, L0_xattn_bo, L0_ffn_router_weight, L0_ffn_router_bias, L0_ffn_gate_w, L0_ffn_up_w, L0_ffn_down_w, L0_ffn_shared_gate_w, L0_ffn_shared_up_w, L0_ffn_shared_down_w):
    import jax
    import jax.numpy as jnp

    def _L0_xattn_ref(x, latents, mask, ln_x_g, ln_x_b, ln_l_g, ln_l_b, qn_g, kn_g, Wq, Wkv, Wlkv, Wo, bo):
        import jax, jax.numpy as jnp
        import numpy as np
        DIM_IN, DIM_LAT, DIM_HEAD = (192, 256, 64)
        INNER = max(DIM_LAT, DIM_IN)
        HEADS = INNER // DIM_HEAD
        SCALE = DIM_HEAD ** (-0.5)
        RMS_EPS = 1e-08
        LN_EPS = 1e-05

        def layernorm(x, g, b):
            mu = jnp.mean(x, axis=-1, keepdims=True)
            var = jnp.mean((x - mu) ** 2, axis=-1, keepdims=True)
            return (x - mu) * jax.lax.rsqrt(var + LN_EPS) * g + b

        def rmsnorm(x, gamma):
            norm = jnp.sqrt(jnp.sum(x * x, axis=-1, keepdims=True)) * x.shape[-1] ** (-0.5)
            return x / jnp.maximum(norm, RMS_EPS) * gamma
        b, n, _ = x.shape
        m = latents.shape[1]
        xn = layernorm(x, ln_x_g, ln_x_b)
        ln = layernorm(latents, ln_l_g, ln_l_b)
        q = ln @ Wq.T
        kv = jnp.concatenate([xn @ Wkv.T, ln @ Wlkv.T], axis=1)
        k, v = (kv[..., :INNER], kv[..., INNER:])
        split_heads = lambda t: t.reshape(t.shape[0], t.shape[1], HEADS, DIM_HEAD).transpose(0, 2, 1, 3)
        q, k, v = (split_heads(q), split_heads(k), split_heads(v))
        qn = rmsnorm(q, qn_g) * SCALE
        kn = rmsnorm(k, kn_g)
        attn = jnp.einsum('bhid,bhjd->bhij', qn, kn)
        full_mask = jnp.pad(mask, ((0, 0), (0, m)), constant_values=True)
        attn = jnp.where(full_mask[:, None, None, :], attn, -jnp.finfo(attn.dtype).max)
        attn = jax.nn.softmax(attn, axis=-1)
        out = jnp.einsum('bhij,bhjd->bhid', attn, v)
        out = out.transpose(0, 2, 1, 3).reshape(b, m, INNER)
        return out @ Wo.T + bo

    def _L0_ffn_ref(hidden_states, router_weight, router_bias, gate_w, up_w, down_w, shared_gate_w, shared_up_w, shared_down_w):
        import jax, jax.numpy as jnp
        import numpy as np
        from jax import lax
        B, S, H = (2, 256, 256)
        I = 128
        E = 32
        TOP_K = 4
        N_GROUP = 4
        TOPK_GROUP = 2
        SCALE = 2.5
        N_SHARED = 2
        SH_I = I * N_SHARED

        def _route(tokens, router_weight, router_bias):
            logits = tokens.astype(jnp.float32) @ router_weight.astype(jnp.float32).T
            scores = jax.nn.sigmoid(logits)
            sfc = scores + router_bias[None, :]
            T = tokens.shape[0]
            grp = sfc.reshape(T, N_GROUP, E // N_GROUP)
            group_scores = lax.top_k(grp, 2)[0].sum(-1)
            _, gidx = lax.top_k(group_scores, TOPK_GROUP)
            gmask = jax.nn.one_hot(gidx, N_GROUP, dtype=sfc.dtype).sum(1)
            smask = jnp.broadcast_to(gmask[:, :, None], (T, N_GROUP, E // N_GROUP)).reshape(T, E)
            tmp = jnp.where(smask > 0, sfc, 0.0)
            _, topk_idx = lax.top_k(tmp, TOP_K)
            topk_w = jnp.take_along_axis(scores, topk_idx, axis=1)
            topk_w = topk_w / (topk_w.sum(-1, keepdims=True) + 1e-20)
            topk_w = topk_w * SCALE
            return (topk_idx, topk_w)
        tokens = hidden_states.reshape(-1, H)
        topk_idx, topk_w = _route(tokens, router_weight, router_bias)
        gate_vals = jax.nn.silu(jnp.einsum('th,eih->tei', tokens, gate_w))
        up_vals = jnp.einsum('th,eih->tei', tokens, up_w)
        hidden_vals = gate_vals * up_vals
        expert_out = jnp.einsum('tei,ehi->teh', hidden_vals, down_w)
        sel = jnp.take_along_axis(expert_out, topk_idx[:, :, None], axis=1)
        mixed = (sel * topk_w[:, :, None].astype(sel.dtype)).sum(1)
        mixed = mixed.reshape(hidden_states.shape)
        sg = jax.nn.silu(jnp.einsum('bsh,ih->bsi', hidden_states, shared_gate_w))
        su = jnp.einsum('bsh,ih->bsi', hidden_states, shared_up_w)
        shared = jnp.einsum('bsi,hi->bsh', sg * su, shared_down_w)
        return mixed + shared
    x = x + _L0_xattn_ref(ctx_768, _layernorm(x, axis=-1), mask_BxS2_bk0, L0_xattn_ln_x_g, L0_xattn_ln_x_b, L0_xattn_ln_l_g, L0_xattn_ln_l_b, L0_xattn_qn_g, L0_xattn_kn_g, L0_xattn_Wq, L0_xattn_Wkv, L0_xattn_Wlkv, L0_xattn_Wo, L0_xattn_bo)
    x = x + _L0_ffn_ref(_layernorm(x, axis=-1), L0_ffn_router_weight, L0_ffn_router_bias, L0_ffn_gate_w, L0_ffn_up_w, L0_ffn_down_w, L0_ffn_shared_gate_w, L0_ffn_shared_up_w, L0_ffn_shared_down_w)
    return x

_drawn_inputs = setup_inputs


def setup_inputs(seed=0):
    import zlib

    import numpy as np

    out = dict(_drawn_inputs(seed))
    spreads = {'L0_xattn_ln_x_g': (1.0, 0.6),
     'L0_xattn_ln_x_b': (0.0, 0.479),
     'L0_xattn_ln_l_g': (1.0, 0.2),
     'L0_xattn_ln_l_b': (0.0, 0.1),
     'L0_xattn_qn_g': (1.0, 0.597),
     'L0_xattn_kn_g': (1.0, 0.6),
     'L0_xattn_bo': (0.0, 0.1),
     'L0_ffn_router_bias': (0.0, 0.517)}
    factors = {'L0_ffn_router_weight': 4.639,
     'L0_ffn_gate_w': 3.89,
     'L0_ffn_up_w': 3.852,
     'L0_ffn_down_w': 3.854,
     'L0_ffn_shared_gate_w': 3.46,
     'L0_ffn_shared_up_w': 3.419,
     'L0_ffn_shared_down_w': 3.418}
    for name, (base, spread) in spreads.items():
        noise = np.random.default_rng([zlib.crc32(name.encode()), seed]).standard_normal(out[name].shape)
        drawn = base * np.exp(spread * noise) if base else spread * noise
        out[name] = jnp.asarray(drawn.astype(out[name].dtype))
    for name, factor in factors.items():
        out[name] = (out[name] * factor).astype(out[name].dtype)
    return out
```

```python
import concourse.bass as bass
from concourse import mybir
from contextlib import ExitStack

P = 128
NB, D, DC = 64, 256, 192
H, DH = 4, 64
E, I, TOPK, NG = 32, 128, 4, 4
UNITS = NB // 2
T = NB * P
ROW = D + 2
TILES = (T * TOPK + E * (P - 1)) // P
SLOTS = 8
TILES = -(-TILES // SLOTS) * SLOTS
FILL = 4
NPT = -(-TILES // P)
KC = DC - P
LN_EPS, RMS_EPS = 1e-5, 1e-8
SCALE, ROUTE_SCALE = DH ** -0.5, 2.5
NEG = 1e30
BIG = 3e38
NOWHERE = T * TOPK + 7


class Unit:

    def __init__(self, i, par):
        self.i, self.par = i, par
        self.n = 2 * i + par

    def __add__(self, d):
        q, r = divmod(self.par + d, 2)
        return Unit(self.i + q, r)

    def exists(self):
        return not isinstance(self.n, int) or 0 <= self.n < UNITS


def ge(eng, sem, value):
    if isinstance(value, int) and value <= 0:
        return
    eng.wait_ge(sem, value)


def upto(value, cap):
    return min(value, cap) if isinstance(value, int) else value


def at(start, n):
    return slice(start, start + n) if isinstance(start, int) else bass.ds(start, n)


def steps_of_phase_a(eng, step):
    for s in range(4):
        step(Unit(s // 2, s % 2))
    with eng.Fori(2, UNITS // 2 - 1) as i:
        step(Unit(i, 0))
        step(Unit(i, 1))
    for s in range(UNITS - 2, UNITS + 1):
        step(Unit(s // 2, s % 2))


RSQRT_STEPS = 11
S1_LINKS = 3 + RSQRT_STEPS
S2_LINKS = 1 + RSQRT_STEPS
S3A_LINKS = 3 + RSQRT_STEPS
S3B_LINKS = 28
BLANK_UNIT = 16 * 2 * TOPK // FILL
CONSTS = 23
MADE = 16


def build(nc, x, ctx, mask, ln_x_g, ln_x_b, ln_l_g, ln_l_b, qn_g, kn_g, wq, wkv, wlkv, wo, bo,
          rw, rb, gate, up, down, sgate, sup, sdown, out):
    fp32, bf16, i32, u8 = mybir.dt.float32, mybir.dt.bfloat16, mybir.dt.int32, mybir.dt.uint8
    ALU, ACT, AX = mybir.AluOpType, mybir.ActivationFunctionType, mybir.AxisListType.X

    lists = nc.dram_tensor("lists", [TILES * P, ROW], fp32).ap()
    expert_out = nc.dram_tensor("expert_out", [T * TOPK, D], fp32).ap()
    tile_table = nc.dram_tensor("tile_table", [NPT * P], i32).ap()

    with ExitStack() as c:
        def sb(name, shape, dt=fp32):
            return c.enter_context(nc.sbuf_tensor(name, shape, dt))

        def pb(name, shape):
            return c.enter_context(nc.psum_tensor(name, shape, fp32))

        def sem(name):
            return c.enter_context(nc.semaphore(name))

        x1 = sb("x1", [P, NB, D])
        mr = sb("mr", [P, NB, 2])
        ident = sb("ident", [P, P])
        w_sg = sb("w_sg", [P, 2, 2 * P])
        w_su = sb("w_su", [P, 2, 2 * P])
        w_sd = sb("w_sd", [P, 2, D])
        arena = sb("arena", [P, E * 3 * D])
        used = [0]

        def part(*shape):
            n = 1
            for s in shape:
                n *= s
            v = arena[:, used[0]:used[0] + n]
            used[0] += n
            if len(shape) == 1:
                return v
            names = "abcd"[:len(shape)]
            return v.rearrange(f"p ({' '.join(names)}) -> p {' '.join(names)}",
                               **dict(zip(names, shape)))

        w_lat = part(2, 3 * D)
        w_ctx = part(2, 2 * D)
        w_o = part(2, D)
        w_r = part(2, E)
        c_in = part(2, 2, DC)
        x_hat = part(2, D)
        c_hat = part(2, DC)
        lnT = part(2, 2 * P)
        cT = part(2, 2 * P)
        sq = part(3 * D)
        raw = part(2, 3 * D)
        nqk = part(2, 3 * D)
        qT = part(2, 2, 2, P)
        kT = part(4, 2, 2 * P)
        probs = part(2, H, 2 * P)
        probsT = part(2, 2, H * P)
        o_n = part(D)
        oT = part(D)
        y_b = part(D)
        n1T = part(2, 2 * P)
        vv = part(4 * 2, H, DH + 1)
        wj = part(2, TOPK, E)
        assert used[0] <= E * 3 * D
        w_gu = arena[:, 0:E * 2 * D].rearrange("p (e k n) -> p e k n", e=E, k=2)
        w_dn = arena[:, E * 2 * D:E * 3 * D].rearrange("p (e n) -> p e n", e=E)

        pay = sb("pay", [P, 4, TOPK, ROW])
        mask_u8 = sb("mask_u8", [1, 2, 2, P], u8)
        mask_row = sb("mask_row", [1, 2, 2, 2, 2 * P], bf16)
        ones_row = sb("ones_row", [1, P], bf16)
        ones_sq = sb("ones_sq", [P, P], bf16)
        tri = sb("tri", [P, P], bf16)
        gl, bl = sb("gl", [P, 2]), sb("bl", [P, 2])
        gx, bx = sb("gx", [P, 2]), sb("bx", [P, 2])
        gqk = sb("gqk", [P, 3])
        bo_b = sb("bo_b", [P, D])
        rb_b = sb("rb_b", [P, 1, E])
        stats = sb("stats", [P, 4, 6])
        mv = sb("mv", [P, 4, 2])
        va, ra = sb("va", [P, 4]), sb("ra", [P, 4])
        ss, rq = sb("ss", [P, 24]), sb("rq", [P, 24])
        v1 = sb("v1", [P, 2])
        ry, rt = sb("ry", [P, 24]), sb("rt", [P, 24])
        nmax = sb("nmax", [P, 2, H])
        rden = sb("rden", [P, H])
        esc = sb("esc", [P, 2, E])
        sc = sb("sc", [P, 2, E])
        sfc = sb("sfc", [P, 2, E])
        g8 = sb("g8", [P, 2, NG, 8])
        gs = sb("gs", [P, 2, 10])
        gr = sb("gr", [P, 2, 10])
        m8 = sb("m8", [P, 2, 8])
        gm = sb("gm", [P, 2, NG])
        t36 = sb("t36", [P, 2, 36])
        r36 = sb("r36", [P, 2, 36])
        n8 = sb("n8", [P, 2, 8])
        chosen = sb("chosen", [P, 2, 2, E], bf16)
        wts = sb("wts", [P, 2, E])
        wsum = sb("wsum", [P, 2])
        before = sb("before", [P, 2, E], bf16)
        kept = sb("kept", [P, 1, E])
        off = sb("off", [P, 1, E])
        need_i = sb("need_i", [P, E], i32)
        need = sb("need", [P, 1, E], i32)
        new = sb("new", [P, 1, E])
        given = sb("given", [P, 2, E])
        off_n = sb("off_n", [P, 1, E])
        delta = sb("delta", [P, 1, E])
        moved = sb("moved", [P, 1, E])
        later = sb("later", [P, 2, E])
        history = sb("history", [P, UNITS, E])
        code = sb("code", [P, 2, E])
        code2 = sb("code2", [P, 2, E])
        c8 = sb("c8", [P, 2, 8])
        w4 = sb("w4", [P, 2, TOPK])
        mv2, r1 = sb("mv2", [P, 2, 2]), sb("r1", [P, 2])
        slot = sb("slot", [P, 2, 2, TOPK], i32)
        place = sb("place", [P, 2, TOPK], i32)
        first = sb("first", [P, NPT])
        page_e = sb("page_e", [P, NPT])
        page_i = sb("page_i", [P, NPT], i32)
        tab_pc = sb("tab_pc", [P, NPT], i32)
        tab = sb("tab", [1, NPT * P], i32)
        hist_j = sb("hist_j", [P, UNITS * E], bf16)
        pad = sb("pad", [P, FILL, ROW])
        ones_e = sb("ones_e", [P, E])
        dest = sb("dest", [P, SLOTS], i32)

        ps = [pb(f"ps{n}", [P, 512]) for n in range(5)]
        psS = pb("psS", [P, 2, 2, 2 * P])
        psO = pb("psO", [P, 512])

        consts = sem("consts")
        made = sem("made")
        gains = sem("gains")
        loaded = [sem("loaded0"), sem("loaded1")]
        mask_ready = sem("mask_ready")
        hats, xhat = sem("hats"), sem("xhat")
        t_x, t_c, t_k, t_q, t_n = sem("t_x"), sem("t_c"), sem("t_k"), sem("t_q"), sem("t_n")
        e_x, e_c, e_k, e_q, e_n = sem("e_x"), sem("e_c"), sem("e_k"), sem("e_q"), sem("e_n")
        pa_full, pb_full, pc_full = sem("pa_full"), sem("pb_full"), sem("pc_full")
        pa_free, pb_free, pc_free = sem("pa_free"), sem("pb_free"), sem("pc_free")
        sq_full, ss_done, scaled = sem("sq_full"), sem("ss_done"), sem("scaled")
        s_full, m_done, exp_done = sem("s_full"), sem("m_done"), sem("exp_done")
        pt_full, pt_act, pt_dve = sem("pt_full"), sem("pt_act"), sem("pt_dve")
        pv_full, on_done, ot_full, ot_ev = sem("pv_full"), sem("on_done"), sem("ot_full"), sem("ot_ev")
        y_full, y_done, x1_done = sem("y_full"), sem("y_done"), sem("x1_done")
        pay_x, lg_full, lg_exp = sem("pay_x"), sem("lg_full"), sem("lg_exp")
        ch_done, pos_full = sem("ch_done"), sem("pos_full")
        before_done = sem("before_done")
        rows_ready = sem("rows_ready")
        scat = [sem("scat0"), sem("scat1")]
        d1, d2, d3, dS = sem("d1"), sem("d2"), sem("d3"), sem("dS")
        q3 = sem("q3")
        table_made = sem("table_made")
        table_out, table_in = sem("table_out"), sem("table_in")
        dB = sem("dB")
        blank = [sem("blank0"), sem("blank1")]
        blank_start = sem("blank_start")
        weights_e = sem("weights_e")

        rows = pay.rearrange("p a k n -> p (a k) n")
        xs = [rows[:, n, :] for n in range(SLOTS)]
        yy = [rows[:, SLOTS + n, 0:D] for n in range(SLOTS)]
        xsT = pad.rearrange("p k n -> p (k n)")[:, 0:4 * D].rearrange("p (b n) -> p b n", b=4)
        flat_h = history.rearrange("p u e -> p (u e)")
        sg = flat_h[:, 0:4 * I].rearrange("p (b n) -> p b n", b=4)
        hh = flat_h[:, 4 * I:8 * I].rearrange("p (b n) -> p b n", b=4)
        hT = hist_j[:, :].bitcast(fp32).rearrange("p (b n) -> p b n", b=4)
        xs_in = [sem(f"xs_in{n}") for n in range(SLOTS)]
        dest_kept = sem("dest_kept")
        xst_full, xst_ev, gu_full = sem("xst_full"), sem("xst_ev"), sem("gu_full")
        sg_done, hh_done, ht_full, ht_ev = sem("sg_done"), sem("hh_done"), sem("ht_full"), sem("ht_ev")
        dn_full, yy_done = sem("dn_full"), sem("yy_done")
        y_out = [sem(f"y_out{n}") for n in range(SLOTS)]
        er_in = [sem("er_in0"), sem("er_in1")]
        nh, nt_full, nt_ev = sem("nh"), sem("nt_full"), sem("nt_ev")
        sgu_full, ssg_done, sh_done = sem("sgu_full"), sem("ssg_done"), sem("sh_done")
        sd_full, dC, dD, res_done = sem("sd_full"), sem("dC"), sem("dD"), sem("res_done")
        stored = [sem("stored0"), sem("stored1")]

        block = c.enter_context(nc.Block())

        def apart(eng, sem, value):
            if isinstance(value, int):
                return ge(eng, sem, value)
            value = eng.to_reg(value)
            eng.wait_ge(made, MADE)
            eng.wait_ge(sem, value)

        def arrived(t, n):
            return 16 * (t // SLOTS + 1) if isinstance(t, int) else 16 // SLOTS * (t - n) + 16

        def left(t, n):
            return 16 * (t // SLOTS) if isinstance(t, int) else 16 // SLOTS * (t - n)

        def col(v, a, b):
            return v[a:b].rearrange("(p o) -> p o", o=1)

        def wide(v):
            return v.rearrange("(a n) -> a n", a=1).to_broadcast([P, v.shape[0]])

        er = arena[:, 0:2 * 2 * TOPK * D].rearrange("p (a j k n) -> p a j k n", a=2, j=2, k=TOPK)
        n1h = arena[:, 8192:8192 + 512].rearrange("p (j n) -> p j n", j=2)
        ncT = arena[:, 8704:8704 + 512].rearrange("p (k n) -> p k n", k=2)
        shs = arena[:, 9216:9216 + 512].rearrange("p (m n) -> p m n", m=2)
        shh = arena[:, 9728:9728 + 512].rearrange("p (m n) -> p m n", m=2)
        esum = arena[:, 10240:10240 + 512].rearrange("p (j n) -> p j n", j=2)
        e2 = arena[:, 10752:10752 + 1024].rearrange("p (j k n) -> p j k n", j=2, k=2)
        res = arena[:, 12288:12288 + 1024].rearrange("p (a j n) -> p a j n", a=2, j=2)

        @block.sync
        def _(sp):
            for dst, src in (
                (w_lat[:, :, 0:D], wq.rearrange("(k p) n -> p k n", p=P)),
                (w_lat[:, :, D:3 * D], wlkv.rearrange("(k p) n -> p k n", p=P)),
                (w_ctx[:, 0, :], wkv[0:P, :]), (w_ctx[0:KC, 1, :], wkv[P:DC, :]),
                (w_o, wo.rearrange("(k p) n -> p k n", p=P)),
                (w_r, rw.rearrange("(k p) n -> p k n", p=P)),
                (gl[:, 0:1], col(ln_l_g, 0, P)), (gl[:, 1:2], col(ln_l_g, P, D)),
                (bl[:, 0:1], col(ln_l_b, 0, P)), (bl[:, 1:2], col(ln_l_b, P, D)),
                (gx[:, 0:1], col(ln_x_g, 0, P)), (gx[0:KC, 1:2], col(ln_x_g, P, DC)),
                (bx[:, 0:1], col(ln_x_b, 0, P)), (bx[0:KC, 1:2], col(ln_x_b, P, DC)),
                (gqk[0:DH, 1:2], col(qn_g, 0, DH)), (gqk[DH:P, 1:2], col(qn_g, 0, DH)),
                (gqk[0:DH, 2:3], col(kn_g, 0, DH)), (gqk[DH:P, 2:3], col(kn_g, 0, DH)),
                (bo_b[:, :], wide(bo)), (rb_b[:, 0, :], wide(rb)),
                (w_sg[:, :, :], sgate.rearrange("(k p) n -> p k n", p=P)),
                (w_su[:, :, :], sup.rearrange("(k p) n -> p k n", p=P)),
                (w_sd[:, :, :], sdown.rearrange("(k p) n -> p k n", p=P)),
            ):
                sp.dma_start(dst, src).then_inc(consts, 16)

            def load(u):
                apart(sp, hats, u.n - 1)
                apart(sp, mask_ready, u.n - 1)
                sp.dma_start(x1[:, at(2 * u.n, 2), :],
                             x[at(2 * u.n, 2)].rearrange("j p n -> p j n")).then_inc(loaded[u.par], 16)
                sp.dma_start(c_in[:, u.par], ctx[at(2 * u.n, 2)].rearrange("j p n -> p j n"))\
                  .then_inc(loaded[u.par], 16)
                sp.dma_start(mask_u8[0:1, u.par], mask[0:1, at(2 * u.n, 2), :])\
                  .then_inc(loaded[u.par], 16)

            def blank_pages(at_page, n, signal):
                for m in range(0, n, FILL):
                    sp.dma_start(lists[at((at_page + m) * P, FILL * P), :].rearrange("(k p) n -> p k n", p=P),
                                 pad[:, :, :]).then_inc(signal, 16)

            def blank_unit(u):
                apart(sp, blank[u.par], BLANK_UNIT * u.i)
                blank_pages(2 * TOPK * u.n + E, 2 * TOPK, blank[u.par])

            def step(s):
                if (s + 2).exists():
                    load(s + 2)
                if s.exists():
                    blank_unit(s)

            load(Unit(0, 0))
            load(Unit(0, 1))
            sp.wait_ge(made, MADE)
            blank_pages(0, E, blank_start)
            steps_of_phase_a(sp, step)

            sp.wait_ge(x1_done, NB)
            sp.wait_ge(rows_ready, UNITS)
            for k in range(2):
                for which, w in ((0, gate), (1, up)):
                    sp.dma_start(w_gu[:, :, k, which * I:(which + 1) * I], w[:, k]).then_inc(weights_e, 16)
            sp.dma_start(w_dn, down).then_inc(weights_e, 16)
            sp.wait_ge(table_made, 1)
            sp.dma_start(tile_table.rearrange("(c p) -> p c", p=P), tab_pc[:, :]).then_inc(table_out, 16)
            sp.wait_ge(table_out, 16)
            sp.dma_start(tab[0:1, :], tile_table.rearrange("(a n) -> a n", a=1)).then_inc(table_in, 16)
            sp.wait_ge(table_in, 16)
            sp.wait_ge(scat[0], 16 * 8 * UNITS // 2)
            sp.wait_ge(scat[1], 16 * 8 * UNITS // 2)
            for par in range(2):
                sp.wait_ge(blank[par], BLANK_UNIT * UNITS // 2)

            def load_tile(t, n):
                if not (isinstance(t, int) and t < SLOTS):
                    apart(sp, hh_done, t - SLOTS + 1)
                    apart(sp, dest_kept, t - SLOTS + 1)
                sp.dma_start(xs[n], lists[at(t * P, P), :]).then_inc(xs_in[n], 16)

            for n in range(SLOTS):
                load_tile(n, n)
            with sp.Fori(SLOTS, TILES - SLOTS + 1, SLOTS) as t:
                for n in range(SLOTS):
                    load_tile(t + n, n)

            for n in range(SLOTS):
                sp.wait_ge(y_out[n], 16 * (TILES // SLOTS))
            sp.wait_ge(dn_full, TILES)
            er_d = expert_out.rearrange("(b p k) n -> p b k n", p=P, k=TOPK)
            out_d = out.rearrange("b p n -> p b n")

            def load_er(u):
                apart(sp, dC, u.n - 1)
                sp.dma_start(er[:, u.par], er_d[:, at(2 * u.n, 2)]).then_inc(er_in[u.par], 16)

            load_er(Unit(0, 0))
            load_er(Unit(0, 1))
            load_er(Unit(1, 0))
            load_er(Unit(1, 1))
            with sp.Fori(2, UNITS // 2) as i:
                load_er(Unit(i, 0))
                load_er(Unit(i, 1))

        @block.gpsimd
        def _(pool):
            pool.memset(ident[:, :], 0.0).then_inc(q3, 1)
            pool.memset(tri[:, :], 0.0).then_inc(q3, 1)
            pool.memset(ones_sq[:, :], 1.0).then_inc(made, 1)
            pool.memset(ones_row[:, :], 1.0).then_inc(made, 1)
            pool.memset(ones_e[:, :], 1.0).then_inc(made, 1)
            pool.memset(mask_row[:, :, :, :, :], 0.0).then_inc(q3, 1)
            pool.memset(vv[:, :, :, :], 1.0).then_inc(made, 1)
            pool.memset(before[:, :, :], 0.0).then_inc(made, 1)
            pool.memset(gs[:, :, :], BIG).then_inc(made, 1)
            pool.memset(t36[:, :, :], BIG).then_inc(made, 1)
            pool.memset(pad[:, :, 0:D + 1], 0.0).then_inc(made, 1)
            pool.memset(pad[:, :, D + 1:ROW].bitcast(i32), NOWHERE).then_inc(made, 1)
            pool.memset(kept[:, :, :], 0.0).then_inc(made, 1)
            pool.memset(off[:, :, :], 0.0).then_inc(made, 1)
            pool.memset(given[:, :, :], 0.0).then_inc(made, 1)
            pool.iota(first[:, :], pattern=[[P * P, NPT]], base=0, channel_multiplier=P,
                      allow_small_or_imprecise_dtypes=True).then_inc(made, 1)
            pool.iota(place[:, :, :], pattern=[[P * TOPK, 2], [1, TOPK]], base=0,
                      channel_multiplier=TOPK).then_inc(made, 1)
            pool.wait_ge(q3, 3)
            pool.affine_select(out=ident[:, :], in_=ident[:, :], compare_op=ALU.not_equal, fill=1.0,
                               base=0, pattern=[[-1, P]], channel_multiplier=1).then_inc(made, 1)
            pool.affine_select(out=tri[:, :], in_=tri[:, :], compare_op=ALU.is_ge, fill=1.0,
                               base=0, pattern=[[-1, P]], channel_multiplier=1).then_inc(made, 1)
            pool.wait_ge(made, MADE)
            def mask_bias(u):
                apart(pool, loaded[u.par], 48 * (u.i + 1))
                apart(pool, s_full, 2 * (u.n - 1))
                pool.tensor_scalar(mask_row[0:1, u.par, :, 0, 0:P], mask_u8[0:1, u.par], NEG, -NEG,
                                   ALU.mult, ALU.add)
                pool.tensor_scalar(mask_row[0:1, u.par, :, 1, 0:P], mask_u8[0:1, u.par], NEG, -NEG,
                                   ALU.mult, ALU.add).then_inc(mask_ready, 1)

            def stage1(u):
                apart(pool, loaded[u.par], 48 * (u.i + 1))
                apart(pool, d1, S1_LINKS * (u.n + 1))
                apart(pool, t_c, u.n)
                for j in range(2):
                    h = pool.tensor_scalar(c_hat[:, j, :], c_in[:, u.par, j, :], mv[:, 2 + j, 0:1],
                                           ra[:, 2 + j:3 + j], ALU.subtract, ALU.mult)
                h.then_inc(hats, 1)

            def scale_qk(u):
                apart(pool, d2, S2_LINKS * (u.n + 1))
                apart(pool, pb_free, 2 * u.n + 2)
                apart(pool, t_q, u.n)
                for j in range(2):
                    pool.tensor_tensor(nqk[:, j, :].rearrange("p (g d) -> p g d", d=DH),
                                       raw[:, j, :].rearrange("p (g d) -> p g d", d=DH),
                                       rq[:, 12 * j:12 * j + 12].rearrange("p (g o) -> p g o", o=1)
                                       .to_broadcast([P, 12, DH]), ALU.mult).then_inc(scaled, 1)

            def stage3(u):
                apart(pool, rows_ready, u.n + 1)
                if isinstance(u.n, int) and u.n == 0:
                    pool.wait_ge(blank_start, 16 * E // FILL)
                apart(pool, blank[u.par], BLANK_UNIT * (u.i + 1))
                for j in range(2):
                    for k in range(TOPK):
                        pool.indirect_dma_start(
                            lists, bass.IndirectOffsetOnAxis(ap=slot[:, u.par, j, k:k + 1], axis=0),
                            pay[:, 2 * u.par + j, k, :], None).then_inc(scat[u.par], 16)

            def step(s):
                if (s + 1).exists():
                    mask_bias(s + 1)
                if (s + 2).exists():
                    stage1(s + 2)
                if (s + 1).exists():
                    scale_qk(s + 1)
                if (s + -1).exists():
                    stage3(s + -1)

            mask_bias(Unit(0, 0))
            stage1(Unit(0, 0))
            stage1(Unit(0, 1))
            scale_qk(Unit(0, 0))
            steps_of_phase_a(pool, step)

            def keep_dest(t, n):
                apart(pool, xs_in[n], arrived(t, n))
                apart(pool, y_out[n], left(t, n))
                pool.tensor_copy(dest[:, n:n + 1], xs[n][:, D + 1:ROW].bitcast(i32)).then_inc(dest_kept, 1)

            def scatter_tile(t, n):
                apart(pool, dest_kept, t + 1)
                apart(pool, yy_done, t + 1)
                pool.indirect_dma_start(
                    expert_out, bass.IndirectOffsetOnAxis(ap=dest[:, n:n + 1], axis=0),
                    yy[n], None, bounds_check=T * TOPK - 1, oob_is_err=False).then_inc(y_out[n], 16)

            for t in range(SLOTS):
                keep_dest(t, t)
                if t >= 4:
                    scatter_tile(t - 4, t - 4)
            with pool.Fori(SLOTS, TILES - SLOTS + 1, SLOTS) as t:
                for n in range(SLOTS):
                    keep_dest(t + n, n)
                    scatter_tile(t + (n - 4), (n - 4) % SLOTS)
            for t in range(TILES - 4, TILES):
                scatter_tile(t, t % SLOTS)

        @block.tensor
        def _(pe):
            pe.wait_ge(consts, 16 * CONSTS)
            pe.wait_ge(made, MADE)

            def turn_inputs(u):
                pe.wait_ge(xhat, u.n + 1)
                ge(pe, e_k, 2 * u.n)
                for j in range(2):
                    for k in range(2):
                        m = pe.transpose(ps[0][:, k * D + j * P:k * D + (j + 1) * P],
                                         x_hat[:, j, k * P:(k + 1) * P], ident[:, :])
                m.then_inc(t_x, 1)
                pe.wait_ge(hats, u.n + 1)
                ge(pe, e_q, u.n)
                for j in range(2):
                    pe.transpose(ps[1][:, j * P:(j + 1) * P], c_hat[:, j, 0:P], ident[:, :])
                    m = pe.transpose(ps[1][0:KC, D + j * P:D + (j + 1) * P], c_hat[:, j, P:DC], ident[:, :])
                m.then_inc(t_c, 1)

            def turn_n1(u):
                pe.wait_ge(pay_x, 2 * u.n + 2)
                pe.wait_ge(e_x, upto(u.n + 3, UNITS))
                pe.wait_ge(e_k, upto(2 * u.n + 4, NB))
                ge(pe, e_n, u.n)
                for j in range(2):
                    for k in range(2):
                        m = pe.transpose(ps[0][:, k * D + j * P:k * D + (j + 1) * P],
                                         pay[:, 2 * u.par + j, 0, k * P:(k + 1) * P], ident[:, :])
                m.then_inc(t_n, 1)

            def project(u, j):
                b = 2 * u.n + j
                pe.wait_ge(e_x, u.n + 1)
                pe.wait_ge(e_c, u.n + 1)
                tok = slice(j * P, (j + 1) * P)
                ge(pe, pa_free, b)
                for k in range(2):
                    m = pe.matmul(ps[2][:, :], lnT[:, k, tok], w_lat[:, k, 0:2 * D], start=k == 0, stop=k == 1)
                m.then_inc(pa_full, 1)
                ge(pe, pb_free, b)
                pe.matmul(ps[3][:, :], cT[:, 0, tok], w_ctx[:, 0, :], start=True, stop=False)
                pe.matmul(ps[3][:, :], cT[0:KC, 1, tok], w_ctx[0:KC, 1, :], start=False, stop=True)\
                  .then_inc(pb_full, 1)
                ge(pe, pc_free, b)
                if j == 0:
                    ge(pe, rows_ready, u.n - 2)
                for k in range(2):
                    m = pe.matmul(ps[4][:, 0:D], lnT[:, k, tok], w_lat[:, k, 2 * D:3 * D], start=k == 0, stop=k == 1)
                m.then_inc(pc_full, 1)

            def turn_qk(u):
                for j in range(2):
                    bank = ps[1 - j]
                    pe.wait_ge(scaled, 2 * u.n + j + 1)
                    if j == 0:
                        pe.wait_ge(e_c, u.n + 1)
                    else:
                        pe.wait_ge(e_x, u.n + 1)
                        ge(pe, e_n, u.n - 1)
                    for k in range(2):
                        pe.transpose(bank[:, k * D:k * D + P], nqk[:, j, 2 * D + k * P:2 * D + (k + 1) * P], ident[:, :])
                        m = pe.transpose(bank[:, k * D + P:(k + 1) * D], nqk[:, j, D + k * P:D + (k + 1) * P], ident[:, :])
                    m.then_inc(t_k, 1)
                pe.wait_ge(e_k, 2 * u.n + 1)
                for k in range(2):
                    for j in range(2):
                        m = pe.transpose(ps[1][:, k * D + j * P:k * D + (j + 1) * P],
                                         nqk[:, j, k * P:(k + 1) * P], ident[:, :])
                m.then_inc(t_q, 1)

            def scores(u, j):
                b = 2 * u.n + j
                pe.wait_ge(mask_ready, u.n + 1)
                pe.wait_ge(e_q, u.n + 1)
                pe.wait_ge(e_k, b + 1)
                ge(pe, pt_act, b)
                ge(pe, pt_dve, b)
                for r in range(2):
                    pe.matmul(psS[:, r], ones_row[:, :], mask_row[0:1, u.par, j], start=True, stop=False)
                for ch in range(2):
                    for r in range(2):
                        rows = slice(r * DH, (r + 1) * DH)
                        m = pe.matmul(psS[:, r, ch], qT[rows, u.par, ch, j, :],
                                      kT[rows, 2 * u.par + j, ch, :], start=False, stop=ch == 1)
                m.then_inc(s_full, 1)

            def turn_probs(u, j):
                b = 2 * u.n + j
                pe.wait_ge(exp_done, b + 1)
                for key in range(2):
                    for g in range(H):
                        m = pe.transpose(psS[:, key].rearrange("p a n -> p (a n)")[:, g * P:(g + 1) * P],
                                         probs[:, j, g, key * P:(key + 1) * P], ident[:, :])
                m.then_inc(pt_full, 1)

            def mix_values(u, j):
                b = 2 * u.n + j
                pe.wait_ge(pt_act, b + 1)
                pe.wait_ge(pt_dve, b + 1)
                pe.wait_ge(pc_free, b + 1)
                ge(pe, y_done, b)
                for g in range(H):
                    h = 2 * (g % 2) + g // 2
                    for key in range(2):
                        m = pe.matmul(psO[:, g * (DH + 1):(g + 1) * (DH + 1)],
                                      probsT[:, j, key, g * P:(g + 1) * P], vv[:, 4 * u.par + 2 * j + key, h, :],
                                      start=key == 0, stop=key == 1)
                m.then_inc(pv_full, 1)

            def turn_o(u, j):
                b = 2 * u.n + j
                pe.wait_ge(on_done, b + 1)
                for k in range(2):
                    m = pe.transpose(psO[:, k * P:(k + 1) * P], o_n[:, k * P:(k + 1) * P], ident[:, :])
                m.then_inc(ot_full, 1)

            def out_proj(u, j):
                b = 2 * u.n + j
                pe.wait_ge(ot_ev, b + 1)
                for k in range(2):
                    m = pe.matmul(psO[:, D:2 * D], oT[:, k * P:(k + 1) * P], w_o[:, k, :], start=k == 0, stop=k == 1)
                m.then_inc(y_full, 1)

            def logits(u):
                pe.wait_ge(e_n, u.n + 1)
                pe.wait_ge(pc_free, upto(2 * u.n + 6, NB))
                for j in range(2):
                    for k in range(2):
                        m = pe.matmul(ps[4][:, D + j * E:D + (j + 1) * E], n1T[:, k, j * P:(j + 1) * P], w_r[:, k, :],
                                      start=k == 0, stop=k == 1)
                m.then_inc(lg_full, 1)

            def positions(u):
                pe.wait_ge(ch_done, u.n + 1)
                pe.wait_ge(lg_exp, u.n + 1)
                pe.wait_ge(before_done, u.n + 1)
                for j in range(2):
                    o = ps[4][:, D + (2 + j) * E:D + (3 + j) * E]
                    pe.matmul(o, tri[:, :], chosen[:, u.par, j, :], start=True, stop=False)
                    if j == 1:
                        pe.matmul(o, ones_sq[:, :], chosen[:, u.par, 0, :], start=False, stop=False)
                    pe.matmul(o, ones_sq[:, :], before[:, u.par, :], start=False, stop=True)
                pe.matmul(ps[4][:, D + 4 * E:D + 5 * E], ones_sq[:, :], before[:, 1 - u.par, :],
                          start=True, stop=True).then_inc(pos_full, 1)

            def step(s):
                a, cc = s + 1, s + -1
                if s.exists():
                    scores(s, 0)
                if a.exists():
                    turn_inputs(a)
                if cc.exists():
                    turn_n1(cc)
                if a.exists():
                    project(a, 0)
                if s.exists():
                    turn_probs(s, 0)
                if a.exists():
                    project(a, 1)
                if cc.exists():
                    logits(cc)
                if s.exists():
                    mix_values(s, 0)
                    scores(s, 1)
                    turn_o(s, 0)
                if cc.exists():
                    positions(cc)
                if s.exists():
                    out_proj(s, 0)
                    turn_probs(s, 1)
                if a.exists():
                    turn_qk(a)
                if s.exists():
                    mix_values(s, 1)
                    turn_o(s, 1)
                    out_proj(s, 1)

            turn_inputs(Unit(0, 0))
            project(Unit(0, 0), 0)
            project(Unit(0, 0), 1)
            turn_qk(Unit(0, 0))
            steps_of_phase_a(pe, step)

            pe.wait_ge(rows_ready, UNITS)

            pe.wait_ge(table_in, 16)
            pe.wait_ge(weights_e, 16 * 5)

            def turn_x(t, n):
                pe.wait_ge(xs_in[n], arrived(t, n))
                ge(pe, xst_ev, t - 1)
                for k in range(2):
                    m = pe.transpose(ps[n % 2][:, k * P:(k + 1) * P], xs[n][:, k * P:(k + 1) * P], ident[:, :])
                m.then_inc(xst_full, 1)

            def gate_up(t, n, e):
                pe.wait_ge(xst_ev, t + 1)
                ge(pe, hh_done, t - 1)
                for k in range(2):
                    m = pe.matmul(ps[2 + n % 2][:, 0:D], xsT[:, n % 4, k * P:(k + 1) * P],
                                  w_gu[:, at(e, 1), k, :].rearrange("p a n -> p (a n)"), start=k == 0, stop=k == 1)
                m.then_inc(gu_full, 1)

            def turn_h(t, n):
                pe.wait_ge(hh_done, t + 1)
                ge(pe, ht_ev, t - 1)
                pe.transpose((ps[4], psO)[n % 2][:, 0:P], hh[:, n % 4, :], ident[:, :]).then_inc(ht_full, 1)

            dbank = [psS[:, 0].rearrange("p a n -> p (a n)"), psS[:, 1].rearrange("p a n -> p (a n)")]

            def down_proj(t, n, e):
                pe.wait_ge(ht_ev, t + 1)
                ge(pe, yy_done, t - 1)
                pe.matmul(dbank[n % 2][:, 0:D], hT[:, n % 4, :],
                          w_dn[:, at(e, 1), :].rearrange("p a n -> p (a n)"), start=True, stop=True)\
                  .then_inc(dn_full, 1)

            def expert(t):
                return pe.value_load(tab[0:1, at(t, 1)], min_val=0, max_val=E - 1)

            turn_x(0, 0)
            turn_x(1, 1)
            for t in range(SLOTS):
                gate_up(t, t, expert(t))
                if t >= 2:
                    turn_h(t - 2, t - 2)
                turn_x(t + 2, (t + 2) % SLOTS)
                if t >= 3:
                    down_proj(t - 3, t - 3, expert(t - 3))
            now_regs = [pe.alloc_register(f"expert{d}") for d in range(SLOTS + 3)]
            with pe.Fori(SLOTS, TILES - 2 * SLOTS + 1, SLOTS) as t:
                pe.load(now_regs, tab[0:1, at(t - 3, SLOTS + 3)])
                now = [pe.snap(r, min_val=0, max_val=E - 1) for r in now_regs]
                for n in range(SLOTS):
                    gate_up(t + n, n, now[n + 3])
                    turn_h(t + (n - 2), (n - 2) % SLOTS)
                    turn_x(t + (n + 2), (n + 2) % SLOTS)
                    down_proj(t + (n - 3), (n - 3) % SLOTS, now[n])
            for t in range(TILES - SLOTS, TILES + 3):
                if t < TILES:
                    gate_up(t, t % SLOTS, expert(t))
                if t - 2 < TILES:
                    turn_h(t - 2, (t - 2) % SLOTS)
                if t + 2 < TILES:
                    turn_x(t + 2, (t + 2) % SLOTS)
                down_proj(t - 3, (t - 3) % SLOTS, expert(t - 3))

            pe.wait_ge(yy_done, TILES)
            pe.wait_ge(ht_ev, TILES)

            def shared_turn(u):
                pe.wait_ge(nh, u.n + 1)
                ge(pe, nt_ev, u.n)
                for j in range(2):
                    for k in range(2):
                        m = pe.transpose(ps[0][:, k * D + j * P:k * D + (j + 1) * P],
                                         n1h[:, j, k * P:(k + 1) * P], ident[:, :])
                m.then_inc(nt_full, 1)

            def shared_up(u):
                pe.wait_ge(nt_ev, u.n + 1)
                for mm in range(2):
                    ge(pe, sh_done, 2 * u.n - 1 + mm)
                    for which, w in ((0, w_sg), (1, w_su)):
                        for k in range(2):
                            m = pe.matmul(ps[1 + 2 * mm + which][:, 0:D], w[:, k, mm * P:(mm + 1) * P], ncT[:, k, :],
                                          start=k == 0, stop=k == 1)
                    m.then_inc(sgu_full, 1)

            def shared_down(u):
                pe.wait_ge(sh_done, 2 * u.n + 2)
                for j in range(2):
                    ge(pe, res_done, 2 * u.n + j - 1)
                    for mm in range(2):
                        m = pe.matmul(dbank[j][:, 0:D], shh[:, mm, j * P:(j + 1) * P], w_sd[:, mm, :],
                                      start=mm == 0, stop=mm == 1)
                    m.then_inc(sd_full, 1)

            def shared(u):
                shared_turn(u)
                shared_up(u)
                shared_down(u)

            shared(Unit(0, 0))
            shared(Unit(0, 1))
            with pe.Fori(1, UNITS // 2) as i:
                shared(Unit(i, 0))
                shared(Unit(i, 1))

        @block.scalar
        def _(act):
            act.wait_ge(consts, 16 * CONSTS)
            act.wait_ge(made, MADE)

            def inputs(u):
                act.wait_ge(t_x, u.n + 1)
                ge(act, pc_full, 2 * u.n)
                for k in range(2):
                    a = act.activation(lnT[:, k, :], ps[0][:, k * D:(k + 1) * D], ACT.Identity,
                                       bias=bl[:, k:k + 1], scale=gl[:, k:k + 1])
                a.then_inc(e_x, 1)
                act.wait_ge(t_c, u.n + 1)
                act.activation(cT[:, 0, :], ps[1][:, 0:D], ACT.Identity, bias=bx[:, 0:1], scale=gx[:, 0:1])
                act.activation(cT[0:KC, 1, :], ps[1][0:KC, D:2 * D], ACT.Identity,
                               bias=bx[0:KC, 1:2], scale=gx[0:KC, 1:2]).then_inc(e_c, 1)

            def projected(u, j):
                b = 2 * u.n + j
                act.wait_ge(pa_full, b + 1)
                ge(act, ss_done, b)
                act.activation(sq[:, 0:2 * D], ps[2][:, :], ACT.Square)
                ge(act, scaled, 2 * u.n - 1 + j)
                act.activation(raw[:, j, 0:2 * D], ps[2][:, :], ACT.Copy).then_inc(pa_free, 1)
                act.wait_ge(pb_full, b + 1)
                act.activation(sq[:, 2 * D:3 * D], ps[3][:, 0:D], ACT.Square).then_inc(sq_full, 1)
                act.activation(raw[:, j, 2 * D:3 * D], ps[3][:, 0:D], ACT.Copy)
                ge(act, pv_full, 2 * u.n - 3 + j)
                act.activation(vv[:, 4 * u.par + 2 * j, :, 0:DH],
                               ps[3][:, D:2 * D].rearrange("p (h d) -> p h d", d=DH), ACT.Copy).then_inc(pb_free, 1)
                act.wait_ge(pc_full, b + 1)
                act.activation(vv[:, 4 * u.par + 2 * j + 1, :, 0:DH],
                               ps[4][:, 0:D].rearrange("p (h d) -> p h d", d=DH), ACT.Copy).then_inc(pc_free, 1)

            def exps(u, j):
                b = 2 * u.n + j
                act.wait_ge(m_done, b + 1)
                ge(act, pt_full, b - 1)
                for g in range(H):
                    a = act.activation(probs[:, j, g, :], psS[:, g // 2, g % 2], ACT.Exp,
                                       bias=nmax[:, j, g:g + 1])
                a.then_inc(exp_done, 1)

            def probs_copy(u, j):
                b = 2 * u.n + j
                act.wait_ge(pt_full, b + 1)
                ge(act, pv_full, b - 1)
                act.activation(probsT[:, j, 1, :], psS[:, 1].rearrange("p a n -> p (a n)"), ACT.Copy).then_inc(pt_act, 1)

            def o_copy(u, j):
                b = 2 * u.n + j
                act.wait_ge(ot_full, b + 1)
                ge(act, y_full, b)
                act.activation(oT, psO[:, 0:D], ACT.Copy).then_inc(ot_ev, 1)

            def n1_copy(u):
                act.wait_ge(t_n, u.n + 1)
                ge(act, lg_full, u.n)
                act.activation(n1T.rearrange("p k n -> p (k n)"), ps[0][:, :], ACT.Copy).then_inc(e_n, 1)

            def logit_exp(u):
                act.wait_ge(lg_full, u.n + 1)
                ge(act, ch_done, u.n)
                act.activation(esc[:, :, :].rearrange("p j e -> p (j e)"), ps[4][:, D:D + 2 * E], ACT.Exp,
                               scale=-1.0).then_inc(lg_exp, 1)

            def step(s):
                a, cc = s + 1, s + -1
                if a.exists():
                    inputs(a)
                if cc.exists():
                    n1_copy(cc)
                if s.exists():
                    exps(s, 0)
                if a.exists():
                    projected(a, 0)
                if s.exists():
                    probs_copy(s, 0)
                if a.exists():
                    projected(a, 1)
                if cc.exists():
                    logit_exp(cc)
                if s.exists():
                    exps(s, 1)
                    o_copy(s, 0)
                    probs_copy(s, 1)
                    o_copy(s, 1)

            inputs(Unit(0, 0))
            projected(Unit(0, 0), 0)
            projected(Unit(0, 0), 1)
            steps_of_phase_a(act, step)

            def rows_copy(t, n):
                act.wait_ge(xst_full, t + 1)
                ge(act, gu_full, t - 3)
                act.activation(xsT[:, n % 4, :], ps[n % 2][:, 0:D], ACT.Copy).then_inc(xst_ev, 1)

            def gate_silu(t, n):
                act.wait_ge(gu_full, t + 1)
                ge(act, hh_done, t - 3)
                act.activation(sg[:, n % 4, :], ps[2 + n % 2][:, 0:I], ACT.Silu).then_inc(sg_done, 1)

            rows_copy(0, 0)
            rows_copy(1, 1)
            for t in range(SLOTS):
                gate_silu(t, t)
                rows_copy(t + 2, (t + 2) % SLOTS)
            with act.Fori(SLOTS, TILES - 2 * SLOTS + 1, SLOTS) as t:
                for n in range(SLOTS):
                    gate_silu(t + n, n)
                    rows_copy(t + (n + 2), (n + 2) % SLOTS)
            for t in range(TILES - SLOTS, TILES):
                gate_silu(t, t % SLOTS)
                if t + 2 < TILES:
                    rows_copy(t + 2, (t + 2) % SLOTS)

            act.wait_ge(dn_full, TILES)
            out_d = out.rearrange("b p n -> p b n")

            def shared(u):
                act.wait_ge(nt_full, u.n + 1)
                ge(act, sgu_full, 2 * u.n)
                act.activation(ncT.rearrange("p k n -> p (k n)"), ps[0][:, :], ACT.Copy).then_inc(nt_ev, 1)
                for mm in range(2):
                    act.wait_ge(sgu_full, 2 * u.n + mm + 1)
                    ge(act, sh_done, 2 * u.n - 1 + mm)
                    act.activation(shs[:, mm, :], ps[1 + 2 * mm][:, 0:D], ACT.Silu).then_inc(ssg_done, 1)

            def store(u):
                act.wait_ge(res_done, 2 * u.n + 2)
                act.dma_start(out_d[:, at(2 * u.n, 2), :], res[:, u.par]).then_inc(stored[u.par], 16)

            shared(Unit(0, 0))
            shared(Unit(0, 1))
            store(Unit(0, 0))
            with act.Fori(1, UNITS // 2) as i:
                shared(Unit(i, 0))
                store(Unit(i - 1, 1))
                shared(Unit(i, 1))
                store(Unit(i, 0))
            store(Unit(UNITS // 2 - 1, 1))
            for s in stored:
                act.wait_ge(s, 16 * UNITS // 2)

        @block.vector
        def _(dve):
            dve.wait_ge(consts, 16 * CONSTS)
            dve.wait_ge(made, MADE)

            def chain(order, per_unit, u):
                n = [0]

                def link(ins, before_plain=False):
                    n[0] += 1
                    ins.then_inc(order, 1)
                    (apart if before_plain else ge)(dve, order, per_unit * u.n + n[0])

                return link, n

            def rsqrt(link, y, v, w):
                g, t = ry[:, 0:w], rt[:, 0:w]
                link(dve.tensor_scalar(t.bitcast(i32), v.bitcast(i32), 1, None, ALU.logical_shift_right))
                link(dve.tensor_scalar(g.bitcast(i32), t.bitcast(i32), -1.0, float(0x5f3759df), ALU.mult, ALU.add))
                for n in range(3):
                    link(dve.scalar_tensor_tensor(t, g, -0.5, g, ALU.mult, ALU.mult))
                    link(dve.tensor_tensor(t, t, v, ALU.mult))
                    link(dve.scalar_tensor_tensor(y if n == 2 else g, t, 1.5, g, ALU.add, ALU.mult))

            dve.tensor_tensor(gqk[:, 0:1], gqk[:, 1:2], gqk[:, 2:3], ALU.mult).then_inc(gains, 1)
            dve.wait_ge(gains, 1)
            dve.tensor_scalar(gqk[:, 0:1], gqk[:, 0:1], SCALE, None, ALU.mult).then_inc(gains, 1)
            dve.wait_ge(gains, 2)

            def statistics(u):
                link, n = chain(d1, S1_LINKS, u)
                dve.wait_ge(loaded[u.par], 48 * (u.i + 1))
                apart(dve, hats, u.n)
                for j in range(2):
                    dve.bn_stats(stats[:, j, :], x1[:, at(2 * u.n + j, 1), :].rearrange("p a n -> p (a n)"))
                dve.bn_stats(stats[:, 2, :], c_in[:, u.par, 0, :])
                link(dve.bn_stats(stats[:, 3, :], c_in[:, u.par, 1, :]), True)
                for j in range(3):
                    dve.bn_aggr(mv[:, j, :], stats[:, j, :])
                link(dve.bn_aggr(mv[:, 3, :], stats[:, 3, :]))
                dve.tensor_scalar(va[:, 0:2], mv[:, 0:2, 1], 1.0 + LN_EPS, LN_EPS * LN_EPS, ALU.mult, ALU.add)
                link(dve.tensor_scalar(va[:, 2:4], mv[:, 2:4, 1], LN_EPS, None, ALU.add))
                rsqrt(link, ra[:, :], va[:, :], 4)
                ge(dve, t_x, u.n)
                for j in range(2):
                    m = dve.tensor_scalar(x_hat[:, j, :], x1[:, at(2 * u.n + j, 1), :].rearrange("p a n -> p (a n)"),
                                          mv[:, j, 0:1], ra[:, j:j + 1], ALU.subtract, ALU.mult)
                m.then_inc(xhat, 1)
                assert n[0] == S1_LINKS

            def square_sums(u, j):
                b = 2 * u.n + j
                dve.wait_ge(sq_full, b + 1)
                dve.tensor_reduce(ss[:, 12 * j:12 * j + 12], sq.rearrange("p (g d) -> p g d", d=DH), AX, ALU.add)\
                   .then_inc(ss_done, 1)

            def head_norms(u):
                link, n = chain(d2, S2_LINKS, u)
                ge(dve, scaled, 2 * u.n)
                dve.wait_ge(ss_done, 2 * u.n + 2)
                link(dve.tensor_scalar(ss[:, :], ss[:, :], 1.0 / DH, RMS_EPS * RMS_EPS, ALU.mult, ALU.max))
                rsqrt(link, rq[:, :], ss[:, :], 24)
                assert n[0] == S2_LINKS

            def qk_copy(u):
                for j in range(2):
                    dve.wait_ge(t_k, 2 * u.n + j + 1)
                    ge(dve, s_full, 2 * (u.n - 2) + j + 1)
                    dve.tensor_copy(kT[:, 2 * u.par + j].rearrange("p k n -> p (k n)"), ps[1 - j][:, :]).then_inc(e_k, 1)
                dve.wait_ge(t_q, u.n + 1)
                dve.tensor_scalar(qT[:, u.par].rearrange("p k j n -> p (k j n)"), ps[1][:, :], gqk[:, 0:1], None, ALU.mult)\
                   .then_inc(e_q, 1)

            def maxima(u, j):
                b = 2 * u.n + j
                dve.wait_ge(s_full, b + 1)
                ge(dve, exp_done, b - 1)
                dve.tensor_reduce(nmax[:, j, :], psS[:, :, :, :].rearrange("p r k n -> p (r k) n"), AX, ALU.max,
                                  negate=True).then_inc(m_done, 1)

            def probs_copy(u, j):
                b = 2 * u.n + j
                dve.wait_ge(pt_full, b + 1)
                ge(dve, pv_full, b - 1)
                dve.tensor_copy(probsT[:, j, 0, :], psS[:, 0].rearrange("p a n -> p (a n)")).then_inc(pt_dve, 1)

            def normalise_o(u, j):
                b = 2 * u.n + j
                dve.wait_ge(pv_full, b + 1)
                ge(dve, ot_full, b)
                o = psO[:, 0:H * (DH + 1)].rearrange("p (g d) -> p g d", d=DH + 1)
                dve.reciprocal(rden[:, :], o[:, :, DH]).then_inc(dS, 1)
                dve.wait_ge(dS, b + 1)
                dve.tensor_tensor(o_n.rearrange("p (k r d) -> p r k d", k=2, r=2),
                                  o[:, :, 0:DH].rearrange("p (r k) d -> p r k d", k=2),
                                  rden[:, :].rearrange("p (r k o) -> p r k o", k=2, o=1).to_broadcast([P, 2, 2, DH]),
                                  ALU.mult).then_inc(on_done, 1)

            def residual(u, j):
                b = 2 * u.n + j
                dve.wait_ge(y_full, b + 1)
                dve.tensor_tensor(y_b, psO[:, D:2 * D], bo_b[:, :], ALU.add).then_inc(y_done, 1)
                dve.wait_ge(y_done, b + 1)
                xb = x1[:, at(b, 1), :].rearrange("p a n -> p (a n)")
                dve.tensor_tensor(xb, xb, y_b, ALU.add).then_inc(x1_done, 1)

            def norm_rows(u):
                link, n = chain(d3, S3A_LINKS + S3B_LINKS, u)
                apart(dve, x1_done, 2 * u.n + 2)
                for j in range(2):
                    m = dve.bn_stats(stats[:, j, :], x1[:, at(2 * u.n + j, 1), :].rearrange("p a n -> p (a n)"))
                link(m, True)
                for j in range(2):
                    m = dve.bn_aggr(mv2[:, j, :], stats[:, j, :])
                link(m)
                dve.tensor_copy(mr[:, at(2 * u.n, 2), 0:1], mv2[:, :, 0:1])
                link(dve.tensor_scalar(v1[:, :], mv2[:, :, 1], LN_EPS, None, ALU.add))
                rsqrt(link, r1[:, :], v1[:, :], 2)
                dve.tensor_copy(mr[:, at(2 * u.n, 2), 1:2], r1[:, :].rearrange("p (j o) -> p j o", o=1))
                assert n[0] == S3A_LINKS
                ge(dve, scat[u.par], 128 * u.i)
                for j in range(2):
                    xb = x1[:, at(2 * u.n + j, 1), :]
                    dve.tensor_scalar(pay[:, 2 * u.par + j, :, 0:D], xb.to_broadcast([P, TOPK, D]),
                                      mv2[:, j, 0:1], r1[:, j:j + 1], ALU.subtract, ALU.mult).then_inc(pay_x, 1)

            def route(u):
                link, n = chain(d3, S3A_LINKS + S3B_LINKS, u)
                n[0] = S3A_LINKS
                dve.wait_ge(lg_exp, u.n + 1)
                link(dve.tensor_scalar(esc[:, :, :], esc[:, :, :], 1.0, None, ALU.add))
                link(dve.reciprocal(sc[:, :, :], esc[:, :, :]))
                link(dve.tensor_tensor(sfc[:, :, :], sc[:, :, :], rb_b[:, :, :].to_broadcast([P, 2, E]), ALU.add), True)
                for j in range(2):
                    for g in range(NG):
                        m = dve.max(g8[:, j, g, :], sfc[:, j, 8 * g:8 * g + 8])
                link(m)
                link(dve.tensor_tensor(gs[:, :, 0:NG], g8[:, :, :, 0], g8[:, :, :, 1], ALU.add), True)
                for j in range(2):
                    m = dve.max(m8[:, j, :], gs[:, j, :])
                link(m, True)
                for j in range(2):
                    m = dve.match_replace(gr[:, j, :], m8[:, j, :], gs[:, j, :], -BIG)
                link(m)
                link(dve.tensor_tensor(gm[:, :, :], gr[:, :, 0:NG], gs[:, :, 0:NG], ALU.not_equal))
                for j in range(2):
                    m = dve.tensor_tensor(t36[:, j, 0:E].rearrange("p (g e) -> p g e", g=NG),
                                          sfc[:, j, :].rearrange("p (g e) -> p g e", g=NG),
                                          gm[:, j, :].rearrange("p (g o) -> p g o", o=1).to_broadcast([P, NG, E // NG]),
                                          ALU.mult)
                link(m, True)
                for j in range(2):
                    m = dve.max(n8[:, j, :], t36[:, j, :])
                link(m, True)
                for j in range(2):
                    m = dve.match_replace(r36[:, j, :], n8[:, j, :], t36[:, j, :], -BIG)
                link(m)
                ge(dve, pos_full, u.n)
                link(dve.tensor_tensor(chosen[:, u.par], r36[:, :, 0:E], t36[:, :, 0:E], ALU.not_equal))
                dve.tensor_tensor(before[:, 1 - u.par, :], before[:, u.par, :], chosen[:, u.par, 0, :], ALU.add)\
                   .then_inc(ch_done, 1)
                link(dve.tensor_tensor(wts[:, :, :], chosen[:, u.par], sc[:, :, :], ALU.mult))
                dve.tensor_tensor(before[:, 1 - u.par, :], before[:, 1 - u.par, :], chosen[:, u.par, 1, :], ALU.add)\
                   .then_inc(before_done, 1)
                link(dve.tensor_reduce(wsum[:, :], wts[:, :, :], AX, ALU.add))
                link(dve.tensor_scalar(wsum[:, :], wsum[:, :], 1e-20, None, ALU.add))
                link(dve.reciprocal(wsum[:, :], wsum[:, :]))
                dve.wait_ge(pos_full, u.n + 1)
                rank = ps[4][:, D + 2 * E:D + 4 * E].rearrange("p (j e) -> p j e", j=2)
                both = [P, 2, E]
                link(dve.tensor_scalar(need_i[:, :], ps[4][:, D + 4 * E:D + 5 * E], float(P - 1), None, ALU.add))
                link(dve.tensor_scalar(need[:, 0, :], need_i[:, :], 7, 7, ALU.logical_shift_right, ALU.logical_shift_left))
                dve.tensor_tensor(later[:, :, :], rank, kept[:, :, :].to_broadcast(both), ALU.is_ge)
                dve.scalar_tensor_tensor(code[:, :, :], rank, 1.0, off[:, :, :].to_broadcast(both), ALU.add, ALU.add)
                link(dve.tensor_tensor(new[:, :, :], need[:, :, :], kept[:, :, :], ALU.subtract))
                link(dve.tensor_tensor_scan(given[:, u.par, :], ones_e[:, :], new[:, 0, :],
                                            given[:, 1 - u.par, E - 1:E], ALU.mult, ALU.add))
                link(dve.tensor_tensor(off_n[:, :, :], given[:, u.par:u.par + 1, :], need[:, :, :], ALU.subtract))
                link(dve.tensor_tensor(delta[:, :, :], off_n[:, :, :], off[:, :, :], ALU.subtract))
                dve.tensor_tensor(later[:, :, :], later[:, :, :], delta[:, :, :].to_broadcast(both), ALU.mult)
                link(dve.scalar_tensor_tensor(moved[:, :, :], new[:, :, :], 0.0, delta[:, :, :], ALU.is_gt, ALU.mult))
                dve.tensor_tensor(code[:, :, :], code[:, :, :], later[:, :, :], ALU.add)
                dve.tensor_tensor(off[:, :, :], off[:, :, :], moved[:, :, :], ALU.add)
                dve.tensor_copy(kept[:, :, :], need[:, :, :])
                link(dve.tensor_copy(history[:, at(u.n, 1), :], given[:, u.par:u.par + 1, :]))
                link(dve.tensor_tensor(code2[:, :, :], code[:, :, :], chosen[:, u.par], ALU.mult), True)
                for j in range(2):
                    m = dve.max(c8[:, j, :], code2[:, j, :])
                link(m)
                for j in range(2):
                    for k in range(TOPK):
                        m = dve.scalar_tensor_tensor(wj[:, j, k, :], code2[:, j, :], c8[:, j, k:k + 1], wts[:, j, :],
                                                     ALU.is_equal, ALU.mult, accum_out=w4[:, j, k:k + 1])
                link(m)
                dve.tensor_scalar(slot[:, u.par], c8[:, :, 0:TOPK], -1.0, None, ALU.add)
                for j in range(2):
                    dve.tensor_scalar(pay[:, 2 * u.par + j, :, D:D + 1],
                                      w4[:, j, :].rearrange("p (k o) -> p k o", o=1), wsum[:, j:j + 1], ROUTE_SCALE,
                                      ALU.mult, ALU.mult)
                    m = dve.tensor_copy(pay[:, 2 * u.par + j, :, D + 1:ROW].bitcast(i32),
                                        place[:, j, :].rearrange("p (k o) -> p k o", o=1))
                link(m)
                dve.tensor_scalar(place[:, :, :], place[:, :, :], float(2 * P * TOPK), None, ALU.add).then_inc(rows_ready, 1)
                dve.wait_ge(rows_ready, u.n + 1)
                assert n[0] - S3A_LINKS == S3B_LINKS, n[0] - S3A_LINKS

            def step(s):
                a, cc = s + 1, s + -1
                if cc.exists():
                    norm_rows(cc)
                if s.exists():
                    maxima(s, 0)
                if (s + 2).exists():
                    statistics(s + 2)
                if a.exists():
                    square_sums(a, 0)
                if s.exists():
                    probs_copy(s, 0)
                if a.exists():
                    square_sums(a, 1)
                    head_norms(a)
                if s.exists():
                    normalise_o(s, 0)
                    maxima(s, 1)
                if cc.exists():
                    route(cc)
                if s.exists():
                    residual(s, 0)
                    probs_copy(s, 1)
                if a.exists():
                    qk_copy(a)
                if s.exists():
                    normalise_o(s, 1)
                    residual(s, 1)

            statistics(Unit(0, 0))
            square_sums(Unit(0, 0), 0)
            square_sums(Unit(0, 0), 1)
            head_norms(Unit(0, 0))
            statistics(Unit(0, 1))
            qk_copy(Unit(0, 0))
            steps_of_phase_a(dve, step)

            for q in range(NPT):
                m = dve.tensor_scalar(hist_j[:, :], history[:, :, :].rearrange("p u e -> p (u e)"), first[:, q:q + 1],
                                      0.0, ALU.is_le, ALU.add, accum_out=page_e[:, q:q + 1])
                m.then_inc(dB, 1)
                dve.wait_ge(dB, q + 1)
            dve.tensor_copy(page_i[:, :], page_e[:, :]).then_inc(dB, 1)
            dve.wait_ge(dB, NPT + 1)
            dve.tensor_scalar(tab_pc[:, :], page_i[:, :], E - 1, None, ALU.bitwise_and).then_inc(table_made, 1)

            def hidden(t, n):
                dve.wait_ge(sg_done, t + 1)
                ge(dve, ht_full, t - 3)
                dve.scalar_tensor_tensor(hh[:, n % 4, :], sg[:, n % 4, :], xs[n][:, D:D + 1],
                                         ps[2 + n % 2][:, I:2 * I], ALU.mult, ALU.mult).then_inc(hh_done, 1)

            def hidden_copy(t, n):
                dve.wait_ge(ht_full, t + 1)
                ge(dve, dn_full, t - 3)
                dve.tensor_copy(hT[:, n % 4, :], (ps[4], psO)[n % 2][:, 0:P]).then_inc(ht_ev, 1)

            dbank = [psS[:, 0].rearrange("p a n -> p (a n)"), psS[:, 1].rearrange("p a n -> p (a n)")]

            def result_copy(t, n):
                dve.wait_ge(dn_full, t + 1)
                ge(dve, y_out[n], left(t, n))
                dve.tensor_copy(yy[n], dbank[n % 2][:, 0:D]).then_inc(yy_done, 1)

            def tile_step(t, n):
                if not isinstance(t, int) or t < TILES:
                    hidden(t, n)
                if not isinstance(t, int) or 2 <= t < TILES + 2:
                    hidden_copy(t + -2, (n - 2) % SLOTS)
                if not isinstance(t, int) or t >= 3:
                    result_copy(t + -3, (n - 3) % SLOTS)

            for t in range(2 * SLOTS):
                tile_step(t, t % SLOTS)
            with dve.Fori(2 * SLOTS, TILES - SLOTS + 1, SLOTS) as t:
                for n in range(SLOTS):
                    tile_step(t + n, n)
            for t in range(TILES, TILES + 3):
                tile_step(t, t % SLOTS)

            def norm_again(u):
                ge(dve, nt_full, u.n)
                for j in range(2):
                    b = at(2 * u.n + j, 1)
                    m = dve.tensor_scalar(n1h[:, j, :], x1[:, b, :].rearrange("p a n -> p (a n)"),
                                          mr[:, b, 0:1].rearrange("p a n -> p (a n)"),
                                          mr[:, b, 1:2].rearrange("p a n -> p (a n)"), ALU.subtract, ALU.mult)
                m.then_inc(nh, 1)

            def shared(u):
                for mm in range(2):
                    dve.wait_ge(ssg_done, 2 * u.n + mm + 1)
                    ge(dve, sd_full, 2 * u.n)
                    dve.tensor_tensor(shh[:, mm, :], shs[:, mm, :], ps[2 + 2 * mm][:, 0:D], ALU.mult).then_inc(sh_done, 1)
                dve.wait_ge(er_in[u.par], 16 * (u.i + 1))
                dve.tensor_tensor(e2, er[:, u.par, :, 0:2, :], er[:, u.par, :, 2:4, :], ALU.add).then_inc(dC, 1)
                dve.wait_ge(dC, u.n + 1)
                dve.tensor_tensor(esum, e2[:, :, 0, :], e2[:, :, 1, :], ALU.add).then_inc(dD, 1)
                dve.wait_ge(dD, 2 * u.n + 1)
                ge(dve, stored[u.par], 16 * u.i)
                dve.tensor_tensor(res[:, u.par], esum, x1[:, at(2 * u.n, 2), :], ALU.add).then_inc(dD, 1)
                dve.wait_ge(dD, 2 * u.n + 2)
                for j in range(2):
                    dve.wait_ge(sd_full, 2 * u.n + j + 1)
                    dve.tensor_tensor(res[:, u.par, j, :], res[:, u.par, j, :], dbank[j][:, 0:D], ALU.add)\
                       .then_inc(res_done, 1)

            dve.wait_ge(dn_full, TILES)
            norm_again(Unit(0, 0))
            shared(Unit(0, 0))
            norm_again(Unit(0, 1))
            shared(Unit(0, 1))
            with dve.Fori(1, UNITS // 2) as i:
                for par in range(2):
                    norm_again(Unit(i, par))
                    shared(Unit(i, par))


def kernel(x, ctx_768, mask_BxS2_bk0, L0_xattn_ln_x_g, L0_xattn_ln_x_b, L0_xattn_ln_l_g, L0_xattn_ln_l_b,
           L0_xattn_qn_g, L0_xattn_kn_g, L0_xattn_Wq, L0_xattn_Wkv, L0_xattn_Wlkv, L0_xattn_Wo, L0_xattn_bo,
           L0_ffn_router_weight, L0_ffn_router_bias, L0_ffn_gate_w, L0_ffn_up_w, L0_ffn_down_w,
           L0_ffn_shared_gate_w, L0_ffn_shared_up_w, L0_ffn_shared_down_w):
    import numpy as np
    import concourse.bacc as bacc
    from concourse.bass_utils import run_bass_kernel_spmd

    def by_chunk(w):
        return np.asarray(w).transpose(2, 0, 1).reshape(2, P, E, I).transpose(1, 0, 2, 3)

    arrays = dict(
        x=x, ctx=ctx_768, mask=np.asarray(mask_BxS2_bk0).reshape(1, NB, P),
        ln_x_g=L0_xattn_ln_x_g, ln_x_b=L0_xattn_ln_x_b, ln_l_g=L0_xattn_ln_l_g, ln_l_b=L0_xattn_ln_l_b,
        qn_g=L0_xattn_qn_g, kn_g=L0_xattn_kn_g,
        wq=np.asarray(L0_xattn_Wq).T, wkv=np.asarray(L0_xattn_Wkv).T, wlkv=np.asarray(L0_xattn_Wlkv).T,
        wo=np.asarray(L0_xattn_Wo).T, bo=L0_xattn_bo,
        rw=np.asarray(L0_ffn_router_weight).T, rb=L0_ffn_router_bias,
        gate=by_chunk(L0_ffn_gate_w), up=by_chunk(L0_ffn_up_w),
        down=np.asarray(L0_ffn_down_w).transpose(2, 0, 1),
        sgate=np.asarray(L0_ffn_shared_gate_w).T, sup=np.asarray(L0_ffn_shared_up_w).T,
        sdown=np.asarray(L0_ffn_shared_down_w).T)
    arrays = {k: np.ascontiguousarray(v) for k, v in arrays.items()}
    nc = bacc.Bacc("TRN2", target_bir_lowering=False, num_devices=1)
    args = [nc.dram_tensor(f"in_{k}", v.shape, mybir.dt.from_np(v.dtype), kind="ExternalInput").ap()
            for k, v in arrays.items()]
    out = nc.dram_tensor("out_0", (NB, P, D), mybir.dt.float32, kind="ExternalOutput").ap()
    with nc.allow_non_contiguous_dma(reason="gains by partition and the tile table: a few small loads"):
        build(nc, *args, out)
    r = run_bass_kernel_spmd(nc, [{f"in_{k}": v for k, v in arrays.items()}], core_ids=[0])
    return r.results[0]["out_0"]
```

```python
import concourse.bass as bass
from concourse import mybir
from contextlib import ExitStack

P = 128
NB, D, DC = 64, 256, 192
H, DH = 4, 64
E, I, TOPK, NG = 32, 128, 4, 4
UNITS = NB // 2
T = NB * P
ROW = D + 2
TILES = (T * TOPK + E * (P - 1)) // P
SLOTS = 8
TILES = -(-TILES // SLOTS) * SLOTS
FILL = 4
NPT = -(-TILES // P)
KC = DC - P
LN_EPS, RMS_EPS = 1e-5, 1e-8
SCALE, ROUTE_SCALE = DH ** -0.5, 2.5
NEG = 1e30
BIG = 3e38
NOWHERE = T * TOPK + 7


class Unit:

    def __init__(self, i, par):
        self.i, self.par = i, par
        self.n = 2 * i + par

    def __add__(self, d):
        q, r = divmod(self.par + d, 2)
        return Unit(self.i + q, r)

    def exists(self):
        return not isinstance(self.n, int) or 0 <= self.n < UNITS


def ge(eng, sem, value):
    if isinstance(value, int) and value <= 0:
        return
    eng.wait_ge(sem, value)


def upto(value, cap):
    return min(value, cap) if isinstance(value, int) else value


def at(start, n):
    return slice(start, start + n) if isinstance(start, int) else bass.ds(start, n)


def steps_of_phase_a(eng, step, peeled=4):
    for s in range(4):
        step(Unit(s // 2, s % 2))
    with eng.Fori(2, (UNITS + 2 - peeled) // 2) as i:
        step(Unit(i, 0))
        step(Unit(i, 1))
    for s in range(UNITS + 2 - peeled, UNITS + 2):
        step(Unit(s // 2, s % 2))


RSQRT_STEPS = 8
N_LINKS = 4 + RSQRT_STEPS
C_LINKS, R_LINKS = 16, 26
H_LINKS = 1 + RSQRT_STEPS
BLANK_UNIT = 16 * 2 * TOPK // FILL
CONSTS = 23
MADE = 16


def build(nc, x, ctx, mask, ln_x_g, ln_x_b, ln_l_g, ln_l_b, qn_g, kn_g, wq, wkv, wlkv, wo, bo,
          rw, rb, gate, up, down, sgate, sup, sdown, out):
    fp32, bf16, i32, u8 = mybir.dt.float32, mybir.dt.bfloat16, mybir.dt.int32, mybir.dt.uint8
    ALU, ACT, AX = mybir.AluOpType, mybir.ActivationFunctionType, mybir.AxisListType.X

    lists = nc.dram_tensor("lists", [TILES * P, ROW], fp32).ap()
    expert_out = nc.dram_tensor("expert_out", [T * TOPK, D], fp32).ap()
    tile_table = nc.dram_tensor("tile_table", [NPT * P], i32).ap()

    with ExitStack() as c:
        def sb(name, shape, dt=fp32):
            return c.enter_context(nc.sbuf_tensor(name, shape, dt))

        def pb(name, shape):
            return c.enter_context(nc.psum_tensor(name, shape, fp32))

        def sem(name):
            return c.enter_context(nc.semaphore(name))

        x1 = sb("x1", [P, NB, D])
        mr = sb("mr", [P, NB, 2])
        ident = sb("ident", [P, P])
        w_sg = sb("w_sg", [P, 2, 2 * P])
        w_su = sb("w_su", [P, 2, 2 * P])
        w_sd = sb("w_sd", [P, 2, D])
        arena = sb("arena", [P, E * 3 * D])
        used = [0]

        def part(*shape):
            n = 1
            for s in shape:
                n *= s
            v = arena[:, used[0]:used[0] + n]
            used[0] += n
            if len(shape) == 1:
                return v
            names = "abcd"[:len(shape)]
            return v.rearrange(f"p ({' '.join(names)}) -> p {' '.join(names)}",
                               **dict(zip(names, shape)))

        w_lat = part(2, 3 * D)
        w_ctx = part(2, 2 * D)
        w_o = part(2, D)
        w_r = part(2, E)
        c_in = part(2, 2, DC)
        x_hat = part(2, D)
        c_hat = part(2, DC)
        lnT = part(2, 2 * P)
        cT = part(2, 2 * P)
        sq = part(2, 3 * D)
        raw = part(2, 3 * D)
        nqk = part(2, 3 * D)
        qT = part(2, 2, 2, P)
        kT = part(4, 2, 2 * P)
        probs = part(2, H, 2 * P)
        probsT = part(2, 2, H * P)
        o_n = part(D)
        oT = part(D)
        n1T = part(2, 2 * P)
        vv = part(4 * 2, H, DH + 1)
        wj = part(2, TOPK, E)
        assert used[0] <= E * 3 * D
        w_gu = arena[:, 0:E * 2 * D].rearrange("p (e k n) -> p e k n", e=E, k=2)
        w_dn = arena[:, E * 2 * D:E * 3 * D].rearrange("p (e n) -> p e n", e=E)

        pay = sb("pay", [P, 4, TOPK, ROW])
        mask_u8 = sb("mask_u8", [1, 2, 2, P], u8)
        mask_row = sb("mask_row", [1, 2, 2, 2, 2 * P], bf16)
        ones_row = sb("ones_row", [1, P], bf16)
        ones_sq = sb("ones_sq", [P, P], bf16)
        tri = sb("tri", [P, P], bf16)
        gl, bl = sb("gl", [P, 2]), sb("bl", [P, 2])
        gx, bx = sb("gx", [P, 2]), sb("bx", [P, 2])
        gqk = sb("gqk", [P, 3])
        bo_b = sb("bo_b", [P, D])
        rb_b = sb("rb_b", [P, 1, E])
        stats = sb("stats", [P, 6, 6])
        mv = sb("mv", [P, 6, 2])
        va, ra, nb = sb("va", [P, 6]), sb("ra", [P, 6]), sb("nb", [P, 6])
        ss, rq = sb("ss", [P, 24]), sb("rq", [P, 24])
        ry, rt = sb("ry", [P, 6]), sb("rt", [P, 6])
        hy, ht = sb("hy", [P, 24]), sb("ht", [P, 24])
        nmax = sb("nmax", [P, 2, H])
        rden = sb("rden", [P, H])
        esc = sb("esc", [P, 2, E])
        sc = sb("sc", [P, 2, E])
        sfc = sb("sfc", [P, 2, E])
        g8 = sb("g8", [P, 2, NG, 8])
        gs = sb("gs", [P, 2, 10])
        gr = sb("gr", [P, 2, 10])
        m8 = sb("m8", [P, 2, 8])
        gm = sb("gm", [P, 2, NG])
        t36 = sb("t36", [P, 2, 36])
        r36 = sb("r36", [P, 2, 36])
        n8 = sb("n8", [P, 2, 8])
        chosen = sb("chosen", [P, 2, 2, E], bf16)
        wts = sb("wts", [P, 2, E])
        wsum = sb("wsum", [P, 2])
        before = sb("before", [P, 2, E], bf16)
        kept = sb("kept", [P, 1, E])
        off = sb("off", [P, 1, E])
        need_i = sb("need_i", [P, E], i32)
        need = sb("need", [P, 1, E], i32)
        new = sb("new", [P, 1, E])
        given = sb("given", [P, 2, E])
        off_n = sb("off_n", [P, 1, E])
        delta = sb("delta", [P, 1, E])
        moved = sb("moved", [P, 1, E])
        later = sb("later", [P, 2, E])
        history = sb("history", [P, UNITS, E])
        code = sb("code", [P, 2, E])
        code2 = sb("code2", [P, 2, E])
        c8 = sb("c8", [P, 2, 8])
        w4 = sb("w4", [P, 2, TOPK])
        slot = sb("slot", [P, 2, 2, TOPK], i32)
        place = sb("place", [P, 2, TOPK], i32)
        first = sb("first", [P, NPT])
        page_e = sb("page_e", [P, NPT])
        page_i = sb("page_i", [P, NPT], i32)
        tab_pc = sb("tab_pc", [P, NPT], i32)
        tab = sb("tab", [1, NPT * P], i32)
        hist_j = sb("hist_j", [P, UNITS * E], bf16)
        pad = sb("pad", [P, FILL, ROW])
        ones_e = sb("ones_e", [P, E])
        dest = sb("dest", [P, SLOTS], i32)

        ps = [pb(f"ps{n}", [P, 512]) for n in range(5)]
        psS = pb("psS", [P, 2, 2, 2 * P])
        psO = pb("psO", [P, 512])

        consts = sem("consts")
        made = sem("made")
        gains = sem("gains")
        loaded = [sem("loaded0"), sem("loaded1")]
        mask_ready = sem("mask_ready")
        hats, xhat = sem("hats"), sem("xhat")
        t_x, t_c, t_k, t_q, t_n = sem("t_x"), sem("t_c"), sem("t_k"), sem("t_q"), sem("t_n")
        e_x, e_c, e_k, e_q, e_n = sem("e_x"), sem("e_c"), sem("e_k"), sem("e_q"), sem("e_n")
        pa_full, pb_full, pc_full = sem("pa_full"), sem("pb_full"), sem("pc_full")
        pa_free, pb_free, pc_free = sem("pa_free"), sem("pb_free"), sem("pc_free")
        sq_full, ss_done, scaled = sem("sq_full"), sem("ss_done"), sem("scaled")
        s_full, m_done, exp_done = sem("s_full"), sem("m_done"), sem("exp_done")
        pt_full, pt_ev = sem("pt_full"), sem("pt_ev")
        pv_full, on_done, ot_full, ot_ev = sem("pv_full"), sem("on_done"), sem("ot_full"), sem("ot_ev")
        y_full, y_done = sem("y_full"), sem("y_done")
        pay_x, lg_full, lg_exp = sem("pay_x"), sem("lg_full"), sem("lg_exp")
        ch_done, pos_full = sem("ch_done"), sem("pos_full")
        before_done = sem("before_done")
        rows_ready = sem("rows_ready")
        scat = [sem("scat0"), sem("scat1")]
        dN, dH, dR, dS = sem("dN"), sem("dH"), sem("dR"), sem("dS")
        q3 = sem("q3")
        placed = sem("placed")
        biased = sem("biased")
        ranks_read = sem("ranks_read")
        table_made = sem("table_made")
        table_out, table_in = sem("table_out"), sem("table_in")
        dB = sem("dB")
        blank = [sem("blank0"), sem("blank1")]
        blank_start = sem("blank_start")
        weights_e = sem("weights_e")

        rows = pay.rearrange("p a k n -> p (a k) n")
        xs = [rows[:, n, :] for n in range(SLOTS)]
        yy = [rows[:, SLOTS + n, 0:D] for n in range(SLOTS)]
        xsT = pad.rearrange("p k n -> p (k n)")[:, 0:4 * D].rearrange("p (b n) -> p b n", b=4)
        flat_h = history.rearrange("p u e -> p (u e)")
        sg = flat_h[:, 0:4 * I].rearrange("p (b n) -> p b n", b=4)
        hh = flat_h[:, 4 * I:8 * I].rearrange("p (b n) -> p b n", b=4)
        hT = hist_j[:, :].bitcast(fp32).rearrange("p (b n) -> p b n", b=4)
        xs_in = [sem(f"xs_in{n}") for n in range(SLOTS)]
        dest_kept = sem("dest_kept")
        xst_full, xst_ev, gu_full = sem("xst_full"), sem("xst_ev"), sem("gu_full")
        sg_done, hh_done, ht_full, ht_ev = sem("sg_done"), sem("hh_done"), sem("ht_full"), sem("ht_ev")
        dn_full, yy_done = sem("dn_full"), sem("yy_done")
        y_out = [sem(f"y_out{n}") for n in range(SLOTS)]
        er_in = [sem("er_in0"), sem("er_in1")]
        nh, nt_full, nt_ev = sem("nh"), sem("nt_full"), sem("nt_ev")
        sgu_full, ssg_done, sh_done = sem("sgu_full"), sem("ssg_done"), sem("sh_done")
        sd_full, dC, dD, res_done = sem("sd_full"), sem("dC"), sem("dD"), sem("res_done")
        stored = [sem("stored0"), sem("stored1")]

        block = c.enter_context(nc.Block())

        def apart(eng, sem, value):
            if isinstance(value, int):
                return ge(eng, sem, value)
            value = eng.to_reg(value)
            eng.wait_ge(made, MADE)
            eng.wait_ge(sem, value)

        def arrived(t, n):
            return 16 * (t // SLOTS + 1) if isinstance(t, int) else 16 // SLOTS * (t - n) + 16

        def left(t, n):
            return 16 * (t // SLOTS) if isinstance(t, int) else 16 // SLOTS * (t - n)

        def rsqrt(eng, link, y, v, g, t):
            link(eng.tensor_scalar(g.bitcast(i32), v.bitcast(i32), -0.5, float(0x5f3759df), ALU.mult, ALU.add))
            link(eng.tensor_tensor(t, g, g, ALU.mult))
            link(eng.tensor_tensor(t, t, v, ALU.mult))
            link(eng.scalar_tensor_tensor(t, t, -10.0 / 3.0, t, ALU.add, ALU.mult))
            link(eng.scalar_tensor_tensor(g, t, 5.0, g, ALU.add, ALU.mult))
            link(eng.scalar_tensor_tensor(t, g, -27.0 / 1024.0, g, ALU.mult, ALU.mult))
            link(eng.tensor_tensor(t, t, v, ALU.mult))
            link(eng.scalar_tensor_tensor(y, t, 9.0 / 16.0, g, ALU.add, ALU.mult))

        def col(v, a, b):
            return v[a:b].rearrange("(p o) -> p o", o=1)

        def wide(v):
            return v.rearrange("(a n) -> a n", a=1).to_broadcast([P, v.shape[0]])

        er = arena[:, 0:2 * 2 * TOPK * D].rearrange("p (a j k n) -> p a j k n", a=2, j=2, k=TOPK)
        n1h = arena[:, 8192:8192 + 512].rearrange("p (j n) -> p j n", j=2)
        ncT = arena[:, 8704:8704 + 512].rearrange("p (k n) -> p k n", k=2)
        shs = arena[:, 9216:9216 + 512].rearrange("p (m n) -> p m n", m=2)
        shh = arena[:, 9728:9728 + 512].rearrange("p (m n) -> p m n", m=2)
        esum = arena[:, 10240:10240 + 512].rearrange("p (j n) -> p j n", j=2)
        e2 = arena[:, 10752:10752 + 1024].rearrange("p (j k n) -> p j k n", j=2, k=2)
        res = arena[:, 12288:12288 + 1024].rearrange("p (a j n) -> p a j n", a=2, j=2)

        @block.sync
        def _(sp):
            for dst, src in (
                (w_lat[:, :, 0:D], wq.rearrange("(k p) n -> p k n", p=P)),
                (w_lat[:, :, D:3 * D], wlkv.rearrange("(k p) n -> p k n", p=P)),
                (w_ctx[:, 0, :], wkv[0:P, :]), (w_ctx[0:KC, 1, :], wkv[P:DC, :]),
                (w_o, wo.rearrange("(k p) n -> p k n", p=P)),
                (w_r, rw.rearrange("(k p) n -> p k n", p=P)),
                (gl[:, 0:1], col(ln_l_g, 0, P)), (gl[:, 1:2], col(ln_l_g, P, D)),
                (bl[:, 0:1], col(ln_l_b, 0, P)), (bl[:, 1:2], col(ln_l_b, P, D)),
                (gx[:, 0:1], col(ln_x_g, 0, P)), (gx[0:KC, 1:2], col(ln_x_g, P, DC)),
                (bx[:, 0:1], col(ln_x_b, 0, P)), (bx[0:KC, 1:2], col(ln_x_b, P, DC)),
                (gqk[0:DH, 1:2], col(qn_g, 0, DH)), (gqk[DH:P, 1:2], col(qn_g, 0, DH)),
                (gqk[0:DH, 2:3], col(kn_g, 0, DH)), (gqk[DH:P, 2:3], col(kn_g, 0, DH)),
                (bo_b[:, :], wide(bo)), (rb_b[:, 0, :], wide(rb)),
                (w_sg[:, :, :], sgate.rearrange("(k p) n -> p k n", p=P)),
                (w_su[:, :, :], sup.rearrange("(k p) n -> p k n", p=P)),
                (w_sd[:, :, :], sdown.rearrange("(k p) n -> p k n", p=P)),
            ):
                sp.dma_start(dst, src).then_inc(consts, 16)

            def load(u):
                apart(sp, hats, u.n - 1)
                apart(sp, mask_ready, u.n - 1)
                sp.dma_start(x1[:, at(2 * u.n, 2), :],
                             x[at(2 * u.n, 2)].rearrange("j p n -> p j n")).then_inc(loaded[u.par], 16)
                sp.dma_start(c_in[:, u.par], ctx[at(2 * u.n, 2)].rearrange("j p n -> p j n"))\
                  .then_inc(loaded[u.par], 16)
                sp.dma_start(mask_u8[0:1, u.par], mask[0:1, at(2 * u.n, 2), :])\
                  .then_inc(loaded[u.par], 16)

            def blank_pages(at_page, n, signal):
                for m in range(0, n, FILL):
                    sp.dma_start(lists[at((at_page + m) * P, FILL * P), :].rearrange("(k p) n -> p k n", p=P),
                                 pad[:, :, :]).then_inc(signal, 16)

            def blank_unit(u):
                apart(sp, blank[u.par], BLANK_UNIT * u.i)
                blank_pages(2 * TOPK * u.n + E, 2 * TOPK, blank[u.par])

            def step(s):
                if (s + 3).exists():
                    load(s + 3)
                if s.exists():
                    blank_unit(s)

            load(Unit(0, 0))
            load(Unit(0, 1))
            sp.wait_ge(made, MADE)
            blank_pages(0, E, blank_start)
            load(Unit(1, 0))
            steps_of_phase_a(sp, step, peeled=6)

            sp.wait_ge(y_done, NB)
            sp.wait_ge(rows_ready, UNITS)
            for k in range(2):
                for which, w in ((0, gate), (1, up)):
                    sp.dma_start(w_gu[:, :, k, which * I:(which + 1) * I], w[:, k]).then_inc(weights_e, 16)
            sp.dma_start(w_dn, down).then_inc(weights_e, 16)
            sp.wait_ge(table_made, 1)
            sp.dma_start(tile_table.rearrange("(c p) -> p c", p=P), tab_pc[:, :]).then_inc(table_out, 16)
            sp.wait_ge(table_out, 16)
            sp.dma_start(tab[0:1, :], tile_table.rearrange("(a n) -> a n", a=1)).then_inc(table_in, 16)
            sp.wait_ge(table_in, 16)
            sp.wait_ge(scat[0], 16 * 8 * UNITS // 2)
            sp.wait_ge(scat[1], 16 * 8 * UNITS // 2)
            for par in range(2):
                sp.wait_ge(blank[par], BLANK_UNIT * UNITS // 2)

            def load_tile(t, n):
                if not (isinstance(t, int) and t < SLOTS):
                    apart(sp, hh_done, t - SLOTS + 1)
                    apart(sp, dest_kept, t - SLOTS + 1)
                sp.dma_start(xs[n], lists[at(t * P, P), :]).then_inc(xs_in[n], 16)

            for n in range(SLOTS):
                load_tile(n, n)
            with sp.Fori(SLOTS, TILES - SLOTS + 1, SLOTS) as t:
                for n in range(SLOTS):
                    load_tile(t + n, n)

            for n in range(SLOTS):
                sp.wait_ge(y_out[n], 16 * (TILES // SLOTS))
            sp.wait_ge(dn_full, TILES)
            er_d = expert_out.rearrange("(b p k) n -> p b k n", p=P, k=TOPK)
            out_d = out.rearrange("b p n -> p b n")

            def load_er(u):
                apart(sp, dC, u.n - 1)
                sp.dma_start(er[:, u.par], er_d[:, at(2 * u.n, 2)]).then_inc(er_in[u.par], 16)

            load_er(Unit(0, 0))
            load_er(Unit(0, 1))
            load_er(Unit(1, 0))
            load_er(Unit(1, 1))
            with sp.Fori(2, UNITS // 2) as i:
                load_er(Unit(i, 0))
                load_er(Unit(i, 1))

        @block.gpsimd
        def _(pool):
            pool.memset(ident[:, :], 0.0).then_inc(q3, 1)
            pool.memset(tri[:, :], 0.0).then_inc(q3, 1)
            pool.memset(ones_sq[:, :], 1.0).then_inc(made, 1)
            pool.memset(ones_row[:, :], 1.0).then_inc(made, 1)
            pool.memset(ones_e[:, :], 1.0).then_inc(made, 1)
            pool.memset(mask_row[:, :, :, :, :], 0.0).then_inc(q3, 1)
            pool.memset(vv[:, :, :, :], 1.0).then_inc(made, 1)
            pool.memset(before[:, :, :], 0.0).then_inc(made, 1)
            pool.memset(gs[:, :, :], BIG).then_inc(made, 1)
            pool.memset(t36[:, :, :], BIG).then_inc(made, 1)
            pool.memset(pad[:, :, 0:D + 1], 0.0).then_inc(made, 1)
            pool.memset(pad[:, :, D + 1:ROW].bitcast(i32), NOWHERE).then_inc(made, 1)
            pool.memset(kept[:, :, :], 0.0).then_inc(made, 1)
            pool.memset(off[:, :, :], 0.0).then_inc(made, 1)
            pool.memset(given[:, :, :], 0.0).then_inc(made, 1)
            pool.iota(first[:, :], pattern=[[P * P, NPT]], base=0, channel_multiplier=P,
                      allow_small_or_imprecise_dtypes=True).then_inc(made, 1)
            pool.iota(place[:, :, :], pattern=[[P * TOPK, 2], [1, TOPK]], base=0,
                      channel_multiplier=TOPK).then_inc(made, 1)
            pool.wait_ge(q3, 3)
            pool.affine_select(out=ident[:, :], in_=ident[:, :], compare_op=ALU.not_equal, fill=1.0,
                               base=0, pattern=[[-1, P]], channel_multiplier=1).then_inc(made, 1)
            pool.affine_select(out=tri[:, :], in_=tri[:, :], compare_op=ALU.is_ge, fill=1.0,
                               base=0, pattern=[[-1, P]], channel_multiplier=1).then_inc(made, 1)
            pool.wait_ge(made, MADE)
            def mask_bias(u):
                apart(pool, loaded[u.par], 48 * (u.i + 1))
                apart(pool, s_full, 2 * (u.n - 1))
                pool.tensor_scalar(mask_row[0:1, u.par, :, 0, 0:P], mask_u8[0:1, u.par], NEG, -NEG,
                                   ALU.mult, ALU.add)
                pool.tensor_scalar(mask_row[0:1, u.par, :, 1, 0:P], mask_u8[0:1, u.par], NEG, -NEG,
                                   ALU.mult, ALU.add).then_inc(mask_ready, 1)

            def scale_qk(u):
                apart(pool, dH, H_LINKS * (u.n + 1))
                apart(pool, pb_free, 2 * u.n + 2)
                apart(pool, t_q, u.n)
                for j in range(2):
                    pool.tensor_tensor(nqk[:, j, :].rearrange("p (g d) -> p g d", d=DH),
                                       raw[:, j, :].rearrange("p (g d) -> p g d", d=DH),
                                       rq[:, 12 * j:12 * j + 12].rearrange("p (g o) -> p g o", o=1)
                                       .to_broadcast([P, 12, DH]), ALU.mult).then_inc(scaled, 1)

            def add_bias(u):
                apart(pool, hats, u.n + 1)
                xu = x1[:, at(2 * u.n, 2), :]
                pool.tensor_tensor(xu, xu, bo_b[:, :].rearrange("p (o n) -> p o n", o=1).to_broadcast([P, 2, D]),
                                   ALU.add).then_inc(biased, 1)

            def places(u):
                apart(pool, pay_x, 2 * u.n + 2)
                apart(pool, placed, 2 * u.n)
                pool.tensor_copy(pay[:, 2 * u.par:2 * u.par + 2, :, D + 1:ROW].bitcast(i32),
                                 place[:, :, :].rearrange("p j (k o) -> p j k o", o=1)).then_inc(placed, 1)
                apart(pool, placed, 2 * u.n + 1)
                pool.tensor_scalar(place[:, :, :], place[:, :, :], float(2 * P * TOPK), None, ALU.add)\
                    .then_inc(placed, 1)

            def scatter(u):
                apart(pool, rows_ready, u.n + 1)
                if isinstance(u.n, int) and u.n == 0:
                    pool.wait_ge(blank_start, 16 * E // FILL)
                apart(pool, blank[u.par], BLANK_UNIT * (u.i + 1))
                for j in range(2):
                    for k in range(TOPK):
                        pool.indirect_dma_start(
                            lists, bass.IndirectOffsetOnAxis(ap=slot[:, u.par, j, k:k + 1], axis=0),
                            pay[:, 2 * u.par + j, k, :], None).then_inc(scat[u.par], 16)

            def step(s):
                if (s + 1).exists():
                    mask_bias(s + 1)
                if (s + 2).exists():
                    add_bias(s + 2)
                if (s + -2).exists():
                    places(s + -2)
                if (s + 1).exists():
                    scale_qk(s + 1)
                if (s + -2).exists():
                    scatter(s + -2)

            mask_bias(Unit(0, 0))
            scale_qk(Unit(0, 0))
            add_bias(Unit(0, 0))
            add_bias(Unit(0, 1))
            steps_of_phase_a(pool, step)

            def keep_dest(t, n):
                apart(pool, xs_in[n], arrived(t, n))
                apart(pool, y_out[n], left(t, n))
                pool.tensor_copy(dest[:, n:n + 1], xs[n][:, D + 1:ROW].bitcast(i32)).then_inc(dest_kept, 1)

            def scatter_tile(t, n):
                apart(pool, dest_kept, t + 1)
                apart(pool, yy_done, t + 1)
                pool.indirect_dma_start(
                    expert_out, bass.IndirectOffsetOnAxis(ap=dest[:, n:n + 1], axis=0),
                    yy[n], None, bounds_check=T * TOPK - 1, oob_is_err=False).then_inc(y_out[n], 16)

            for t in range(SLOTS):
                keep_dest(t, t)
                if t >= 4:
                    scatter_tile(t - 4, t - 4)
            with pool.Fori(SLOTS, TILES - SLOTS + 1, SLOTS) as t:
                for n in range(SLOTS):
                    keep_dest(t + n, n)
                    scatter_tile(t + (n - 4), (n - 4) % SLOTS)
            for t in range(TILES - 4, TILES):
                scatter_tile(t, t % SLOTS)

        @block.tensor
        def _(pe):
            pe.wait_ge(consts, 16 * CONSTS)
            pe.wait_ge(made, MADE)

            def turn_inputs(u):
                pe.wait_ge(xhat, u.n + 1)
                ge(pe, e_k, 2 * u.n)
                for j in range(2):
                    for k in range(2):
                        m = pe.transpose(ps[0][:, k * D + j * P:k * D + (j + 1) * P],
                                         x_hat[:, j, k * P:(k + 1) * P], ident[:, :])
                m.then_inc(t_x, 1)
                pe.wait_ge(hats, u.n + 1)
                ge(pe, e_q, u.n)
                for j in range(2):
                    pe.transpose(ps[1][:, j * P:(j + 1) * P], c_hat[:, j, 0:P], ident[:, :])
                    m = pe.transpose(ps[1][0:KC, D + j * P:D + (j + 1) * P], c_hat[:, j, P:DC], ident[:, :])
                m.then_inc(t_c, 1)

            def turn_n1(u):
                pe.wait_ge(pay_x, 2 * u.n + 2)
                pe.wait_ge(e_x, upto(u.n + 3, UNITS))
                pe.wait_ge(e_k, upto(2 * u.n + 4, NB))
                ge(pe, e_n, u.n)
                for j in range(2):
                    for k in range(2):
                        m = pe.transpose(ps[0][:, k * D + j * P:k * D + (j + 1) * P],
                                         pay[:, 2 * u.par + j, 0, k * P:(k + 1) * P], ident[:, :])
                m.then_inc(t_n, 1)

            def project(u, j):
                b = 2 * u.n + j
                pe.wait_ge(e_x, u.n + 1)
                pe.wait_ge(e_c, u.n + 1)
                tok = slice(j * P, (j + 1) * P)
                if j == 0:
                    ge(pe, y_done, 2 * (u.n - 1))
                ge(pe, pa_free, b)
                for k in range(2):
                    m = pe.matmul(ps[2][:, :], lnT[:, k, tok], w_lat[:, k, 0:2 * D], start=k == 0, stop=k == 1)
                m.then_inc(pa_full, 1)
                ge(pe, pb_free, b)
                pe.matmul(ps[3][:, :], cT[:, 0, tok], w_ctx[:, 0, :], start=True, stop=False)
                pe.matmul(ps[3][:, :], cT[0:KC, 1, tok], w_ctx[0:KC, 1, :], start=False, stop=True)\
                  .then_inc(pb_full, 1)
                ge(pe, pc_free, b)
                if j == 0:
                    ge(pe, ranks_read, u.n - 3)
                    ge(pe, lg_exp, u.n - 2)
                for k in range(2):
                    m = pe.matmul(ps[4][:, 0:D], lnT[:, k, tok], w_lat[:, k, 2 * D:3 * D], start=k == 0, stop=k == 1)
                m.then_inc(pc_full, 1)

            def turn_k(u, j):
                bank = ps[1 - j]
                pe.wait_ge(scaled, 2 * u.n + j + 1)
                if j == 0:
                    pe.wait_ge(e_c, u.n + 1)
                else:
                    pe.wait_ge(e_x, u.n + 1)
                    ge(pe, e_n, u.n - 1)
                for k in range(2):
                    pe.transpose(bank[:, k * D:k * D + P], nqk[:, j, 2 * D + k * P:2 * D + (k + 1) * P], ident[:, :])
                    m = pe.transpose(bank[:, k * D + P:(k + 1) * D], nqk[:, j, D + k * P:D + (k + 1) * P], ident[:, :])
                m.then_inc(t_k, 1)

            def turn_q(u):
                pe.wait_ge(e_k, 2 * u.n + 1)
                for k in range(2):
                    for j in range(2):
                        m = pe.transpose(ps[1][:, k * D + j * P:k * D + (j + 1) * P],
                                         nqk[:, j, k * P:(k + 1) * P], ident[:, :])
                m.then_inc(t_q, 1)

            def scores(u, j):
                b = 2 * u.n + j
                pe.wait_ge(mask_ready, u.n + 1)
                pe.wait_ge(e_q, u.n + 1)
                pe.wait_ge(e_k, b + 1)
                ge(pe, pt_ev, b)
                for r in range(2):
                    pe.matmul(psS[:, r], ones_row[:, :], mask_row[0:1, u.par, j], start=True, stop=False)
                for ch in range(2):
                    for r in range(2):
                        rows = slice(r * DH, (r + 1) * DH)
                        m = pe.matmul(psS[:, r, ch], qT[rows, u.par, ch, j, :],
                                      kT[rows, 2 * u.par + j, ch, :], start=False, stop=ch == 1)
                m.then_inc(s_full, 1)

            def turn_probs(u, j):
                b = 2 * u.n + j
                pe.wait_ge(exp_done, b + 1)
                for key in range(2):
                    for g in range(H):
                        m = pe.transpose(psS[:, key].rearrange("p a n -> p (a n)")[:, g * P:(g + 1) * P],
                                         probs[:, j, g, key * P:(key + 1) * P], ident[:, :])
                m.then_inc(pt_full, 1)

            def mix_values(u, j):
                b = 2 * u.n + j
                pe.wait_ge(pt_ev, b + 1)
                pe.wait_ge(pc_free, b + 1)
                ge(pe, ot_ev, b)
                for g in range(H):
                    h = 2 * (g % 2) + g // 2
                    for key in range(2):
                        m = pe.matmul(psO[:, g * (DH + 1):(g + 1) * (DH + 1)],
                                      probsT[:, j, key, g * P:(g + 1) * P], vv[:, 4 * u.par + 2 * j + key, h, :],
                                      start=key == 0, stop=key == 1)
                m.then_inc(pv_full, 1)

            def turn_o(u, j):
                b = 2 * u.n + j
                pe.wait_ge(on_done, b + 1)
                for k in range(2):
                    m = pe.transpose(psO[:, k * P:(k + 1) * P], o_n[:, k * P:(k + 1) * P], ident[:, :])
                m.then_inc(ot_full, 1)

            def out_proj(u, j):
                b = 2 * u.n + j
                pe.wait_ge(ot_ev, b + 1)
                pe.wait_ge(pb_free, upto(2 * u.n + 4, NB))
                for k in range(2):
                    m = pe.matmul(ps[2 + j][:, 0:D], oT[:, k * P:(k + 1) * P], w_o[:, k, :], start=k == 0, stop=k == 1)
                m.then_inc(y_full, 1)

            def logits(u):
                pe.wait_ge(e_n, u.n + 1)
                ge(pe, ranks_read, u.n)
                pe.wait_ge(pc_free, upto(2 * u.n + 6, NB))
                for j in range(2):
                    for k in range(2):
                        m = pe.matmul(ps[4][:, D + j * E:D + (j + 1) * E], n1T[:, k, j * P:(j + 1) * P], w_r[:, k, :],
                                      start=k == 0, stop=k == 1)
                m.then_inc(lg_full, 1)

            def positions(u):
                pe.wait_ge(ch_done, u.n + 1)
                pe.wait_ge(lg_exp, upto(u.n + 1, UNITS))
                pe.wait_ge(pc_free, upto(2 * u.n + 8, NB))
                pe.wait_ge(before_done, u.n + 1)
                for j in range(2):
                    o = ps[4][:, D + (2 + j) * E:D + (3 + j) * E]
                    pe.matmul(o, tri[:, :], chosen[:, u.par, j, :], start=True, stop=False)
                    if j == 1:
                        pe.matmul(o, ones_sq[:, :], chosen[:, u.par, 0, :], start=False, stop=False)
                    pe.matmul(o, ones_sq[:, :], before[:, u.par, :], start=False, stop=True)
                pe.matmul(ps[4][:, D + 4 * E:D + 5 * E], ones_sq[:, :], before[:, 1 - u.par, :],
                          start=True, stop=True).then_inc(pos_full, 1)

            def step(s):
                a, cc, r = s + 1, s + -1, s + -2
                if s.exists():
                    scores(s, 0)
                if a.exists():
                    project(a, 0)
                if s.exists():
                    turn_probs(s, 0)
                if a.exists():
                    project(a, 1)
                if s.exists():
                    scores(s, 1)
                if r.exists():
                    positions(r)
                if s.exists():
                    mix_values(s, 0)
                if cc.exists():
                    turn_n1(cc)
                if s.exists():
                    turn_o(s, 0)
                if cc.exists():
                    logits(cc)
                if s.exists():
                    out_proj(s, 0)
                    turn_probs(s, 1)
                if a.exists():
                    turn_k(a, 0)
                if s.exists():
                    mix_values(s, 1)
                if a.exists():
                    turn_k(a, 1)
                    turn_q(a)
                if s.exists():
                    turn_o(s, 1)
                    out_proj(s, 1)
                if (s + 2).exists():
                    turn_inputs(s + 2)

            turn_inputs(Unit(0, 0))
            project(Unit(0, 0), 0)
            project(Unit(0, 0), 1)
            turn_k(Unit(0, 0), 0)
            turn_k(Unit(0, 0), 1)
            turn_q(Unit(0, 0))
            turn_inputs(Unit(0, 1))
            steps_of_phase_a(pe, step)

            pe.wait_ge(rows_ready, UNITS)

            pe.wait_ge(table_in, 16)
            pe.wait_ge(weights_e, 16 * 5)

            def turn_x(t, n):
                pe.wait_ge(xs_in[n], arrived(t, n))
                ge(pe, xst_ev, t - 1)
                for k in range(2):
                    m = pe.transpose(ps[n % 2][:, k * P:(k + 1) * P], xs[n][:, k * P:(k + 1) * P], ident[:, :])
                m.then_inc(xst_full, 1)

            def gate_up(t, n, e):
                pe.wait_ge(xst_ev, t + 1)
                ge(pe, hh_done, t - 1)
                for k in range(2):
                    m = pe.matmul(ps[2 + n % 2][:, 0:D], xsT[:, n % 4, k * P:(k + 1) * P],
                                  w_gu[:, at(e, 1), k, :].rearrange("p a n -> p (a n)"), start=k == 0, stop=k == 1)
                m.then_inc(gu_full, 1)

            def turn_h(t, n):
                pe.wait_ge(hh_done, t + 1)
                ge(pe, ht_ev, t - 1)
                pe.transpose((ps[4], psO)[n % 2][:, 0:P], hh[:, n % 4, :], ident[:, :]).then_inc(ht_full, 1)

            dbank = [psS[:, 0].rearrange("p a n -> p (a n)"), psS[:, 1].rearrange("p a n -> p (a n)")]

            def down_proj(t, n, e):
                pe.wait_ge(ht_ev, t + 1)
                ge(pe, yy_done, t - 1)
                pe.matmul(dbank[n % 2][:, 0:D], hT[:, n % 4, :],
                          w_dn[:, at(e, 1), :].rearrange("p a n -> p (a n)"), start=True, stop=True)\
                  .then_inc(dn_full, 1)

            def expert(t):
                return pe.value_load(tab[0:1, at(t, 1)], min_val=0, max_val=E - 1)

            turn_x(0, 0)
            turn_x(1, 1)
            for t in range(SLOTS):
                gate_up(t, t, expert(t))
                if t >= 2:
                    turn_h(t - 2, t - 2)
                turn_x(t + 2, (t + 2) % SLOTS)
                if t >= 3:
                    down_proj(t - 3, t - 3, expert(t - 3))
            now_regs = [pe.alloc_register(f"expert{d}") for d in range(SLOTS + 3)]
            with pe.Fori(SLOTS, TILES - 2 * SLOTS + 1, SLOTS) as t:
                pe.load(now_regs, tab[0:1, at(t - 3, SLOTS + 3)])
                now = [pe.snap(r, min_val=0, max_val=E - 1) for r in now_regs]
                for n in range(SLOTS):
                    gate_up(t + n, n, now[n + 3])
                    turn_h(t + (n - 2), (n - 2) % SLOTS)
                    turn_x(t + (n + 2), (n + 2) % SLOTS)
                    down_proj(t + (n - 3), (n - 3) % SLOTS, now[n])
            for t in range(TILES - SLOTS, TILES + 3):
                if t < TILES:
                    gate_up(t, t % SLOTS, expert(t))
                if t - 2 < TILES:
                    turn_h(t - 2, (t - 2) % SLOTS)
                if t + 2 < TILES:
                    turn_x(t + 2, (t + 2) % SLOTS)
                down_proj(t - 3, (t - 3) % SLOTS, expert(t - 3))

            pe.wait_ge(yy_done, TILES)
            pe.wait_ge(ht_ev, TILES)

            def shared_turn(u):
                pe.wait_ge(nh, u.n + 1)
                ge(pe, nt_ev, u.n)
                for j in range(2):
                    for k in range(2):
                        m = pe.transpose(ps[0][:, k * D + j * P:k * D + (j + 1) * P],
                                         n1h[:, j, k * P:(k + 1) * P], ident[:, :])
                m.then_inc(nt_full, 1)

            def shared_up(u):
                pe.wait_ge(nt_ev, u.n + 1)
                for mm in range(2):
                    ge(pe, sh_done, 2 * u.n - 1 + mm)
                    for which, w in ((0, w_sg), (1, w_su)):
                        for k in range(2):
                            m = pe.matmul(ps[1 + 2 * mm + which][:, 0:D], w[:, k, mm * P:(mm + 1) * P], ncT[:, k, :],
                                          start=k == 0, stop=k == 1)
                    m.then_inc(sgu_full, 1)

            def shared_down(u):
                pe.wait_ge(sh_done, 2 * u.n + 2)
                for j in range(2):
                    ge(pe, res_done, 2 * u.n + j - 1)
                    for mm in range(2):
                        m = pe.matmul(dbank[j][:, 0:D], shh[:, mm, j * P:(j + 1) * P], w_sd[:, mm, :],
                                      start=mm == 0, stop=mm == 1)
                    m.then_inc(sd_full, 1)

            def shared(u):
                shared_turn(u)
                shared_up(u)
                shared_down(u)

            shared(Unit(0, 0))
            shared(Unit(0, 1))
            with pe.Fori(1, UNITS // 2) as i:
                shared(Unit(i, 0))
                shared(Unit(i, 1))

        @block.scalar
        def _(act):
            act.wait_ge(consts, 16 * CONSTS)
            act.wait_ge(made, MADE)

            def normalise(u):
                act.wait_ge(dN, N_LINKS * (u.n + 1))
                ge(act, t_x, u.n)
                for j in range(2):
                    a = act.activation(x_hat[:, j, :], x1[:, at(2 * u.n + j, 1), :].rearrange("p a n -> p (a n)"),
                                       ACT.Identity, bias=nb[:, j:j + 1], scale=ra[:, j:j + 1])
                a.then_inc(xhat, 1)
                ge(act, t_c, u.n)
                for j in range(2):
                    a = act.activation(c_hat[:, j, :], c_in[:, u.par, j, :],
                                       ACT.Identity, bias=nb[:, 2 + j:3 + j], scale=ra[:, 2 + j:3 + j])
                a.then_inc(hats, 1)

            def rows_to_scatter(u):
                act.wait_ge(dN, N_LINKS * (u.n + 4))
                ge(act, scat[u.par], 128 * u.i)
                for j in range(2):
                    act.activation(pay[:, 2 * u.par + j, :, 0:D], x1[:, at(2 * u.n + j, 1), :].to_broadcast([P, TOPK, D]),
                                   ACT.Identity, bias=nb[:, 4 + j:5 + j], scale=ra[:, 4 + j:5 + j]).then_inc(pay_x, 1)

            def inputs(u):
                act.wait_ge(t_x, u.n + 1)
                ge(act, pc_full, 2 * u.n)
                for k in range(2):
                    a = act.activation(lnT[:, k, :], ps[0][:, k * D:(k + 1) * D], ACT.Identity,
                                       bias=bl[:, k:k + 1], scale=gl[:, k:k + 1])
                a.then_inc(e_x, 1)
                act.wait_ge(t_c, u.n + 1)
                act.activation(cT[:, 0, :], ps[1][:, 0:D], ACT.Identity, bias=bx[:, 0:1], scale=gx[:, 0:1])
                act.activation(cT[0:KC, 1, :], ps[1][0:KC, D:2 * D], ACT.Identity,
                               bias=bx[0:KC, 1:2], scale=gx[0:KC, 1:2]).then_inc(e_c, 1)

            def projected(u, j):
                b = 2 * u.n + j
                act.wait_ge(pa_full, b + 1)
                ge(act, ss_done, b - 1)
                act.activation(sq[:, j, 0:2 * D], ps[2][:, :], ACT.Square)
                ge(act, scaled, 2 * u.n - 1 + j)
                act.activation(raw[:, j, 0:2 * D], ps[2][:, :], ACT.Copy).then_inc(pa_free, 1)
                act.wait_ge(pb_full, b + 1)
                act.activation(sq[:, j, 2 * D:3 * D], ps[3][:, 0:D], ACT.Square).then_inc(sq_full, 1)
                act.activation(raw[:, j, 2 * D:3 * D], ps[3][:, 0:D], ACT.Copy)
                ge(act, pv_full, 2 * u.n - 3 + j)
                act.activation(vv[:, 4 * u.par + 2 * j, :, 0:DH],
                               ps[3][:, D:2 * D].rearrange("p (h d) -> p h d", d=DH), ACT.Copy).then_inc(pb_free, 1)
                act.wait_ge(pc_full, b + 1)
                act.activation(vv[:, 4 * u.par + 2 * j + 1, :, 0:DH],
                               ps[4][:, 0:D].rearrange("p (h d) -> p h d", d=DH), ACT.Copy).then_inc(pc_free, 1)

            def exps(u, j):
                b = 2 * u.n + j
                act.wait_ge(m_done, b + 1)
                ge(act, pt_full, b - 1)
                for g in range(H):
                    a = act.activation(probs[:, j, g, :], psS[:, g // 2, g % 2], ACT.Exp,
                                       bias=nmax[:, j, g:g + 1])
                a.then_inc(exp_done, 1)

            def probs_copy(u, j):
                b = 2 * u.n + j
                act.wait_ge(pt_full, b + 1)
                ge(act, pv_full, b - 1)
                for key in range(2):
                    a = act.activation(probsT[:, j, key, :], psS[:, key].rearrange("p a n -> p (a n)"), ACT.Copy)
                a.then_inc(pt_ev, 1)

            def o_copy(u, j):
                b = 2 * u.n + j
                act.wait_ge(ot_full, b + 1)
                ge(act, y_full, b)
                act.activation(oT, psO[:, 0:D], ACT.Copy).then_inc(ot_ev, 1)

            def n1_copy(u):
                act.wait_ge(t_n, u.n + 1)
                ge(act, lg_full, u.n)
                act.activation(n1T.rearrange("p k n -> p (k n)"), ps[0][:, :], ACT.Copy).then_inc(e_n, 1)

            def logit_exp(u):
                act.wait_ge(lg_full, u.n + 1)
                ge(act, ch_done, u.n)
                act.activation(esc[:, :, :].rearrange("p j e -> p (j e)"), ps[4][:, D:D + 2 * E], ACT.Exp,
                               scale=-1.0).then_inc(lg_exp, 1)

            def k_copy(u, j):
                act.wait_ge(t_k, 2 * u.n + j + 1)
                ge(act, s_full, 2 * (u.n - 2) + j + 1)
                act.activation(kT[:, 2 * u.par + j].rearrange("p k n -> p (k n)"), ps[1 - j][:, :], ACT.Copy)\
                   .then_inc(e_k, 1)

            def q_copy(u):
                act.wait_ge(t_q, u.n + 1)
                act.activation(qT[:, u.par].rearrange("p k j n -> p (k j n)"), ps[1][:, :], ACT.Copy,
                               scale=gqk[:, 0:1]).then_inc(e_q, 1)

            def step(s):
                a, cc = s + 1, s + -1
                if s.exists():
                    exps(s, 0)
                if a.exists():
                    projected(a, 0)
                if s.exists():
                    probs_copy(s, 0)
                if (s + 2).exists():
                    normalise(s + 2)
                if a.exists():
                    projected(a, 1)
                if cc.exists():
                    rows_to_scatter(cc)
                if s.exists():
                    exps(s, 1)
                if cc.exists():
                    n1_copy(cc)
                if s.exists():
                    o_copy(s, 0)
                if cc.exists():
                    logit_exp(cc)
                if s.exists():
                    probs_copy(s, 1)
                if a.exists():
                    k_copy(a, 0)
                    k_copy(a, 1)
                    q_copy(a)
                if s.exists():
                    o_copy(s, 1)
                if (s + 2).exists():
                    inputs(s + 2)

            act.wait_ge(gains, 2)
            normalise(Unit(0, 0))
            inputs(Unit(0, 0))
            normalise(Unit(0, 1))
            projected(Unit(0, 0), 0)
            projected(Unit(0, 0), 1)
            k_copy(Unit(0, 0), 0)
            k_copy(Unit(0, 0), 1)
            q_copy(Unit(0, 0))
            inputs(Unit(0, 1))
            steps_of_phase_a(act, step)

            def rows_copy(t, n):
                act.wait_ge(xst_full, t + 1)
                ge(act, gu_full, t - 3)
                act.activation(xsT[:, n % 4, :], ps[n % 2][:, 0:D], ACT.Copy).then_inc(xst_ev, 1)

            def gate_silu(t, n):
                act.wait_ge(gu_full, t + 1)
                ge(act, hh_done, t - 3)
                act.activation(sg[:, n % 4, :], ps[2 + n % 2][:, 0:I], ACT.Silu).then_inc(sg_done, 1)

            rows_copy(0, 0)
            rows_copy(1, 1)
            for t in range(SLOTS):
                gate_silu(t, t)
                rows_copy(t + 2, (t + 2) % SLOTS)
            with act.Fori(SLOTS, TILES - 2 * SLOTS + 1, SLOTS) as t:
                for n in range(SLOTS):
                    gate_silu(t + n, n)
                    rows_copy(t + (n + 2), (n + 2) % SLOTS)
            for t in range(TILES - SLOTS, TILES):
                gate_silu(t, t % SLOTS)
                if t + 2 < TILES:
                    rows_copy(t + 2, (t + 2) % SLOTS)

            act.wait_ge(dn_full, TILES)
            out_d = out.rearrange("b p n -> p b n")

            def shared(u):
                act.wait_ge(nt_full, u.n + 1)
                ge(act, sgu_full, 2 * u.n)
                act.activation(ncT.rearrange("p k n -> p (k n)"), ps[0][:, :], ACT.Copy).then_inc(nt_ev, 1)
                for mm in range(2):
                    act.wait_ge(sgu_full, 2 * u.n + mm + 1)
                    ge(act, sh_done, 2 * u.n - 1 + mm)
                    act.activation(shs[:, mm, :], ps[1 + 2 * mm][:, 0:D], ACT.Silu).then_inc(ssg_done, 1)

            def store(u):
                act.wait_ge(res_done, 2 * u.n + 2)
                act.dma_start(out_d[:, at(2 * u.n, 2), :], res[:, u.par]).then_inc(stored[u.par], 16)

            shared(Unit(0, 0))
            shared(Unit(0, 1))
            store(Unit(0, 0))
            with act.Fori(1, UNITS // 2) as i:
                shared(Unit(i, 0))
                store(Unit(i - 1, 1))
                shared(Unit(i, 1))
                store(Unit(i, 0))
            store(Unit(UNITS // 2 - 1, 1))
            for s in stored:
                act.wait_ge(s, 16 * UNITS // 2)

        @block.vector
        def _(dve):
            dve.wait_ge(consts, 16 * CONSTS)
            dve.wait_ge(made, MADE)

            def chain(order, per_unit, u):
                n = [0]

                def link(ins, before_plain=False):
                    n[0] += 1
                    ins.then_inc(order, 1)
                    (apart if before_plain else ge)(dve, order, per_unit * u.n + n[0])

                return link, n

            dve.tensor_tensor(gqk[:, 0:1], gqk[:, 1:2], gqk[:, 2:3], ALU.mult).then_inc(gains, 1)
            dve.wait_ge(gains, 1)
            dve.tensor_scalar(gqk[:, 0:1], gqk[:, 0:1], SCALE, None, ALU.mult).then_inc(gains, 1)
            dve.wait_ge(gains, 2)

            def parts_of(run):
                return run.exists(), (run + -3).exists()

            def row_statistics(run):
                link, n = chain(dN, N_LINKS, run)
                new, old = parts_of(run)
                if new:
                    apart(dve, loaded[run.par], 48 * (run.i + 1))
                    for j in range(2):
                        dve.bn_stats(stats[:, j, :], x1[:, at(2 * run.n + j, 1), :].rearrange("p a n -> p (a n)"))
                        m = dve.bn_stats(stats[:, 2 + j, :], c_in[:, run.par, j, :])
                if old:
                    u = run + -3
                    apart(dve, y_done, 2 * u.n + 2)
                    for j in range(2):
                        m = dve.bn_stats(stats[:, 4 + j, :], x1[:, at(2 * u.n + j, 1), :].rearrange("p a n -> p (a n)"))
                link(m, True)
                for j in range(0 if new else 4, 6 if old else 4):
                    m = dve.bn_aggr(mv[:, j, :], stats[:, j, :])
                link(m)

            def deviations(run):
                link, n = chain(dN, N_LINKS, run)
                n[0] = 2
                new, old = parts_of(run)
                if new:
                    dve.tensor_scalar(va[:, 0:2], mv[:, 0:2, 1], 1.0 + LN_EPS, LN_EPS * LN_EPS, ALU.mult, ALU.add)
                lo, hi = 2 if new else 4, 6 if old else 4
                link(dve.tensor_scalar(va[:, lo:hi], mv[:, lo:hi, 1], LN_EPS, None, ALU.add))
                lo = 0 if new else 4
                ge(dve, hats, upto(run.n, UNITS))
                ge(dve, pay_x, 2 * (run.n - 3))
                rsqrt(dve, link, ra[:, lo:hi], va[:, lo:hi], ry[:, lo:hi], rt[:, lo:hi])
                if old:
                    u = run + -3
                    dve.tensor_copy(mr[:, at(2 * u.n, 2), 0:1], mv[:, 4:6, 0:1])
                    dve.tensor_copy(mr[:, at(2 * u.n, 2), 1:2], ra[:, 4:6].rearrange("p (j o) -> p j o", o=1))
                link(dve.scalar_tensor_tensor(nb[:, lo:hi], mv[:, lo:hi, 0], -1.0, ra[:, lo:hi], ALU.mult, ALU.mult))
                assert n[0] == N_LINKS

            def square_sums(u, j):
                b = 2 * u.n + j
                dve.wait_ge(sq_full, b + 1)
                ge(dve, scaled, 2 * u.n)
                dve.tensor_reduce(ss[:, 12 * j:12 * j + 12], sq[:, j, :].rearrange("p (g d) -> p g d", d=DH), AX, ALU.add)\
                   .then_inc(ss_done, 1)

            def maxima(u, j):
                b = 2 * u.n + j
                dve.wait_ge(s_full, b + 1)
                ge(dve, exp_done, b - 1)
                dve.tensor_reduce(nmax[:, j, :], psS[:, :, :, :].rearrange("p r k n -> p (r k) n"), AX, ALU.max,
                                  negate=True).then_inc(m_done, 1)

            def normalise_o(u, j):
                b = 2 * u.n + j
                dve.wait_ge(pv_full, b + 1)
                ge(dve, ot_full, b)
                o = psO[:, 0:H * (DH + 1)].rearrange("p (g d) -> p g d", d=DH + 1)
                dve.reciprocal(rden[:, :], o[:, :, DH]).then_inc(dS, 1)
                dve.wait_ge(dS, b + 1)
                dve.tensor_tensor(o_n.rearrange("p (k r d) -> p r k d", k=2, r=2),
                                  o[:, :, 0:DH].rearrange("p (r k) d -> p r k d", k=2),
                                  rden[:, :].rearrange("p (r k o) -> p r k o", k=2, o=1).to_broadcast([P, 2, 2, DH]),
                                  ALU.mult).then_inc(on_done, 1)

            def residual(u, j):
                b = 2 * u.n + j
                dve.wait_ge(y_full, b + 1)
                dve.wait_ge(biased, u.n + 1)
                xb = x1[:, at(b, 1), :].rearrange("p a n -> p (a n)")
                dve.tensor_tensor(xb, xb, ps[2 + j][:, 0:D], ALU.add).then_inc(y_done, 1)

            def head_norms(u):
                link, n = chain(dH, H_LINKS, u)
                dve.wait_ge(ss_done, 2 * u.n + 2)
                link(dve.tensor_scalar(ss[:, :], ss[:, :], 1.0 / DH, RMS_EPS * RMS_EPS, ALU.mult, ALU.max))
                rsqrt(dve, link, rq[:, :], ss[:, :], hy[:, :], ht[:, :])
                assert n[0] == H_LINKS

            def choose(u):
                link, n = chain(dR, R_LINKS, u)
                dve.wait_ge(lg_exp, u.n + 1)
                link(dve.tensor_scalar(esc[:, :, :], esc[:, :, :], 1.0, None, ALU.add))
                link(dve.reciprocal(sc[:, :, :], esc[:, :, :]))
                link(dve.tensor_tensor(sfc[:, :, :], sc[:, :, :], rb_b[:, :, :].to_broadcast([P, 2, E]), ALU.add), True)
                for j in range(2):
                    for g in range(NG):
                        m = dve.max(g8[:, j, g, :], sfc[:, j, 8 * g:8 * g + 8])
                link(m)
                link(dve.tensor_tensor(gs[:, :, 0:NG], g8[:, :, :, 0], g8[:, :, :, 1], ALU.add), True)
                for j in range(2):
                    m = dve.max(m8[:, j, :], gs[:, j, :])
                link(m, True)
                for j in range(2):
                    m = dve.match_replace(gr[:, j, :], m8[:, j, :], gs[:, j, :], -BIG)
                link(m)
                link(dve.tensor_tensor(gm[:, :, :], gr[:, :, 0:NG], gs[:, :, 0:NG], ALU.not_equal))
                for j in range(2):
                    m = dve.tensor_tensor(t36[:, j, 0:E].rearrange("p (g e) -> p g e", g=NG),
                                          sfc[:, j, :].rearrange("p (g e) -> p g e", g=NG),
                                          gm[:, j, :].rearrange("p (g o) -> p g o", o=1).to_broadcast([P, NG, E // NG]),
                                          ALU.mult)
                link(m, True)
                for j in range(2):
                    m = dve.max(n8[:, j, :], t36[:, j, :])
                link(m, True)
                for j in range(2):
                    m = dve.match_replace(r36[:, j, :], n8[:, j, :], t36[:, j, :], -BIG)
                link(m)
                ge(dve, pos_full, u.n)
                link(dve.tensor_tensor(chosen[:, u.par], r36[:, :, 0:E], t36[:, :, 0:E], ALU.not_equal))
                dve.tensor_tensor(before[:, 1 - u.par, :], before[:, u.par, :], chosen[:, u.par, 0, :], ALU.add)\
                   .then_inc(ch_done, 1)
                link(dve.tensor_tensor(wts[:, :, :], chosen[:, u.par], sc[:, :, :], ALU.mult))
                dve.tensor_tensor(before[:, 1 - u.par, :], before[:, 1 - u.par, :], chosen[:, u.par, 1, :], ALU.add)\
                   .then_inc(before_done, 1)
                link(dve.tensor_reduce(wsum[:, :], wts[:, :, :], AX, ALU.add))
                link(dve.tensor_scalar(wsum[:, :], wsum[:, :], 1e-20, None, ALU.add))
                link(dve.reciprocal(wsum[:, :], wsum[:, :]))
                assert n[0] == C_LINKS, n[0]

            def assign(u):
                link, n = chain(dR, R_LINKS, u)
                n[0] = C_LINKS
                dve.wait_ge(pos_full, u.n + 1)
                rank = ps[4][:, D + 2 * E:D + 4 * E].rearrange("p (j e) -> p j e", j=2)
                both = [P, 2, E]
                dve.tensor_tensor(later[:, :, :], rank, kept[:, :, :].to_broadcast(both), ALU.is_ge)
                dve.scalar_tensor_tensor(code[:, :, :], rank, 1.0, off[:, :, :].to_broadcast(both), ALU.add, ALU.add)
                dve.tensor_scalar(need_i[:, :], ps[4][:, D + 4 * E:D + 5 * E], float(P - 1), None, ALU.add)\
                   .then_inc(ranks_read, 1)
                dve.wait_ge(ranks_read, u.n + 1)
                link(dve.tensor_scalar(need[:, 0, :], need_i[:, :], 7, 7, ALU.logical_shift_right, ALU.logical_shift_left))
                link(dve.tensor_tensor(new[:, :, :], need[:, :, :], kept[:, :, :], ALU.subtract))
                link(dve.tensor_tensor_scan(given[:, u.par, :], ones_e[:, :], new[:, 0, :],
                                            given[:, 1 - u.par, E - 1:E], ALU.mult, ALU.add))
                link(dve.tensor_tensor(off_n[:, :, :], given[:, u.par:u.par + 1, :], need[:, :, :], ALU.subtract))
                link(dve.tensor_tensor(delta[:, :, :], off_n[:, :, :], off[:, :, :], ALU.subtract))
                dve.tensor_tensor(later[:, :, :], later[:, :, :], delta[:, :, :].to_broadcast(both), ALU.mult)
                link(dve.scalar_tensor_tensor(moved[:, :, :], new[:, :, :], 0.0, delta[:, :, :], ALU.is_gt, ALU.mult))
                dve.tensor_tensor(code[:, :, :], code[:, :, :], later[:, :, :], ALU.add)
                dve.tensor_tensor(off[:, :, :], off[:, :, :], moved[:, :, :], ALU.add)
                dve.tensor_copy(kept[:, :, :], need[:, :, :])
                link(dve.tensor_copy(history[:, at(u.n, 1), :], given[:, u.par:u.par + 1, :]))
                link(dve.tensor_tensor(code2[:, :, :], code[:, :, :], chosen[:, u.par], ALU.mult), True)
                for j in range(2):
                    m = dve.max(c8[:, j, :], code2[:, j, :])
                link(m)
                for j in range(2):
                    for k in range(TOPK):
                        m = dve.scalar_tensor_tensor(wj[:, j, k, :], code2[:, j, :], c8[:, j, k:k + 1], wts[:, j, :],
                                                     ALU.is_equal, ALU.mult, accum_out=w4[:, j, k:k + 1])
                link(m)
                dve.tensor_scalar(slot[:, u.par], c8[:, :, 0:TOPK], -1.0, None, ALU.add)
                for j in range(2):
                    m = dve.tensor_scalar(pay[:, 2 * u.par + j, :, D:D + 1],
                                          w4[:, j, :].rearrange("p (k o) -> p k o", o=1), wsum[:, j:j + 1], ROUTE_SCALE,
                                          ALU.mult, ALU.mult)
                m.then_inc(rows_ready, 1)
                assert n[0] == R_LINKS, n[0]

            def step(s):
                a, r = s + 1, s + -2
                run = s + 2
                if any(parts_of(run)):
                    row_statistics(run)
                if s.exists():
                    maxima(s, 0)
                if any(parts_of(run)):
                    deviations(run)
                if r.exists():
                    choose(r)
                if a.exists():
                    square_sums(a, 0)
                    square_sums(a, 1)
                    head_norms(a)
                if s.exists():
                    maxima(s, 1)
                    normalise_o(s, 0)
                if r.exists():
                    assign(r)
                if s.exists():
                    residual(s, 0)
                    normalise_o(s, 1)
                    residual(s, 1)

            for par in range(2):
                row_statistics(Unit(0, par))
                deviations(Unit(0, par))
            square_sums(Unit(0, 0), 0)
            square_sums(Unit(0, 0), 1)
            head_norms(Unit(0, 0))
            steps_of_phase_a(dve, step)

            for q in range(NPT):
                m = dve.tensor_scalar(hist_j[:, :], history[:, :, :].rearrange("p u e -> p (u e)"), first[:, q:q + 1],
                                      0.0, ALU.is_le, ALU.add, accum_out=page_e[:, q:q + 1])
                m.then_inc(dB, 1)
                dve.wait_ge(dB, q + 1)
            dve.tensor_copy(page_i[:, :], page_e[:, :]).then_inc(dB, 1)
            dve.wait_ge(dB, NPT + 1)
            dve.tensor_scalar(tab_pc[:, :], page_i[:, :], E - 1, None, ALU.bitwise_and).then_inc(table_made, 1)

            def hidden(t, n):
                dve.wait_ge(sg_done, t + 1)
                ge(dve, ht_full, t - 3)
                dve.scalar_tensor_tensor(hh[:, n % 4, :], sg[:, n % 4, :], xs[n][:, D:D + 1],
                                         ps[2 + n % 2][:, I:2 * I], ALU.mult, ALU.mult).then_inc(hh_done, 1)

            def hidden_copy(t, n):
                dve.wait_ge(ht_full, t + 1)
                ge(dve, dn_full, t - 3)
                dve.tensor_copy(hT[:, n % 4, :], (ps[4], psO)[n % 2][:, 0:P]).then_inc(ht_ev, 1)

            dbank = [psS[:, 0].rearrange("p a n -> p (a n)"), psS[:, 1].rearrange("p a n -> p (a n)")]

            def result_copy(t, n):
                dve.wait_ge(dn_full, t + 1)
                ge(dve, y_out[n], left(t, n))
                dve.tensor_copy(yy[n], dbank[n % 2][:, 0:D]).then_inc(yy_done, 1)

            def tile_step(t, n):
                if not isinstance(t, int) or t < TILES:
                    hidden(t, n)
                if not isinstance(t, int) or 2 <= t < TILES + 2:
                    hidden_copy(t + -2, (n - 2) % SLOTS)
                if not isinstance(t, int) or t >= 3:
                    result_copy(t + -3, (n - 3) % SLOTS)

            for t in range(2 * SLOTS):
                tile_step(t, t % SLOTS)
            with dve.Fori(2 * SLOTS, TILES - SLOTS + 1, SLOTS) as t:
                for n in range(SLOTS):
                    tile_step(t + n, n)
            for t in range(TILES, TILES + 3):
                tile_step(t, t % SLOTS)

            def norm_again(u):
                ge(dve, nt_full, u.n)
                for j in range(2):
                    b = at(2 * u.n + j, 1)
                    m = dve.tensor_scalar(n1h[:, j, :], x1[:, b, :].rearrange("p a n -> p (a n)"),
                                          mr[:, b, 0:1].rearrange("p a n -> p (a n)"),
                                          mr[:, b, 1:2].rearrange("p a n -> p (a n)"), ALU.subtract, ALU.mult)
                m.then_inc(nh, 1)

            def shared(u):
                for mm in range(2):
                    dve.wait_ge(ssg_done, 2 * u.n + mm + 1)
                    ge(dve, sd_full, 2 * u.n)
                    dve.tensor_tensor(shh[:, mm, :], shs[:, mm, :], ps[2 + 2 * mm][:, 0:D], ALU.mult).then_inc(sh_done, 1)
                dve.wait_ge(er_in[u.par], 16 * (u.i + 1))
                dve.tensor_tensor(e2, er[:, u.par, :, 0:2, :], er[:, u.par, :, 2:4, :], ALU.add).then_inc(dC, 1)
                dve.wait_ge(dC, u.n + 1)
                dve.tensor_tensor(esum, e2[:, :, 0, :], e2[:, :, 1, :], ALU.add).then_inc(dD, 1)
                dve.wait_ge(dD, 2 * u.n + 1)
                ge(dve, stored[u.par], 16 * u.i)
                dve.tensor_tensor(res[:, u.par], esum, x1[:, at(2 * u.n, 2), :], ALU.add).then_inc(dD, 1)
                dve.wait_ge(dD, 2 * u.n + 2)
                for j in range(2):
                    dve.wait_ge(sd_full, 2 * u.n + j + 1)
                    dve.tensor_tensor(res[:, u.par, j, :], res[:, u.par, j, :], dbank[j][:, 0:D], ALU.add)\
                       .then_inc(res_done, 1)

            dve.wait_ge(dn_full, TILES)
            norm_again(Unit(0, 0))
            shared(Unit(0, 0))
            norm_again(Unit(0, 1))
            shared(Unit(0, 1))
            with dve.Fori(1, UNITS // 2) as i:
                for par in range(2):
                    norm_again(Unit(i, par))
                    shared(Unit(i, par))


def kernel(x, ctx_768, mask_BxS2_bk0, L0_xattn_ln_x_g, L0_xattn_ln_x_b, L0_xattn_ln_l_g, L0_xattn_ln_l_b,
           L0_xattn_qn_g, L0_xattn_kn_g, L0_xattn_Wq, L0_xattn_Wkv, L0_xattn_Wlkv, L0_xattn_Wo, L0_xattn_bo,
           L0_ffn_router_weight, L0_ffn_router_bias, L0_ffn_gate_w, L0_ffn_up_w, L0_ffn_down_w,
           L0_ffn_shared_gate_w, L0_ffn_shared_up_w, L0_ffn_shared_down_w):
    import numpy as np
    import concourse.bacc as bacc
    from concourse.bass_utils import run_bass_kernel_spmd

    def by_chunk(w):
        return np.asarray(w).transpose(2, 0, 1).reshape(2, P, E, I).transpose(1, 0, 2, 3)

    arrays = dict(
        x=x, ctx=ctx_768, mask=np.asarray(mask_BxS2_bk0).reshape(1, NB, P),
        ln_x_g=L0_xattn_ln_x_g, ln_x_b=L0_xattn_ln_x_b, ln_l_g=L0_xattn_ln_l_g, ln_l_b=L0_xattn_ln_l_b,
        qn_g=L0_xattn_qn_g, kn_g=L0_xattn_kn_g,
        wq=np.asarray(L0_xattn_Wq).T, wkv=np.asarray(L0_xattn_Wkv).T, wlkv=np.asarray(L0_xattn_Wlkv).T,
        wo=np.asarray(L0_xattn_Wo).T, bo=L0_xattn_bo,
        rw=np.asarray(L0_ffn_router_weight).T, rb=L0_ffn_router_bias,
        gate=by_chunk(L0_ffn_gate_w), up=by_chunk(L0_ffn_up_w),
        down=np.asarray(L0_ffn_down_w).transpose(2, 0, 1),
        sgate=np.asarray(L0_ffn_shared_gate_w).T, sup=np.asarray(L0_ffn_shared_up_w).T,
        sdown=np.asarray(L0_ffn_shared_down_w).T)
    arrays = {k: np.ascontiguousarray(v) for k, v in arrays.items()}
    nc = bacc.Bacc("TRN2", target_bir_lowering=False, num_devices=1)
    args = [nc.dram_tensor(f"in_{k}", v.shape, mybir.dt.from_np(v.dtype), kind="ExternalInput").ap()
            for k, v in arrays.items()]
    out = nc.dram_tensor("out_0", (NB, P, D), mybir.dt.float32, kind="ExternalOutput").ap()
    with nc.allow_non_contiguous_dma(reason="gains by partition and the tile table: a few small loads"):
        build(nc, *args, out)
    r = run_bass_kernel_spmd(nc, [{f"in_{k}": v for k, v in arrays.items()}], core_ids=[0])
    return r.results[0]["out_0"]
```

```python
import concourse.bass as bass
from concourse import mybir
from contextlib import ExitStack

P = 128
NB, D, DC = 64, 256, 192
H, DH = 4, 64
E, I, TOPK, NG = 32, 128, 4, 4
UNITS = NB // 2
T = NB * P
ROW = D + 2
TILES = (T * TOPK + E * (P - 1)) // P
SLOTS = 8
TILES = -(-TILES // SLOTS) * SLOTS
FILL = 4
NPT = -(-TILES // P)
KC = DC - P
LN_EPS, RMS_EPS = 1e-5, 1e-8
SCALE, ROUTE_SCALE = DH ** -0.5, 2.5
NEG = 1e30
BIG = 3e38
NOWHERE = T * TOPK + 7


class Unit:

    def __init__(self, i, par):
        self.i, self.par = i, par
        self.n = 2 * i + par

    def __add__(self, d):
        q, r = divmod(self.par + d, 2)
        return Unit(self.i + q, r)

    def exists(self):
        return not isinstance(self.n, int) or 0 <= self.n < UNITS


def ge(eng, sem, value):
    if isinstance(value, int) and value <= 0:
        return
    eng.wait_ge(sem, value)


def upto(value, cap):
    return min(value, cap) if isinstance(value, int) else value


def at(start, n):
    return slice(start, start + n) if isinstance(start, int) else bass.ds(start, n)


def steps_of_phase_a(eng, step, peeled=4):
    for s in range(4):
        step(Unit(s // 2, s % 2))
    with eng.Fori(2, (UNITS + 2 - peeled) // 2) as i:
        step(Unit(i, 0))
        step(Unit(i, 1))
    for s in range(UNITS + 2 - peeled, UNITS + 2):
        step(Unit(s // 2, s % 2))


def steps_of_phase_c(eng, step):
    for s in range(2):
        step(Unit(0, s))
    with eng.Fori(1, UNITS // 2 - 1) as i:
        step(Unit(i, 0))
        step(Unit(i, 1))
    for s in range(UNITS - 2, UNITS + 1):
        step(Unit(s // 2, s % 2))


RSQRT_STEPS = 8
N_LINKS = 4 + RSQRT_STEPS
G_LINKS, C_LINKS, R_LINKS = 8, 13, 23
H_LINKS = 12
K_LINKS = 1 + RSQRT_STEPS
BLANK_UNIT = 16 * 2 * TOPK // FILL
CONSTS = 20
MADE = 16


def build(nc, x, ctx, mask, ln_x_g, ln_x_b, ln_l_g, ln_l_b, qn_g, kn_g, wq, wkv, wlkv, wo, bo,
          rw, rb, gate, up, down, sgate, sup, sdown, out):
    fp32, bf16, i32, u8 = mybir.dt.float32, mybir.dt.bfloat16, mybir.dt.int32, mybir.dt.uint8
    ALU, ACT, AX = mybir.AluOpType, mybir.ActivationFunctionType, mybir.AxisListType.X

    lists = nc.dram_tensor("lists", [TILES * P, ROW], fp32).ap()
    expert_out = nc.dram_tensor("expert_out", [T * TOPK, D], fp32).ap()
    tile_table = nc.dram_tensor("tile_table", [NPT * P], i32).ap()

    with ExitStack() as c:
        def sb(name, shape, dt=fp32):
            return c.enter_context(nc.sbuf_tensor(name, shape, dt))

        def pb(name, shape):
            return c.enter_context(nc.psum_tensor(name, shape, fp32))

        def sem(name):
            return c.enter_context(nc.semaphore(name))

        x1 = sb("x1", [P, NB, D])
        mr = sb("mr", [P, NB, 2])
        ident = sb("ident", [P, P])
        w_sg = sb("w_sg", [P, 2, 2 * P])
        w_su = sb("w_su", [P, 2, 2 * P])
        w_sd = sb("w_sd", [P, 2, D])
        arena = sb("arena", [P, E * 3 * D])
        used = [0]

        def part(*shape):
            n = 1
            for s in shape:
                n *= s
            v = arena[:, used[0]:used[0] + n]
            used[0] += n
            if len(shape) == 1:
                return v
            names = "abcd"[:len(shape)]
            return v.rearrange(f"p ({' '.join(names)}) -> p {' '.join(names)}",
                               **dict(zip(names, shape)))

        w_lat = part(2, 3 * D)
        w_ctx = part(2, 2 * D)
        w_o = part(2, D)
        c_in = part(2, 2, DC)
        x_hat = part(2, D)
        c_hat = part(2, DC)
        lnT = part(2, 2 * P)
        cT = part(2, 2 * P)
        sq = part(2, 3 * D)
        raw = part(2, 3 * D)
        nqk = part(2, 3 * D)
        qT = part(2, 2, 2, P)
        kT = part(4, 2, 2 * P)
        probs = part(2, H, 2 * P)
        probsT = part(2, 2, H * P)
        o_n = part(D)
        oT = part(D)
        vv = part(4 * 2, H, DH + 1)
        late = 2 * E + 2 * 2 * P + 2 * TOPK * E + 2 * TOPK * ROW
        assert used[0] <= E * 3 * D - late
        used[0] = E * 3 * D - late
        w_r = part(2, E)
        n1T = part(2, 2 * P)
        wj = part(2, TOPK, E)
        pay_last = part(2, TOPK, ROW)
        early = E - -(-late // D)
        w_gu = arena[:, 0:E * 2 * D].rearrange("p (e k n) -> p e k n", e=E, k=2)
        w_dn = arena[:, E * 2 * D:E * 3 * D].rearrange("p (e n) -> p e n", e=E)

        pay = sb("pay", [P, 4, TOPK, ROW])
        mask_u8 = sb("mask_u8", [1, 2, 2, P], u8)
        mask_row = sb("mask_row", [1, 2, 2, 2, 2 * P], bf16)
        ones_row = sb("ones_row", [1, P], bf16)
        ones_sq = sb("ones_sq", [P, P], bf16)
        tri = sb("tri", [P, P], bf16)
        gl, bl = sb("gl", [P, 2]), sb("bl", [P, 2])
        gx, bx = sb("gx", [P, 2]), sb("bx", [P, 2])
        gqk = sb("gqk", [P, 3])
        bo_b = sb("bo_b", [P, D])
        rb_b = sb("rb_b", [P, 1, E])
        stats = sb("stats", [P, 6, 6])
        mv = sb("mv", [P, 6, 2])
        va, ra, nb = sb("va", [P, 6]), sb("ra", [P, 6]), sb("nb", [P, 6])
        ss, rq = sb("ss", [P, 24]), sb("rq", [P, 24])
        ry, rt = sb("ry", [P, 6]), sb("rt", [P, 6])
        hy, ky = sb("hy", [P, 3, 12]), sb("ky", [P, 2, 12])
        nmax = sb("nmax", [P, 2, H])
        rden = sb("rden", [P, H])
        esc = sb("esc", [P, 2, E])
        sc = sb("sc", [P, 2, E])
        sfc = sb("sfc", [P, 2, E])
        g8 = sb("g8", [P, 2, NG, 8])
        gs = sb("gs", [P, 2, 10])
        gr = sb("gr", [P, 2, 10])
        m8 = sb("m8", [P, 2, 8])
        gm = sb("gm", [P, 2, NG])
        t36 = sb("t36", [P, 2, 36])
        r36 = sb("r36", [P, 2, 36])
        n8 = sb("n8", [P, 2, 8])
        chosen = sb("chosen", [P, 2, 2, E], bf16)
        wts = sb("wts", [P, 2, E])
        wsum = sb("wsum", [P, 2])
        before = sb("before", [P, 2, E], bf16)
        kept = sb("kept", [P, 1, E])
        off = sb("off", [P, 1, E])
        need_i = sb("need_i", [P, E], i32)
        need = sb("need", [P, 1, E], i32)
        new = sb("new", [P, 1, E])
        given = sb("given", [P, 2, E])
        off_n = sb("off_n", [P, 1, E])
        delta = sb("delta", [P, 1, E])
        moved = sb("moved", [P, 1, E])
        later = sb("later", [P, 2, E])
        history = sb("history", [P, UNITS, E])
        code = sb("code", [P, 2, E])
        code2 = sb("code2", [P, 2, E])
        c8 = sb("c8", [P, 2, 8])
        w4 = sb("w4", [P, 2, TOPK])
        slot = sb("slot", [P, 3, 2, TOPK], i32)
        place = sb("place", [P, 2, TOPK], i32)
        first = sb("first", [P, NPT])
        page_e = sb("page_e", [P, NPT])
        page_i = sb("page_i", [P, NPT], i32)
        tab_pc = sb("tab_pc", [P, NPT], i32)
        tab = sb("tab", [1, NPT * P], i32)
        hist_j = sb("hist_j", [P, UNITS * E], bf16)
        pad = sb("pad", [P, FILL, ROW])
        ones_e = sb("ones_e", [P, E])
        dest = sb("dest", [P, SLOTS, 2], i32)

        ps = [pb(f"ps{n}", [P, 512]) for n in range(5)]
        psS = pb("psS", [P, 2, 2, 2 * P])
        psO = pb("psO", [P, 512])

        consts = sem("consts")
        made = sem("made")
        shared_in = sem("shared_in")
        gains = sem("gains")
        loaded = [sem("loaded0"), sem("loaded1")]
        mask_ready = sem("mask_ready")
        hats, xhat = sem("hats"), sem("xhat")
        t_x, t_c, t_k, t_q, t_n = sem("t_x"), sem("t_c"), sem("t_k"), sem("t_q"), sem("t_n")
        e_x, e_c, e_k, e_q, e_n = sem("e_x"), sem("e_c"), sem("e_k"), sem("e_q"), sem("e_n")
        pa_full, pb_full, pc_full = sem("pa_full"), sem("pb_full"), sem("pc_full")
        pa_free, pb_free, pc_free = sem("pa_free"), sem("pb_free"), sem("pc_free")
        sq_full, ss_done, scaled = sem("sq_full"), sem("ss_done"), [sem("scaled0"), sem("scaled1")]
        s_full, m_done, exp_done = sem("s_full"), sem("m_done"), sem("exp_done")
        pt_full, pt_ev = sem("pt_full"), sem("pt_ev")
        pv_full, on_done, ot_full, ot_ev = sem("pv_full"), sem("on_done"), sem("ot_full"), sem("ot_ev")
        y_full, y_done = sem("y_full"), sem("y_done")
        pay_x, lg_full, lg_exp = sem("pay_x"), sem("lg_full"), sem("lg_exp")
        ch_done, pos_full = sem("ch_done"), sem("pos_full")
        before_done = sem("before_done")
        rows_ready = sem("rows_ready")
        scat = [sem("scat0"), sem("scat1")]
        dI, dK, dN, dR, dS = sem("dI"), sem("dK"), sem("dN"), sem("dR"), sem("dS")
        q3, qH, weighed = sem("q3"), sem("qH"), sem("weighed")
        placed = sem("placed")
        biased = sem("biased")
        ranks_read = sem("ranks_read")
        table_made = sem("table_made")
        table_out, table_in = sem("table_out"), sem("table_in")
        dB = sem("dB")
        blank = [sem("blank0"), sem("blank1")]
        blank_start = sem("blank_start")
        weights_e = sem("weights_e")

        rows = pay.rearrange("p a k n -> p (a k) n")
        xs = [rows[:, n, :] for n in range(SLOTS)]
        yy = [rows[:, SLOTS + n, 0:D] for n in range(SLOTS)]
        flat_p = pad.rearrange("p k n -> p (k n)")
        xsT = flat_p[:, 0:2 * D].rearrange("p (b n) -> p b n", b=2)
        w_now = [flat_p[:, 2 * D:4 * D].rearrange("p (k n) -> p k n", k=2),
                 hist_j[:, :].bitcast(fp32).rearrange("p (k n) -> p k n", k=2)]
        flat_h = history.rearrange("p u e -> p (u e)")
        sg = flat_h[:, 0:4 * I].rearrange("p (b n) -> p b n", b=4)
        hh = flat_h[:, 4 * I:8 * I].rearrange("p (b n) -> p b n", b=4)
        xs_in = [sem(f"xs_in{n}") for n in range(SLOTS)]
        dest_kept, w_ready = sem("dest_kept"), sem("w_ready")
        xst_full, xst_ev, gu_full = sem("xst_full"), sem("xst_ev"), sem("gu_full")
        sg_done, hh_done = sem("sg_done"), sem("hh_done")
        dn_full, yy_done = sem("dn_full"), sem("yy_done")
        y_out = [sem(f"y_out{n}") for n in range(SLOTS)]
        er_in = [sem("er_in0"), sem("er_in1")]
        nh, nt_full, nt_ev = sem("nh"), sem("nt_full"), sem("nt_ev")
        sgu_full, ssg_done, sh_done = sem("sgu_full"), sem("ssg_done"), sem("sh_done")
        sd_full, dC, dD, res_done = sem("sd_full"), sem("dC"), sem("dD"), sem("res_done")
        stored = [sem("stored0"), sem("stored1")]

        block = c.enter_context(nc.Block())

        def apart(eng, sem, value):
            if isinstance(value, int):
                return ge(eng, sem, value)
            value = eng.to_reg(value)
            eng.wait_ge(made, MADE)
            eng.wait_ge(sem, value)

        def scaling(j):
            return (nqk[:, j, :].rearrange("p (g d) -> p g d", d=DH), raw[:, j, :].rearrange("p (g d) -> p g d", d=DH),
                    rq[:, 12 * j:12 * j + 12].rearrange("p (g o) -> p g o", o=1).to_broadcast([P, 12, DH]))

        def paid(u):
            return pay_last if isinstance(u.n, int) and u.n == UNITS - 1 else pay[:, 2 * u.par:2 * u.par + 2]

        def slots(u):
            return slot[:, 2 if paid(u) is pay_last else u.par]

        def arrived(t, n):
            return 16 * (t // SLOTS + 1) if isinstance(t, int) else 16 // SLOTS * (t - n) + 16

        def left(t, n):
            return 16 * (t // SLOTS) if isinstance(t, int) else 16 // SLOTS * (t - n)

        def rsqrt(link, y, v, g, t):
            link(nc.vector.tensor_scalar(g.bitcast(i32), v.bitcast(i32), -0.5, float(0x5f3759df), ALU.mult, ALU.add))
            link(nc.vector.tensor_tensor(t, g, g, ALU.mult))
            link(nc.vector.tensor_tensor(t, t, v, ALU.mult))
            link(nc.vector.scalar_tensor_tensor(t, t, -10.0 / 3.0, t, ALU.add, ALU.mult))
            link(nc.vector.scalar_tensor_tensor(g, t, 5.0, g, ALU.add, ALU.mult))
            link(nc.vector.scalar_tensor_tensor(t, g, -27.0 / 1024.0, g, ALU.mult, ALU.mult))
            link(nc.vector.tensor_tensor(t, t, v, ALU.mult))
            link(nc.vector.scalar_tensor_tensor(y, t, 9.0 / 16.0, g, ALU.add, ALU.mult))

        def col(v, a, b):
            return v[a:b].rearrange("(p o) -> p o", o=1)

        def wide(v):
            return v.rearrange("(a n) -> a n", a=1).to_broadcast([P, v.shape[0]])

        er = arena[:, 0:2 * 2 * TOPK * D].rearrange("p (a j k n) -> p a j k n", a=2, j=2, k=TOPK)
        used[0] = 2 * 2 * TOPK * D
        n1h = part(2, 2, D)
        ncT = part(2, 2, D)
        shs, shh = part(2, 2, D), part(2, 2, D)
        esum, e2 = part(2, D), part(2, 2, D)
        res = part(2, 2, D)

        @block.sync
        def _(sp):
            def load(u):
                apart(sp, hats, u.n - 1)
                apart(sp, mask_ready, u.n - 1)
                sp.dma_start(x1[:, at(2 * u.n, 2), :],
                             x[at(2 * u.n, 2)].rearrange("j p n -> p j n")).then_inc(loaded[u.par], 16)
                sp.dma_start(c_in[:, u.par], ctx[at(2 * u.n, 2)].rearrange("j p n -> p j n"))\
                  .then_inc(loaded[u.par], 16)
                sp.dma_start(mask_u8[0:1, u.par], mask[0:1, at(2 * u.n, 2), :])\
                  .then_inc(loaded[u.par], 16)

            load(Unit(0, 0))
            for dst, src in (
                (w_lat[:, :, 0:D], wq.rearrange("(k p) n -> p k n", p=P)),
                (w_lat[:, :, D:3 * D], wlkv.rearrange("(k p) n -> p k n", p=P)),
                (w_ctx[:, 0, :], wkv[0:P, :]), (w_ctx[0:KC, 1, :], wkv[P:DC, :]),
                (w_o, wo.rearrange("(k p) n -> p k n", p=P)),
                (w_r, rw.rearrange("(k p) n -> p k n", p=P)),
                (gl[:, 0:1], col(ln_l_g, 0, P)), (gl[:, 1:2], col(ln_l_g, P, D)),
                (bl[:, 0:1], col(ln_l_b, 0, P)), (bl[:, 1:2], col(ln_l_b, P, D)),
                (gx[:, 0:1], col(ln_x_g, 0, P)), (gx[0:KC, 1:2], col(ln_x_g, P, DC)),
                (bx[:, 0:1], col(ln_x_b, 0, P)), (bx[0:KC, 1:2], col(ln_x_b, P, DC)),
                (gqk[0:DH, 1:2], col(qn_g, 0, DH)), (gqk[DH:P, 1:2], col(qn_g, 0, DH)),
                (gqk[0:DH, 2:3], col(kn_g, 0, DH)), (gqk[DH:P, 2:3], col(kn_g, 0, DH)),
                (bo_b[:, :], wide(bo)), (rb_b[:, 0, :], wide(rb)),
            ):
                sp.dma_start(dst, src).then_inc(consts, 16)
            load(Unit(0, 1))
            for dst, src in ((w_sg, sgate), (w_su, sup), (w_sd, sdown)):
                sp.dma_start(dst[:, :, :], src.rearrange("(k p) n -> p k n", p=P)).then_inc(shared_in, 16)

            def blank_pages(at_page, n, signal):
                for m in range(0, n, FILL):
                    sp.dma_start(lists[at((at_page + m) * P, FILL * P), :].rearrange("(k p) n -> p k n", p=P),
                                 pad[:, :, :]).then_inc(signal, 16)

            def blank_unit(u):
                apart(sp, blank[u.par], BLANK_UNIT * u.i)
                blank_pages(2 * TOPK * u.n + E, 2 * TOPK, blank[u.par])

            def step(s):
                if (s + 3).exists():
                    load(s + 3)
                if s.exists():
                    blank_unit(s)

            sp.wait_ge(made, MADE)
            load(Unit(1, 0))
            blank_pages(0, E, blank_start)
            steps_of_phase_a(sp, step, peeled=6)

            sp.wait_ge(y_done, NB)
            for k in range(2):
                for which, w in ((0, gate), (1, up)):
                    sp.dma_start(w_gu[:, :, k, which * I:(which + 1) * I], w[:, k]).then_inc(weights_e, 16)
            sp.dma_start(w_dn[:, 0:early], down[:, 0:early]).then_inc(weights_e, 16)
            sp.wait_ge(table_made, 1)
            sp.dma_start(tile_table.rearrange("(c p) -> p c", p=P), tab_pc[:, :]).then_inc(table_out, 16)
            sp.wait_ge(table_out, 16)
            sp.dma_start(tab[0:1, :], tile_table.rearrange("(a n) -> a n", a=1)).then_inc(table_in, 16)
            sp.wait_ge(table_in, 16)
            sp.wait_ge(scat[0], 16 * 8 * UNITS // 2)
            sp.wait_ge(scat[1], 16 * 8 * UNITS // 2)
            for par in range(2):
                sp.wait_ge(blank[par], BLANK_UNIT * UNITS // 2)
            sp.wait_ge(rows_ready, UNITS)
            sp.dma_start(w_dn[:, early:E], down[:, early:E]).then_inc(weights_e, 16)

            def load_tile(t, n):
                if not (isinstance(t, int) and t < SLOTS):
                    apart(sp, xst_full, t - SLOTS + 1)
                    apart(sp, dest_kept, t - SLOTS + 1)
                sp.dma_start(xs[n], lists[at(t * P, P), :]).then_inc(xs_in[n], 16)

            for n in range(SLOTS):
                load_tile(n, n)
            with sp.Fori(SLOTS, TILES - SLOTS + 1, SLOTS) as t:
                for n in range(SLOTS):
                    load_tile(t + n, n)

            for n in range(SLOTS):
                sp.wait_ge(y_out[n], 16 * (TILES // SLOTS))
            sp.wait_ge(dn_full, TILES)
            er_d = expert_out.rearrange("(b p k) n -> p b k n", p=P, k=TOPK)

            def load_er(u):
                apart(sp, dC, u.n - 1)
                sp.dma_start(er[:, u.par], er_d[:, at(2 * u.n, 2)]).then_inc(er_in[u.par], 16)

            load_er(Unit(0, 0))
            load_er(Unit(0, 1))
            load_er(Unit(1, 0))
            load_er(Unit(1, 1))
            with sp.Fori(2, UNITS // 2) as i:
                load_er(Unit(i, 0))
                load_er(Unit(i, 1))

        @block.gpsimd
        def _(pool):
            pool.memset(ident[:, :], 0.0).then_inc(q3, 1)
            pool.memset(tri[:, :], 0.0).then_inc(q3, 1)
            pool.memset(ones_sq[:, :], 1.0).then_inc(made, 1)
            pool.memset(ones_row[:, :], 1.0).then_inc(made, 1)
            pool.memset(ones_e[:, :], 1.0).then_inc(made, 1)
            pool.memset(mask_row[:, :, :, :, :], 0.0).then_inc(q3, 1)
            pool.memset(vv[:, :, :, :], 1.0).then_inc(made, 1)
            pool.memset(before[:, :, :], 0.0).then_inc(made, 1)
            pool.memset(gs[:, :, :], BIG).then_inc(made, 1)
            pool.memset(t36[:, :, :], BIG).then_inc(made, 1)
            pool.memset(pad[:, :, 0:D + 1], 0.0).then_inc(made, 1)
            pool.memset(pad[:, :, D + 1:ROW].bitcast(i32), NOWHERE).then_inc(made, 1)
            pool.memset(kept[:, :, :], 0.0).then_inc(made, 1)
            pool.memset(off[:, :, :], 0.0).then_inc(made, 1)
            pool.memset(given[:, :, :], 0.0).then_inc(made, 1)
            pool.iota(first[:, :], pattern=[[P * P, NPT]], base=0, channel_multiplier=P,
                      allow_small_or_imprecise_dtypes=True).then_inc(made, 1)
            pool.iota(place[:, :, :], pattern=[[P * TOPK, 2], [1, TOPK]], base=0,
                      channel_multiplier=TOPK).then_inc(made, 1)
            pool.wait_ge(q3, 3)
            pool.affine_select(out=ident[:, :], in_=ident[:, :], compare_op=ALU.not_equal, fill=1.0,
                               base=0, pattern=[[-1, P]], channel_multiplier=1).then_inc(made, 1)
            pool.affine_select(out=tri[:, :], in_=tri[:, :], compare_op=ALU.is_ge, fill=1.0,
                               base=0, pattern=[[-1, P]], channel_multiplier=1).then_inc(made, 1)
            pool.wait_ge(made, MADE)
            def mask_bias(u):
                apart(pool, loaded[u.par], 48 * (u.i + 1))
                apart(pool, s_full, 2 * (u.n - 1))
                pool.tensor_scalar(mask_row[0:1, u.par, :, 0, 0:P], mask_u8[0:1, u.par], NEG, -NEG,
                                   ALU.mult, ALU.add)
                pool.tensor_scalar(mask_row[0:1, u.par, :, 1, 0:P], mask_u8[0:1, u.par], NEG, -NEG,
                                   ALU.mult, ALU.add).then_inc(mask_ready, 1)

            def head_norms(u):
                v, g, h, t, y = ss[:, 0:12], hy[:, 0, :], hy[:, 1, :], hy[:, 2, :], rq[:, 0:12]
                n = [0]

                def link(ins):
                    n[0] += 1
                    ins.then_inc(qH, 1)
                    apart(pool, qH, H_LINKS * u.n + n[0])

                apart(pool, ss_done, 2 * u.n + 1)
                link(pool.tensor_scalar(v, v, 1.0 / DH, RMS_EPS * RMS_EPS, ALU.mult, ALU.max))
                link(pool.tensor_scalar(g.bitcast(i32), v.bitcast(i32), -0.5, float(0x5f3759df), ALU.mult, ALU.add))
                link(pool.tensor_tensor(h, g, g, ALU.mult))
                link(pool.tensor_tensor(h, h, v, ALU.mult))
                link(pool.tensor_scalar(t, h, -10.0 / 3.0, None, ALU.add))
                link(pool.tensor_tensor(t, t, h, ALU.mult))
                link(pool.tensor_scalar(t, t, 5.0, None, ALU.add))
                link(pool.tensor_tensor(g, t, g, ALU.mult))
                link(pool.tensor_tensor(h, g, g, ALU.mult))
                link(pool.tensor_tensor(h, h, v, ALU.mult))
                link(pool.tensor_scalar(h, h, -27.0 / 1024.0, 9.0 / 16.0, ALU.mult, ALU.add))
                link(pool.tensor_tensor(y, h, g, ALU.mult))
                assert n[0] == H_LINKS

            def scale_first(u):
                head_norms(u)
                apart(pool, pb_free, 2 * u.n + 1)
                apart(pool, t_q, u.n)
                pool.tensor_tensor(*scaling(0), ALU.mult).then_inc(scaled[0], 1)

            def add_bias(u):
                apart(pool, hats, u.n + 1)
                xu = x1[:, at(2 * u.n, 2), :]
                pool.tensor_tensor(xu, xu, bo_b[:, :].rearrange("p (o n) -> p o n", o=1).to_broadcast([P, 2, D]),
                                   ALU.add).then_inc(biased, 1)

            def places(u):
                apart(pool, pay_x, 2 * u.n + 2)
                apart(pool, placed, 2 * u.n)
                pool.tensor_copy(paid(u)[:, :, :, D + 1:ROW].bitcast(i32),
                                 place[:, :, :].rearrange("p j (k o) -> p j k o", o=1)).then_inc(placed, 1)
                apart(pool, placed, 2 * u.n + 1)
                pool.tensor_scalar(place[:, :, :], place[:, :, :], float(2 * P * TOPK), None, ALU.add)\
                    .then_inc(placed, 1)

            def weights(u):
                apart(pool, dR, R_LINKS * (u.n + 1))
                pool.tensor_tensor(paid(u)[:, :, :, D:D + 1],
                                   w4[:, :, :].rearrange("p j (k o) -> p j k o", o=1),
                                   wsum[:, :].rearrange("p (j k o) -> p j k o", k=1, o=1).to_broadcast([P, 2, TOPK, 1]),
                                   ALU.mult).then_inc(weighed, 1)

            def scatter(u):
                apart(pool, weighed, u.n + 1)
                apart(pool, rows_ready, u.n + 1)
                if isinstance(u.n, int) and u.n == 0:
                    pool.wait_ge(blank_start, 16 * E // FILL)
                apart(pool, blank[u.par], BLANK_UNIT * (u.i + 1))
                for j in range(2):
                    for k in range(TOPK):
                        pool.indirect_dma_start(
                            lists, bass.IndirectOffsetOnAxis(ap=slots(u)[:, j, k:k + 1], axis=0),
                            paid(u)[:, j, k, :], None).then_inc(scat[u.par], 16)

            def step(s):
                if (s + 1).exists():
                    scale_first(s + 1)
                if (s + 2).exists():
                    add_bias(s + 2)
                if (s + -2).exists():
                    places(s + -2)
                if (s + 2).exists():
                    mask_bias(s + 2)
                if (s + -2).exists():
                    weights(s + -2)
                    scatter(s + -2)

            mask_bias(Unit(0, 0))
            mask_bias(Unit(0, 1))
            scale_first(Unit(0, 0))
            add_bias(Unit(0, 0))
            add_bias(Unit(0, 1))
            steps_of_phase_a(pool, step)

            def keep_dest(t, n):
                apart(pool, xs_in[n], arrived(t, n))
                apart(pool, y_out[n], left(t, n))
                pool.tensor_copy(dest[:, n, :], xs[n][:, D:ROW].bitcast(i32)).then_inc(dest_kept, 1)

            def scatter_tile(t, n):
                apart(pool, dest_kept, t + 1)
                apart(pool, yy_done, t + 1)
                pool.indirect_dma_start(
                    expert_out, bass.IndirectOffsetOnAxis(ap=dest[:, n, 1:2], axis=0),
                    yy[n], None, bounds_check=T * TOPK - 1, oob_is_err=False).then_inc(y_out[n], 16)

            for t in range(SLOTS):
                keep_dest(t, t)
                if t >= 4:
                    scatter_tile(t - 4, t - 4)
            with pool.Fori(SLOTS, TILES - SLOTS + 1, SLOTS) as t:
                for n in range(SLOTS):
                    keep_dest(t + n, n)
                    scatter_tile(t + (n - 4), (n - 4) % SLOTS)
            for t in range(TILES - 4, TILES):
                scatter_tile(t, t % SLOTS)

        @block.tensor
        def _(pe):
            pe.wait_ge(consts, 16 * CONSTS)
            pe.wait_ge(made, MADE)

            def turn_inputs(u):
                pe.wait_ge(xhat, u.n + 1)
                ge(pe, e_k, 2 * u.n)
                for j in range(2):
                    for k in range(2):
                        m = pe.transpose(ps[0][:, k * D + j * P:k * D + (j + 1) * P],
                                         x_hat[:, j, k * P:(k + 1) * P], ident[:, :])
                m.then_inc(t_x, 1)
                pe.wait_ge(hats, u.n + 1)
                ge(pe, e_q, u.n)
                for j in range(2):
                    pe.transpose(ps[1][:, j * P:(j + 1) * P], c_hat[:, j, 0:P], ident[:, :])
                    m = pe.transpose(ps[1][0:KC, D + j * P:D + (j + 1) * P], c_hat[:, j, P:DC], ident[:, :])
                m.then_inc(t_c, 1)

            def turn_n1(u):
                pe.wait_ge(pay_x, 2 * u.n + 2)
                pe.wait_ge(e_x, upto(u.n + 3, UNITS))
                pe.wait_ge(e_k, upto(2 * u.n + 4, NB))
                ge(pe, e_n, u.n)
                for j in range(2):
                    for k in range(2):
                        m = pe.transpose(ps[0][:, k * D + j * P:k * D + (j + 1) * P],
                                         paid(u)[:, j, 0, k * P:(k + 1) * P], ident[:, :])
                m.then_inc(t_n, 1)

            def project_q(u, j):
                b = 2 * u.n + j
                pe.wait_ge(e_x, u.n + 1)
                tok = slice(j * P, (j + 1) * P)
                if j == 0:
                    ge(pe, y_done, 2 * u.n - 3)
                ge(pe, pa_free, b)
                for k in range(2):
                    m = pe.matmul(ps[2][:, :], lnT[:, k, tok], w_lat[:, k, 0:2 * D], start=k == 0, stop=k == 1)
                m.then_inc(pa_full, 1)

            def project_kv(u, j):
                b = 2 * u.n + j
                pe.wait_ge(e_c, u.n + 1)
                tok = slice(j * P, (j + 1) * P)
                if j == 0:
                    ge(pe, y_done, 2 * (u.n - 1))
                ge(pe, pb_free, b)
                pe.matmul(ps[3][:, :], cT[:, 0, tok], w_ctx[:, 0, :], start=True, stop=False)
                pe.matmul(ps[3][:, :], cT[0:KC, 1, tok], w_ctx[0:KC, 1, :], start=False, stop=True)\
                  .then_inc(pb_full, 1)

            def project_v(u, j):
                b = 2 * u.n + j
                pe.wait_ge(e_x, u.n + 1)
                tok = slice(j * P, (j + 1) * P)
                ge(pe, pc_free, b)
                if j == 0:
                    ge(pe, ranks_read, u.n - 3)
                    ge(pe, lg_exp, u.n - 2)
                for k in range(2):
                    m = pe.matmul(ps[4][:, 0:D], lnT[:, k, tok], w_lat[:, k, 2 * D:3 * D], start=k == 0, stop=k == 1)
                m.then_inc(pc_full, 1)

            def turn_k(u, j):
                bank = ps[1 - j]
                pe.wait_ge(scaled[j], u.n + 1)
                if j == 0:
                    pe.wait_ge(e_c, u.n + 1)
                else:
                    pe.wait_ge(e_x, u.n + 1)
                    ge(pe, e_n, u.n - 1)
                for k in range(2):
                    pe.transpose(bank[:, k * D:k * D + P], nqk[:, j, 2 * D + k * P:2 * D + (k + 1) * P], ident[:, :])
                    m = pe.transpose(bank[:, k * D + P:(k + 1) * D], nqk[:, j, D + k * P:D + (k + 1) * P], ident[:, :])
                m.then_inc(t_k, 1)

            def turn_q(u):
                pe.wait_ge(e_k, 2 * u.n + 1)
                for k in range(2):
                    for j in range(2):
                        m = pe.transpose(ps[1][:, k * D + j * P:k * D + (j + 1) * P],
                                         nqk[:, j, k * P:(k + 1) * P], ident[:, :])
                m.then_inc(t_q, 1)

            def scores(u, j):
                b = 2 * u.n + j
                pe.wait_ge(mask_ready, u.n + 1)
                pe.wait_ge(e_q, u.n + 1)
                pe.wait_ge(e_k, b + 1)
                ge(pe, pt_ev, b)
                for r in range(2):
                    pe.matmul(psS[:, r], ones_row[:, :], mask_row[0:1, u.par, j], start=True, stop=False)
                for ch in range(2):
                    for r in range(2):
                        rows = slice(r * DH, (r + 1) * DH)
                        m = pe.matmul(psS[:, r, ch], qT[rows, u.par, ch, j, :],
                                      kT[rows, 2 * u.par + j, ch, :], start=False, stop=ch == 1)
                m.then_inc(s_full, 1)

            def turn_probs(u, j):
                b = 2 * u.n + j
                pe.wait_ge(exp_done, b + 1)
                for key in range(2):
                    for g in range(H):
                        m = pe.transpose(psS[:, key].rearrange("p a n -> p (a n)")[:, g * P:(g + 1) * P],
                                         probs[:, j, g, key * P:(key + 1) * P], ident[:, :])
                m.then_inc(pt_full, 1)

            def mix_values(u, j):
                b = 2 * u.n + j
                pe.wait_ge(pt_ev, b + 1)
                pe.wait_ge(pc_free, b + 1)
                ge(pe, ot_ev, b)
                for g in range(H):
                    h = 2 * (g % 2) + g // 2
                    for key in range(2):
                        m = pe.matmul(psO[:, g * (DH + 1):(g + 1) * (DH + 1)],
                                      probsT[:, j, key, g * P:(g + 1) * P], vv[:, 4 * u.par + 2 * j + key, h, :],
                                      start=key == 0, stop=key == 1)
                m.then_inc(pv_full, 1)

            def turn_o(u, j):
                b = 2 * u.n + j
                pe.wait_ge(on_done, b + 1)
                for k in range(2):
                    m = pe.transpose(psO[:, k * P:(k + 1) * P], o_n[:, k * P:(k + 1) * P], ident[:, :])
                m.then_inc(ot_full, 1)

            def out_proj(u, j):
                b = 2 * u.n + j
                pe.wait_ge(ot_ev, b + 1)
                pe.wait_ge(pb_free, upto(2 * u.n + 4, NB))
                for k in range(2):
                    m = pe.matmul(ps[2 + j][:, 0:D], oT[:, k * P:(k + 1) * P], w_o[:, k, :], start=k == 0, stop=k == 1)
                m.then_inc(y_full, 1)

            def logits(u):
                pe.wait_ge(e_n, u.n + 1)
                ge(pe, ranks_read, u.n)
                pe.wait_ge(pc_free, upto(2 * u.n + 6, NB))
                for j in range(2):
                    for k in range(2):
                        m = pe.matmul(ps[4][:, D + j * E:D + (j + 1) * E], n1T[:, k, j * P:(j + 1) * P], w_r[:, k, :],
                                      start=k == 0, stop=k == 1)
                m.then_inc(lg_full, 1)

            def positions(u):
                pe.wait_ge(ch_done, u.n + 1)
                pe.wait_ge(lg_exp, upto(u.n + 1, UNITS))
                pe.wait_ge(pc_free, upto(2 * u.n + 8, NB))
                pe.wait_ge(before_done, u.n + 1)
                for j in range(2):
                    o = ps[4][:, D + (2 + j) * E:D + (3 + j) * E]
                    pe.matmul(o, tri[:, :], chosen[:, u.par, j, :], start=True, stop=False)
                    if j == 1:
                        pe.matmul(o, ones_sq[:, :], chosen[:, u.par, 0, :], start=False, stop=False)
                    pe.matmul(o, ones_sq[:, :], before[:, u.par, :], start=False, stop=True)
                pe.matmul(ps[4][:, D + 4 * E:D + 5 * E], ones_sq[:, :], before[:, 1 - u.par, :],
                          start=True, stop=True).then_inc(pos_full, 1)

            def step(s):
                a, cc, r = s + 1, s + -1, s + -2
                if s.exists():
                    scores(s, 0)
                if a.exists():
                    project_q(a, 0)
                    project_kv(a, 0)
                    project_v(a, 0)
                if s.exists():
                    turn_probs(s, 0)
                if a.exists():
                    project_q(a, 1)
                if s.exists():
                    scores(s, 1)
                if a.exists():
                    project_kv(a, 1)
                if s.exists():
                    mix_values(s, 0)
                    turn_probs(s, 1)
                    turn_o(s, 0)
                if a.exists():
                    project_v(a, 1)
                if a.exists():
                    turn_k(a, 0)
                if s.exists():
                    mix_values(s, 1)
                if r.exists():
                    positions(r)
                if cc.exists():
                    turn_n1(cc)
                if s.exists():
                    out_proj(s, 0)
                    turn_o(s, 1)
                if a.exists():
                    turn_k(a, 1)
                if cc.exists():
                    logits(cc)
                if a.exists():
                    turn_q(a)
                if s.exists():
                    out_proj(s, 1)
                if (s + 2).exists():
                    turn_inputs(s + 2)

            turn_inputs(Unit(0, 0))
            for j in range(2):
                project_q(Unit(0, 0), j)
                project_kv(Unit(0, 0), j)
                project_v(Unit(0, 0), j)
            turn_k(Unit(0, 0), 0)
            turn_k(Unit(0, 0), 1)
            turn_q(Unit(0, 0))
            turn_inputs(Unit(0, 1))
            steps_of_phase_a(pe, step)

            pe.wait_ge(rows_ready, UNITS)

            pe.wait_ge(table_in, 16)
            pe.wait_ge(weights_e, 16 * 6)

            def turn_x(t, n):
                pe.wait_ge(xs_in[n], arrived(t, n))
                ge(pe, xst_ev, t - 1)
                for k in range(2):
                    m = pe.transpose(ps[n % 2][:, k * P:(k + 1) * P], xs[n][:, k * P:(k + 1) * P], ident[:, :])
                m.then_inc(xst_full, 1)

            def gate_up(t, n):
                pe.wait_ge(w_ready, t + 1)
                ge(pe, hh_done, t - 1)
                for which in range(2):
                    for k in range(2):
                        m = pe.matmul(ps[2 + n % 2][:, which * P:(which + 1) * P],
                                      w_now[n % 2][:, k, which * I:(which + 1) * I],
                                      xsT[:, n % 2, k * P:(k + 1) * P], start=k == 0, stop=k == 1)
                m.then_inc(gu_full, 1)

            dbank = [psS[:, 0].rearrange("p a n -> p (a n)"), psS[:, 1].rearrange("p a n -> p (a n)")]

            def down_proj(t, n, e):
                pe.wait_ge(hh_done, t + 1)
                ge(pe, yy_done, t - 1)
                pe.matmul(dbank[n % 2][:, 0:D], hh[:, n % 4, :],
                          w_dn[:, at(e, 1), :].rearrange("p a n -> p (a n)"), start=True, stop=True)\
                  .then_inc(dn_full, 1)

            def expert(t):
                return pe.value_load(tab[0:1, at(t, 1)], min_val=0, max_val=E - 1)

            turn_x(0, 0)
            turn_x(1, 1)
            for t in range(SLOTS):
                gate_up(t, t)
                turn_x(t + 2, (t + 2) % SLOTS)
                if t >= 1:
                    down_proj(t - 1, t - 1, expert(t - 1))
            now_regs = [pe.alloc_register(f"expert{d}") for d in range(SLOTS)]
            with pe.Fori(SLOTS, TILES - 2 * SLOTS + 1, SLOTS) as t:
                pe.load(now_regs, tab[0:1, at(t - 1, SLOTS)])
                now = [pe.snap(r, min_val=0, max_val=E - 1) for r in now_regs]
                for n in range(SLOTS):
                    gate_up(t + n, n)
                    turn_x(t + (n + 2), (n + 2) % SLOTS)
                    down_proj(t + (n - 1), (n - 1) % SLOTS, now[n])
            for t in range(TILES - SLOTS, TILES + 1):
                if t < TILES:
                    gate_up(t, t % SLOTS)
                if t + 2 < TILES:
                    turn_x(t + 2, (t + 2) % SLOTS)
                down_proj(t - 1, (t - 1) % SLOTS, expert(t - 1))

            pe.wait_ge(yy_done, TILES)
            pe.wait_ge(shared_in, 16 * 3)

            def shared_turn(u):
                pe.wait_ge(nh, u.n + 1)
                ge(pe, nt_ev, u.n)
                for j in range(2):
                    for k in range(2):
                        m = pe.transpose(ps[0][:, k * D + j * P:k * D + (j + 1) * P],
                                         n1h[:, u.par, j, k * P:(k + 1) * P], ident[:, :])
                m.then_inc(nt_full, 1)

            def shared_up(u, mm):
                pe.wait_ge(nt_ev, u.n + 1)
                ge(pe, sh_done, 2 * u.n - 1 + mm)
                for which, w in ((0, w_sg), (1, w_su)):
                    for k in range(2):
                        m = pe.matmul(ps[1 + 2 * mm + which][:, 0:D], w[:, k, mm * P:(mm + 1) * P],
                                      ncT[:, u.par, k, :], start=k == 0, stop=k == 1)
                m.then_inc(sgu_full, 1)

            def shared_down(u):
                pe.wait_ge(sh_done, 2 * u.n + 2)
                for j in range(2):
                    ge(pe, res_done, 2 * u.n + j - 1)
                    for mm in range(2):
                        m = pe.matmul(dbank[j][:, 0:D], shh[:, u.par, mm, j * P:(j + 1) * P], w_sd[:, mm, :],
                                      start=mm == 0, stop=mm == 1)
                    m.then_inc(sd_full, 1)

            def step(s):
                if s.exists():
                    shared_up(s, 0)
                if (s + -1).exists():
                    shared_down(s + -1)
                if (s + 1).exists():
                    shared_turn(s + 1)
                if s.exists():
                    shared_up(s, 1)

            shared_turn(Unit(0, 0))
            steps_of_phase_c(pe, step)

        @block.scalar
        def _(act):
            act.wait_ge(made, MADE)

            def normalise(u):
                act.wait_ge(dN, N_LINKS * (u.n + 1))
                ge(act, t_x, u.n)
                for j in range(2):
                    a = act.activation(x_hat[:, j, :], x1[:, at(2 * u.n + j, 1), :].rearrange("p a n -> p (a n)"),
                                       ACT.Identity, bias=nb[:, j:j + 1], scale=ra[:, j:j + 1])
                a.then_inc(xhat, 1)
                ge(act, t_c, u.n)
                for j in range(2):
                    a = act.activation(c_hat[:, j, :], c_in[:, u.par, j, :],
                                       ACT.Identity, bias=nb[:, 2 + j:3 + j], scale=ra[:, 2 + j:3 + j])
                a.then_inc(hats, 1)

            def rows_to_scatter(u, j):
                if j == 0:
                    act.wait_ge(dN, N_LINKS * (u.n + 4))
                    if paid(u) is not pay_last:
                        ge(act, scat[u.par], 128 * u.i)
                act.activation(paid(u)[:, j, :, 0:D], x1[:, at(2 * u.n + j, 1), :].to_broadcast([P, TOPK, D]),
                               ACT.Identity, bias=nb[:, 4 + j:5 + j], scale=ra[:, 4 + j:5 + j]).then_inc(pay_x, 1)

            def inputs(u):
                act.wait_ge(t_x, u.n + 1)
                ge(act, pc_full, 2 * u.n)
                for k in range(2):
                    a = act.activation(lnT[:, k, :], ps[0][:, k * D:(k + 1) * D], ACT.Identity,
                                       bias=bl[:, k:k + 1], scale=gl[:, k:k + 1])
                a.then_inc(e_x, 1)
                act.wait_ge(t_c, u.n + 1)
                act.activation(cT[:, 0, :], ps[1][:, 0:D], ACT.Identity, bias=bx[:, 0:1], scale=gx[:, 0:1])
                act.activation(cT[0:KC, 1, :], ps[1][0:KC, D:2 * D], ACT.Identity,
                               bias=bx[0:KC, 1:2], scale=gx[0:KC, 1:2]).then_inc(e_c, 1)

            def projected_q(u, j):
                b = 2 * u.n + j
                act.wait_ge(pa_full, b + 1)
                ge(act, ss_done, b - 1)
                act.activation(sq[:, j, 0:2 * D], ps[2][:, :], ACT.Square)
                ge(act, scaled[j], u.n)
                act.activation(raw[:, j, 0:2 * D], ps[2][:, :], ACT.Copy).then_inc(pa_free, 1)

            def projected_kv(u, j):
                b = 2 * u.n + j
                act.wait_ge(pb_full, b + 1)
                act.activation(sq[:, j, 2 * D:3 * D], ps[3][:, 0:D], ACT.Square).then_inc(sq_full, 1)
                act.activation(raw[:, j, 2 * D:3 * D], ps[3][:, 0:D], ACT.Copy)
                ge(act, pv_full, 2 * u.n - 3 + j)
                act.activation(vv[:, 4 * u.par + 2 * j, :, 0:DH],
                               ps[3][:, D:2 * D].rearrange("p (h d) -> p h d", d=DH), ACT.Copy).then_inc(pb_free, 1)

            def values_copy(u, j):
                b = 2 * u.n + j
                act.wait_ge(pc_full, b + 1)
                act.activation(vv[:, 4 * u.par + 2 * j + 1, :, 0:DH],
                               ps[4][:, 0:D].rearrange("p (h d) -> p h d", d=DH), ACT.Copy).then_inc(pc_free, 1)

            def exps(u, j):
                b = 2 * u.n + j
                act.wait_ge(m_done, b + 1)
                ge(act, pt_full, b - 1)
                for g in range(H):
                    a = act.activation(probs[:, j, g, :], psS[:, g // 2, g % 2], ACT.Exp,
                                       bias=nmax[:, j, g:g + 1])
                a.then_inc(exp_done, 1)

            def probs_copy(u, j):
                b = 2 * u.n + j
                act.wait_ge(pt_full, b + 1)
                ge(act, pv_full, b - 1)
                for key in range(2):
                    a = act.activation(probsT[:, j, key, :], psS[:, key].rearrange("p a n -> p (a n)"), ACT.Copy)
                a.then_inc(pt_ev, 1)

            def o_copy(u, j):
                b = 2 * u.n + j
                act.wait_ge(ot_full, b + 1)
                ge(act, y_full, b)
                act.activation(oT, psO[:, 0:D], ACT.Copy).then_inc(ot_ev, 1)

            def n1_copy(u):
                act.wait_ge(t_n, u.n + 1)
                ge(act, lg_full, u.n)
                act.activation(n1T.rearrange("p k n -> p (k n)"), ps[0][:, :], ACT.Copy).then_inc(e_n, 1)

            def logit_exp(u):
                act.wait_ge(lg_full, u.n + 1)
                ge(act, ch_done, u.n)
                act.activation(esc[:, :, :].rearrange("p j e -> p (j e)"), ps[4][:, D:D + 2 * E], ACT.Exp,
                               scale=-1.0).then_inc(lg_exp, 1)

            def k_copy(u, j):
                act.wait_ge(t_k, 2 * u.n + j + 1)
                ge(act, s_full, 2 * (u.n - 2) + j + 1)
                act.activation(kT[:, 2 * u.par + j].rearrange("p k n -> p (k n)"), ps[1 - j][:, :], ACT.Copy)\
                   .then_inc(e_k, 1)

            def q_copy(u):
                act.wait_ge(t_q, u.n + 1)
                act.activation(qT[:, u.par].rearrange("p k j n -> p (k j n)"), ps[1][:, :], ACT.Copy,
                               scale=gqk[:, 0:1]).then_inc(e_q, 1)

            def step(s):
                a, cc = s + 1, s + -1
                if s.exists():
                    exps(s, 0)
                if a.exists():
                    projected_q(a, 0)
                    projected_kv(a, 0)
                    values_copy(a, 0)
                if s.exists():
                    probs_copy(s, 0)
                if (s + 2).exists():
                    normalise(s + 2)
                if a.exists():
                    projected_q(a, 1)
                if s.exists():
                    exps(s, 1)
                if cc.exists():
                    rows_to_scatter(cc, 0)
                if a.exists():
                    projected_kv(a, 1)
                if s.exists():
                    probs_copy(s, 1)
                    o_copy(s, 0)
                if a.exists():
                    values_copy(a, 1)
                if cc.exists():
                    rows_to_scatter(cc, 1)
                if a.exists():
                    k_copy(a, 0)
                if cc.exists():
                    n1_copy(cc)
                if s.exists():
                    o_copy(s, 1)
                if a.exists():
                    k_copy(a, 1)
                if cc.exists():
                    logit_exp(cc)
                if a.exists():
                    q_copy(a)
                if (s + 2).exists():
                    inputs(s + 2)

            normalise(Unit(0, 0))
            act.wait_ge(consts, 16 * CONSTS)
            inputs(Unit(0, 0))
            normalise(Unit(0, 1))
            for j in range(2):
                projected_q(Unit(0, 0), j)
                projected_kv(Unit(0, 0), j)
                values_copy(Unit(0, 0), j)
            k_copy(Unit(0, 0), 0)
            k_copy(Unit(0, 0), 1)
            act.wait_ge(gains, 2)
            q_copy(Unit(0, 0))
            inputs(Unit(0, 1))
            steps_of_phase_a(act, step)

            act.wait_ge(table_in, 16)
            act.wait_ge(weights_e, 16 * 6)

            def rows_copy(t, n, e):
                act.wait_ge(xst_full, t + 1)
                ge(act, gu_full, t - 1)
                act.activation(xsT[:, n % 2, :], ps[n % 2][:, 0:D], ACT.Copy).then_inc(xst_ev, 1)
                act.activation(w_now[n % 2], w_gu[:, at(e, 1)].rearrange("p a k n -> p (a k) n"), ACT.Copy)\
                   .then_inc(w_ready, 1)

            def gate_silu(t, n):
                act.wait_ge(gu_full, t + 1)
                ge(act, hh_done, t - 3)
                act.activation(sg[:, n % 4, :], ps[2 + n % 2][:, 0:P], ACT.Silu).then_inc(sg_done, 1)

            def expert(t):
                return act.value_load(tab[0:1, at(t, 1)], min_val=0, max_val=E - 1)

            rows_copy(0, 0, expert(0))
            rows_copy(1, 1, expert(1))
            for t in range(SLOTS):
                gate_silu(t, t)
                rows_copy(t + 2, (t + 2) % SLOTS, expert(t + 2))
            next_regs = [act.alloc_register(f"next_expert{d}") for d in range(SLOTS)]
            with act.Fori(SLOTS, TILES - 2 * SLOTS + 1, SLOTS) as t:
                act.load(next_regs, tab[0:1, at(t + 2, SLOTS)])
                now = [act.snap(r, min_val=0, max_val=E - 1) for r in next_regs]
                for n in range(SLOTS):
                    gate_silu(t + n, n)
                    rows_copy(t + (n + 2), (n + 2) % SLOTS, now[n])
            for t in range(TILES - SLOTS, TILES):
                gate_silu(t, t % SLOTS)
                if t + 2 < TILES:
                    rows_copy(t + 2, (t + 2) % SLOTS, expert(t + 2))

            act.wait_ge(dn_full, TILES)
            out_d = out.rearrange("b p n -> p b n")

            def turned(u):
                act.wait_ge(nt_full, u.n + 1)
                ge(act, sgu_full, 2 * (u.n - 1))
                act.activation(ncT[:, u.par].rearrange("p k n -> p (k n)"), ps[0][:, :], ACT.Copy).then_inc(nt_ev, 1)

            def shared_silu(u, mm):
                act.wait_ge(sgu_full, 2 * u.n + mm + 1)
                ge(act, sh_done, 2 * (u.n - 2) + mm + 1)
                act.activation(shs[:, u.par, mm, :], ps[1 + 2 * mm][:, 0:D], ACT.Silu).then_inc(ssg_done, 1)

            def store(u):
                act.wait_ge(res_done, 2 * u.n + 2)
                act.dma_start(out_d[:, at(2 * u.n, 2), :], res[:, u.par]).then_inc(stored[u.par], 16)

            def step(s):
                if s.exists():
                    shared_silu(s, 0)
                if (s + 1).exists():
                    turned(s + 1)
                if s.exists():
                    shared_silu(s, 1)
                if (s + -1).exists():
                    store(s + -1)

            turned(Unit(0, 0))
            steps_of_phase_c(act, step)
            for s in stored:
                act.wait_ge(s, 16 * UNITS // 2)

        @block.vector
        def _(dve):
            dve.wait_ge(made, MADE)

            def chain(order, per_unit, u):
                n = [0]

                def link(ins, before_plain=False):
                    n[0] += 1
                    ins.then_inc(order, 1)
                    (apart if before_plain else ge)(dve, order, per_unit * u.n + n[0])

                return link, n

            def parts_of(run):
                return run.exists(), (run + -3).exists()

            def input_statistics(run):
                apart(dve, loaded[run.par], 48 * (run.i + 1))
                for j in range(2):
                    dve.bn_stats(stats[:, j, :], x1[:, at(2 * run.n + j, 1), :].rearrange("p a n -> p (a n)"))
                    m = dve.bn_stats(stats[:, 2 + j, :], c_in[:, run.par, j, :])
                m.then_inc(dI, 1)

            def x1_statistics(run):
                link, n = chain(dN, N_LINKS, run)
                new, old = parts_of(run)
                if old:
                    u = run + -3
                    apart(dve, y_done, 2 * u.n + 2)
                    for j in range(2):
                        m = dve.bn_stats(stats[:, 4 + j, :], x1[:, at(2 * u.n + j, 1), :].rearrange("p a n -> p (a n)"))
                    link(m, True)
                else:
                    link(dve.bn_stats(stats[:, 4, :], c_in[:, run.par, 0, :]), True)
                if new:
                    apart(dve, dI, run.n + 1)
                for j in range(0 if new else 4, 6 if old else 4):
                    m = dve.bn_aggr(mv[:, j, :], stats[:, j, :])
                link(m)

            def deviations(run):
                link, n = chain(dN, N_LINKS, run)
                n[0] = 2
                new, old = parts_of(run)
                if new:
                    dve.tensor_scalar(va[:, 0:2], mv[:, 0:2, 1], 1.0 + LN_EPS, LN_EPS * LN_EPS, ALU.mult, ALU.add)
                lo, hi = 2 if new else 4, 6 if old else 4
                link(dve.tensor_scalar(va[:, lo:hi], mv[:, lo:hi, 1], LN_EPS, None, ALU.add))
                lo = 0 if new else 4
                ge(dve, hats, upto(run.n, UNITS))
                ge(dve, pay_x, 2 * (run.n - 3))
                rsqrt(link, ra[:, lo:hi], va[:, lo:hi], ry[:, lo:hi], rt[:, lo:hi])
                if old:
                    u = run + -3
                    dve.tensor_copy(mr[:, at(2 * u.n, 2), 0:1], mv[:, 4:6, 0:1])
                    dve.tensor_copy(mr[:, at(2 * u.n, 2), 1:2], ra[:, 4:6].rearrange("p (j o) -> p j o", o=1))
                link(dve.scalar_tensor_tensor(nb[:, lo:hi], mv[:, lo:hi, 0], -1.0, ra[:, lo:hi], ALU.mult, ALU.mult))
                assert n[0] == N_LINKS

            def square_sums(u, j):
                b = 2 * u.n + j
                dve.wait_ge(sq_full, b + 1)
                ge(dve, scaled[j], u.n)
                dve.tensor_reduce(ss[:, 12 * j:12 * j + 12], sq[:, j, :].rearrange("p (g d) -> p g d", d=DH), AX, ALU.add)\
                   .then_inc(ss_done, 1)

            def maxima(u, j):
                b = 2 * u.n + j
                dve.wait_ge(s_full, b + 1)
                ge(dve, exp_done, b - 1)
                dve.tensor_reduce(nmax[:, j, :], psS[:, :, :, :].rearrange("p r k n -> p (r k) n"), AX, ALU.max,
                                  negate=True).then_inc(m_done, 1)

            def normalise_o(u, j):
                b = 2 * u.n + j
                dve.wait_ge(pv_full, b + 1)
                ge(dve, ot_full, b)
                o = psO[:, 0:H * (DH + 1)].rearrange("p (g d) -> p g d", d=DH + 1)
                dve.reciprocal(rden[:, :], o[:, :, DH]).then_inc(dS, 1)
                dve.wait_ge(dS, b + 1)
                dve.tensor_tensor(o_n.rearrange("p (k r d) -> p r k d", k=2, r=2),
                                  o[:, :, 0:DH].rearrange("p (r k) d -> p r k d", k=2),
                                  rden[:, :].rearrange("p (r k o) -> p r k o", k=2, o=1).to_broadcast([P, 2, 2, DH]),
                                  ALU.mult).then_inc(on_done, 1)

            def residual(u, j):
                b = 2 * u.n + j
                dve.wait_ge(y_full, b + 1)
                dve.wait_ge(biased, u.n + 1)
                xb = x1[:, at(b, 1), :].rearrange("p a n -> p (a n)")
                dve.tensor_tensor(xb, xb, ps[2 + j][:, 0:D], ALU.add).then_inc(y_done, 1)

            def scale_second(u):
                link, n = chain(dK, K_LINKS, u)
                v = ss[:, 12:24]
                dve.wait_ge(ss_done, 2 * u.n + 2)
                link(dve.tensor_scalar(v, v, 1.0 / DH, RMS_EPS * RMS_EPS, ALU.mult, ALU.max))
                rsqrt(link, rq[:, 12:24], v, ky[:, 0, :], ky[:, 1, :])
                assert n[0] == K_LINKS
                dve.wait_ge(pb_free, 2 * u.n + 2)
                ge(dve, t_q, u.n)
                dve.tensor_tensor(*scaling(1), ALU.mult).then_inc(scaled[1], 1)

            def top_scores(u):
                link, n = chain(dR, R_LINKS, u)
                dve.wait_ge(lg_exp, u.n + 1)
                link(dve.tensor_scalar(esc[:, :, :], esc[:, :, :], 1.0, None, ALU.add))
                link(dve.reciprocal(sc[:, :, :], esc[:, :, :]))
                link(dve.tensor_tensor(sfc[:, :, :], sc[:, :, :], rb_b[:, :, :].to_broadcast([P, 2, E]), ALU.add), True)
                for j in range(2):
                    for g in range(NG):
                        m = dve.max(g8[:, j, g, :], sfc[:, j, 8 * g:8 * g + 8])
                link(m)

            def best_groups(u):
                link, n = chain(dR, R_LINKS, u)
                n[0] = G_LINKS // 2
                link(dve.tensor_tensor(gs[:, :, 0:NG], g8[:, :, :, 0], g8[:, :, :, 1], ALU.add), True)
                for j in range(2):
                    m = dve.max(m8[:, j, :], gs[:, j, :])
                link(m, True)
                for j in range(2):
                    m = dve.match_replace(gr[:, j, :], m8[:, j, :], gs[:, j, :], -BIG)
                link(m)
                link(dve.tensor_tensor(gm[:, :, :], gr[:, :, 0:NG], gs[:, :, 0:NG], ALU.not_equal))

            def best_experts(u):
                link, n = chain(dR, R_LINKS, u)
                n[0] = G_LINKS
                for j in range(2):
                    m = dve.tensor_tensor(t36[:, j, 0:E].rearrange("p (g e) -> p g e", g=NG),
                                          sfc[:, j, :].rearrange("p (g e) -> p g e", g=NG),
                                          gm[:, j, :].rearrange("p (g o) -> p g o", o=1).to_broadcast([P, NG, E // NG]),
                                          ALU.mult)
                link(m, True)
                for j in range(2):
                    m = dve.max(n8[:, j, :], t36[:, j, :])
                link(m, True)
                for j in range(2):
                    m = dve.match_replace(r36[:, j, :], n8[:, j, :], t36[:, j, :], -BIG)
                link(m)

            def choose_experts(u):
                link, n = chain(dR, R_LINKS, u)
                n[0] = G_LINKS + 3
                ge(dve, pos_full, u.n)
                link(dve.tensor_tensor(chosen[:, u.par], r36[:, :, 0:E], t36[:, :, 0:E], ALU.not_equal))
                dve.tensor_tensor(before[:, 1 - u.par, :], before[:, u.par, :], chosen[:, u.par, 0, :], ALU.add)\
                   .then_inc(ch_done, 1)
                link(dve.tensor_tensor(wts[:, :, :], chosen[:, u.par], sc[:, :, :], ALU.mult))
                dve.tensor_tensor(before[:, 1 - u.par, :], before[:, 1 - u.par, :], chosen[:, u.par, 1, :], ALU.add)\
                   .then_inc(before_done, 1)
                assert n[0] == C_LINKS, n[0]

            def read_ranks(u):
                dve.wait_ge(pos_full, u.n + 1)
                rank = ps[4][:, D + 2 * E:D + 4 * E].rearrange("p (j e) -> p j e", j=2)
                both = [P, 2, E]
                dve.tensor_tensor(later[:, :, :], rank, kept[:, :, :].to_broadcast(both), ALU.is_ge)
                dve.scalar_tensor_tensor(code[:, :, :], rank, 1.0, off[:, :, :].to_broadcast(both), ALU.add, ALU.add)
                dve.tensor_scalar(need_i[:, :], ps[4][:, D + 4 * E:D + 5 * E], float(P - 1), None, ALU.add)\
                   .then_inc(ranks_read, 1)

            def assign(u):
                link, n = chain(dR, R_LINKS, u)
                n[0] = C_LINKS
                both = [P, 2, E]
                dve.wait_ge(ranks_read, u.n + 1)
                ge(dve, weighed, u.n)
                dve.tensor_reduce(wsum[:, :], wts[:, :, :], AX, ALU.add)
                link(dve.tensor_scalar(need[:, 0, :], need_i[:, :], 7, 7, ALU.logical_shift_right, ALU.logical_shift_left))
                dve.tensor_scalar(wsum[:, :], wsum[:, :], 1e-20, 1.0 / ROUTE_SCALE, ALU.add, ALU.mult)
                link(dve.tensor_tensor(new[:, :, :], need[:, :, :], kept[:, :, :], ALU.subtract))
                dve.reciprocal(wsum[:, :], wsum[:, :])
                link(dve.tensor_tensor_scan(given[:, u.par, :], ones_e[:, :], new[:, 0, :],
                                            given[:, 1 - u.par, E - 1:E], ALU.mult, ALU.add))
                link(dve.tensor_tensor(off_n[:, :, :], given[:, u.par:u.par + 1, :], need[:, :, :], ALU.subtract))
                link(dve.tensor_tensor(delta[:, :, :], off_n[:, :, :], off[:, :, :], ALU.subtract))
                dve.tensor_tensor(later[:, :, :], later[:, :, :], delta[:, :, :].to_broadcast(both), ALU.mult)
                link(dve.scalar_tensor_tensor(moved[:, :, :], new[:, :, :], 0.0, delta[:, :, :], ALU.is_gt, ALU.mult))
                dve.tensor_tensor(code[:, :, :], code[:, :, :], later[:, :, :], ALU.add)
                dve.tensor_tensor(off[:, :, :], off[:, :, :], moved[:, :, :], ALU.add)
                dve.tensor_copy(kept[:, :, :], need[:, :, :])
                link(dve.tensor_copy(history[:, at(u.n, 1), :], given[:, u.par:u.par + 1, :]))
                link(dve.tensor_tensor(code2[:, :, :], code[:, :, :], chosen[:, u.par], ALU.mult), True)
                for j in range(2):
                    m = dve.max(c8[:, j, :], code2[:, j, :])
                link(m)
                for j in range(2):
                    for k in range(TOPK):
                        m = dve.scalar_tensor_tensor(wj[:, j, k, :], code2[:, j, :], c8[:, j, k:k + 1], wts[:, j, :],
                                                     ALU.is_equal, ALU.mult, accum_out=w4[:, j, k:k + 1])
                link(m)
                dve.tensor_scalar(slots(u), c8[:, :, 0:TOPK], -1.0, None, ALU.add).then_inc(rows_ready, 1)
                assert n[0] == R_LINKS, n[0]

            def step(s):
                a, r = s + 1, s + -2
                run = s + 2
                if s.exists():
                    maxima(s, 0)
                if any(parts_of(run)):
                    x1_statistics(run)
                    deviations(run)
                if a.exists():
                    square_sums(a, 0)
                if r.exists():
                    top_scores(r)
                if s.exists():
                    maxima(s, 1)
                if r.exists():
                    best_groups(r)
                    best_experts(r)
                if s.exists():
                    normalise_o(s, 0)
                if r.exists():
                    choose_experts(r)
                if a.exists():
                    square_sums(a, 1)
                if a.exists():
                    scale_second(a)
                if s.exists():
                    normalise_o(s, 1)
                if r.exists():
                    read_ranks(r)
                if s.exists():
                    residual(s, 0)
                if r.exists():
                    assign(r)
                if s.exists():
                    residual(s, 1)
                if (s + 3).exists():
                    input_statistics(s + 3)

            input_statistics(Unit(0, 0))
            x1_statistics(Unit(0, 0))
            deviations(Unit(0, 0))
            dve.wait_ge(consts, 16 * CONSTS)
            dve.tensor_tensor(gqk[:, 0:1], gqk[:, 1:2], gqk[:, 2:3], ALU.mult).then_inc(gains, 1)
            dve.wait_ge(gains, 1)
            dve.tensor_scalar(gqk[:, 0:1], gqk[:, 0:1], SCALE, None, ALU.mult).then_inc(gains, 1)
            dve.wait_ge(gains, 2)
            input_statistics(Unit(0, 1))
            x1_statistics(Unit(0, 1))
            deviations(Unit(0, 1))
            for j in range(2):
                square_sums(Unit(0, 0), j)
            scale_second(Unit(0, 0))
            input_statistics(Unit(1, 0))
            steps_of_phase_a(dve, step, peeled=6)

            for q in range(NPT):
                m = dve.tensor_scalar(hist_j[:, :], history[:, :, :].rearrange("p u e -> p (u e)"), first[:, q:q + 1],
                                      0.0, ALU.is_le, ALU.add, accum_out=page_e[:, q:q + 1])
                m.then_inc(dB, 1)
                dve.wait_ge(dB, q + 1)
            dve.tensor_copy(page_i[:, :], page_e[:, :]).then_inc(dB, 1)
            dve.wait_ge(dB, NPT + 1)
            dve.tensor_scalar(tab_pc[:, :], page_i[:, :], E - 1, None, ALU.bitwise_and).then_inc(table_made, 1)

            def hidden(t, n):
                dve.wait_ge(sg_done, t + 1)
                ge(dve, dn_full, t - 3)
                dve.tensor_tensor(hh[:, n % 4, :], sg[:, n % 4, :], ps[2 + n % 2][:, P:2 * P], ALU.mult)\
                   .then_inc(hh_done, 1)

            dbank = [psS[:, 0].rearrange("p a n -> p (a n)"), psS[:, 1].rearrange("p a n -> p (a n)")]

            def weigh_result(t, n):
                dve.wait_ge(dn_full, t + 1)
                dve.wait_ge(dest_kept, t + 1)
                ge(dve, y_out[n], left(t, n))
                dve.tensor_scalar(yy[n], dbank[n % 2][:, 0:D], dest[:, n, 0:1].bitcast(fp32), None, ALU.mult)\
                   .then_inc(yy_done, 1)

            def tile_step(t, n):
                if not isinstance(t, int) or t < TILES:
                    hidden(t, n)
                if not isinstance(t, int) or t >= 1:
                    weigh_result(t + -1, (n - 1) % SLOTS)

            for t in range(2 * SLOTS):
                tile_step(t, t % SLOTS)
            with dve.Fori(2 * SLOTS, TILES - SLOTS + 1, SLOTS) as t:
                for n in range(SLOTS):
                    tile_step(t + n, n)
            tile_step(TILES, 0)

            def norm_again(u):
                ge(dve, nt_full, u.n - 1)
                for j in range(2):
                    b = at(2 * u.n + j, 1)
                    m = dve.tensor_scalar(n1h[:, u.par, j, :], x1[:, b, :].rearrange("p a n -> p (a n)"),
                                          mr[:, b, 0:1].rearrange("p a n -> p (a n)"),
                                          mr[:, b, 1:2].rearrange("p a n -> p (a n)"), ALU.subtract, ALU.mult)
                m.then_inc(nh, 1)

            def shared_hidden(u, mm):
                dve.wait_ge(ssg_done, 2 * u.n + mm + 1)
                ge(dve, sd_full, 2 * (u.n - 1))
                dve.tensor_tensor(shh[:, u.par, mm, :], shs[:, u.par, mm, :], ps[2 + 2 * mm][:, 0:D], ALU.mult)\
                   .then_inc(sh_done, 1)

            def sum_rows(u):
                dve.wait_ge(er_in[u.par], 16 * (u.i + 1))
                dve.tensor_tensor(e2, er[:, u.par, :, 0:2, :], er[:, u.par, :, 2:4, :], ALU.add).then_inc(dC, 1)
                dve.wait_ge(dC, u.n + 1)
                dve.tensor_tensor(esum, e2[:, :, 0, :], e2[:, :, 1, :], ALU.add).then_inc(dD, 1)
                dve.wait_ge(dD, 2 * u.n + 1)
                ge(dve, stored[u.par], 16 * u.i)
                dve.tensor_tensor(res[:, u.par], esum, x1[:, at(2 * u.n, 2), :], ALU.add).then_inc(dD, 1)
                dve.wait_ge(dD, 2 * u.n + 2)

            def add_shared(u):
                for j in range(2):
                    dve.wait_ge(sd_full, 2 * u.n + j + 1)
                    dve.tensor_tensor(res[:, u.par, j, :], res[:, u.par, j, :], dbank[j][:, 0:D], ALU.add)\
                       .then_inc(res_done, 1)

            def step(s):
                if s.exists():
                    shared_hidden(s, 0)
                if (s + -1).exists():
                    sum_rows(s + -1)
                if s.exists():
                    shared_hidden(s, 1)
                if (s + -1).exists():
                    add_shared(s + -1)
                if (s + 2).exists():
                    norm_again(s + 2)

            dve.wait_ge(dn_full, TILES)
            norm_again(Unit(0, 0))
            norm_again(Unit(0, 1))
            steps_of_phase_c(dve, step)


def kernel(x, ctx_768, mask_BxS2_bk0, L0_xattn_ln_x_g, L0_xattn_ln_x_b, L0_xattn_ln_l_g, L0_xattn_ln_l_b,
           L0_xattn_qn_g, L0_xattn_kn_g, L0_xattn_Wq, L0_xattn_Wkv, L0_xattn_Wlkv, L0_xattn_Wo, L0_xattn_bo,
           L0_ffn_router_weight, L0_ffn_router_bias, L0_ffn_gate_w, L0_ffn_up_w, L0_ffn_down_w,
           L0_ffn_shared_gate_w, L0_ffn_shared_up_w, L0_ffn_shared_down_w):
    import numpy as np
    import concourse.bacc as bacc
    from concourse.bass_utils import run_bass_kernel_spmd

    def by_chunk(w):
        return np.asarray(w).transpose(2, 0, 1).reshape(2, P, E, I).transpose(1, 0, 2, 3)

    arrays = dict(
        x=x, ctx=ctx_768, mask=np.asarray(mask_BxS2_bk0).reshape(1, NB, P),
        ln_x_g=L0_xattn_ln_x_g, ln_x_b=L0_xattn_ln_x_b, ln_l_g=L0_xattn_ln_l_g, ln_l_b=L0_xattn_ln_l_b,
        qn_g=L0_xattn_qn_g, kn_g=L0_xattn_kn_g,
        wq=np.asarray(L0_xattn_Wq).T, wkv=np.asarray(L0_xattn_Wkv).T, wlkv=np.asarray(L0_xattn_Wlkv).T,
        wo=np.asarray(L0_xattn_Wo).T, bo=L0_xattn_bo,
        rw=np.asarray(L0_ffn_router_weight).T, rb=L0_ffn_router_bias,
        gate=by_chunk(L0_ffn_gate_w), up=by_chunk(L0_ffn_up_w),
        down=np.asarray(L0_ffn_down_w).transpose(2, 0, 1),
        sgate=np.asarray(L0_ffn_shared_gate_w).T, sup=np.asarray(L0_ffn_shared_up_w).T,
        sdown=np.asarray(L0_ffn_shared_down_w).T)
    arrays = {k: np.ascontiguousarray(v) for k, v in arrays.items()}
    nc = bacc.Bacc("TRN2", target_bir_lowering=False, num_devices=1)
    args = [nc.dram_tensor(f"in_{k}", v.shape, mybir.dt.from_np(v.dtype), kind="ExternalInput").ap()
            for k, v in arrays.items()]
    out = nc.dram_tensor("out_0", (NB, P, D), mybir.dt.float32, kind="ExternalOutput").ap()
    with nc.allow_non_contiguous_dma(reason="gains by partition and the tile table: a few small loads"):
        build(nc, *args, out)
    r = run_bass_kernel_spmd(nc, [{f"in_{k}": v for k, v in arrays.items()}], core_ids=[0])
    return r.results[0]["out_0"]
```
